# Optimizing a Trainium2 kernel written in Bass

```python
import numpy as np
import jax
import jax.numpy as jnp

def _softmax(x, axis=-1):
    return jax.nn.softmax(x, axis=axis)

def _gelu(x):
    return jax.nn.gelu(x, approximate=True)

def _silu(x):
    return jax.nn.silu(x)

def _sigmoid(x):
    return jax.nn.sigmoid(x)

def _layernorm(x, axis=-1, eps=1e-05):
    m = jnp.mean(x, axis=axis, keepdims=True)
    v = jnp.var(x, axis=axis, keepdims=True)
    return (x - m) / jnp.sqrt(v + eps)

def _scatter_add(tgt, idx, src, axis=0):
    return tgt.at[idx].add(src)

def _segment_sum(src, seg, n):
    return jax.ops.segment_sum(src, seg, n)
kernel_name = 'mk_gnn_preln_d4_gnn_r32_ad5263'

def setup_inputs(seed: int=0):
    np.random.seed(seed)
    _w = jnp.asarray

    def _rec_inputs():
        import jax
        import jax.numpy as jnp
        _gk = jax.random.key(seed)
        x = -5.39e-05 + 0.9998 * jax.random.normal(jax.random.fold_in(_gk, 1), (3125, 256), jnp.float32)
        src = jax.random.randint(jax.random.fold_in(_gk, 2), (50000,), 0, 3125, jnp.int32)
        dst = jnp.minimum((3125 * jax.random.uniform(jax.random.fold_in(_gk, 3), (50000,)) ** 2.0).astype(jnp.int32), 99999)
        _o = jnp.argsort(dst, stable=True)
        src = src[_o]
        dst = dst[_o]
        edge_attr_2 = jax.random.uniform(jax.random.fold_in(_gk, 12), (50000, 2), jnp.float32, 0.0, 1)
        return (x, src, dst, edge_attr_2)
    x, src, dst, edge_attr_2 = _rec_inputs()

    def _L0_gnn_setup():
        import jax, jax.numpy as jnp
        import numpy as np
        NUM_NODES = 3125
        IN_CH = 256
        HIDDEN = 128
        OUT_CH = 256
        NUM_EDGES = 100000

        def gcn_conv(x, W, b, src, dst, num_nodes):
            h = x @ W
            loop = jnp.arange(num_nodes, dtype=src.dtype)
            s = jnp.concatenate([src, loop])
            d = jnp.concatenate([dst, loop])
            deg = jax.ops.segment_sum(jnp.ones_like(d, dtype=h.dtype), d, num_segments=num_nodes)
            dinv = jnp.where(deg > 0, jax.lax.rsqrt(deg), 0.0)
            norm = dinv[s] * dinv[d]
            msg = h[s] * norm[:, None]
            out = jax.ops.segment_sum(msg, d, num_segments=num_nodes)
            return out + b
        key = jax.random.key(seed)
        k1, k2, k3, k4 = jax.random.split(key, 4)
        edge_index = jax.random.randint(k1, (2, NUM_EDGES), 0, NUM_NODES, dtype=jnp.int64)
        node_features = jax.random.normal(k2, (NUM_NODES, IN_CH), dtype=jnp.float32)
        W1 = jax.random.normal(k3, (IN_CH, HIDDEN), dtype=jnp.float32) * (1.0 / np.sqrt(IN_CH))
        b1 = jnp.zeros((HIDDEN,), dtype=jnp.float32)
        W2 = jax.random.normal(k4, (HIDDEN, OUT_CH), dtype=jnp.float32) * (1.0 / np.sqrt(HIDDEN))
        b2 = jnp.zeros((OUT_CH,), dtype=jnp.float32)
        return {'node_features': node_features, 'W1': W1, 'b1': b1, 'W2': W2, 'b2': b2, 'edge_index': edge_index}
    _L0_gnn_all = _L0_gnn_setup()
    _L0_gnn_in = {k: v for k, v in _L0_gnn_all.items() if k in ('W1', 'b1', 'W2', 'b2')}
    del _L0_gnn_all

    def _L1_gnn_setup():
        import jax, jax.numpy as jnp
        import numpy as np
        N_NODES = 3125
        N_EDGES = 50000
        IN_FEATS = 256
        OUT_FEATS = 64
        NUM_HEADS = 4
        key = jax.random.key(seed)
        k_h, k_adj, k_dir, k_wf, k_wr, k_af = jax.random.split(key, 6)
        h = jax.random.normal(k_h, (N_NODES, IN_FEATS), dtype=jnp.float32)
        adj = jax.random.randint(k_adj, (2, N_EDGES), 0, N_NODES, dtype=jnp.int64)
        bit = jax.random.randint(k_dir, (N_EDGES,), 0, 2).astype(jnp.float32)
        direction = jnp.stack([bit, 1.0 - bit], axis=1)
        s_w = float(np.sqrt(6.0 / (IN_FEATS + OUT_FEATS)))
        s_a = float(np.sqrt(6.0 / (NUM_HEADS + OUT_FEATS)))
        W_forward = jax.random.uniform(k_wf, (OUT_FEATS, IN_FEATS), jnp.float32, -s_w, s_w)
        W_reverse = jax.random.uniform(k_wr, (OUT_FEATS, IN_FEATS), jnp.float32, -s_w, s_w)
        attn_forward = jax.random.uniform(k_af, (1, NUM_HEADS, OUT_FEATS), jnp.float32, -s_a, s_a)
        return {'h': h, 'adj': adj, 'direction': direction, 'W_forward': W_forward, 'W_reverse': W_reverse, 'attn_forward': attn_forward}
    _L1_gnn_all = _L1_gnn_setup()
    _L1_gnn_in = {k: v for k, v in _L1_gnn_all.items() if k in ('W_forward', 'W_reverse', 'attn_forward')}
    del _L1_gnn_all

    def _L2_gnn_setup():
        import jax, jax.numpy as jnp
        import numpy as np
        N_NODES = 50000
        NEG_SLOPE = 0.2

        def _gat_layer(h, W, al, ar, src, dst, residual):
            N = h.shape[0]
            H, D = al.shape
            feat = (h @ W).reshape(N, H, D)
            el = jnp.sum(feat * al[None], axis=-1)
            er = jnp.sum(feat * ar[None], axis=-1)
            e = jax.nn.leaky_relu(el[src] + er[dst], NEG_SLOPE)
            m = jax.ops.segment_max(e, dst, num_segments=N)
            m = jnp.where(jnp.isfinite(m), m, jnp.zeros_like(m))
            ex = jnp.exp(e - m[dst])
            den = jax.ops.segment_sum(ex, dst, num_segments=N)
            a = ex / jnp.maximum(den[dst], jnp.asarray(1e-09, ex.dtype))
            msg = a[:, :, None] * feat[src]
            out = jax.ops.segment_sum(msg, dst, num_segments=N)
            if residual:
                out = out + h.reshape(N, H, D)
            out = jax.nn.relu(out)
            return out.reshape(N, H * D)
        key = jax.random.key(seed)
        ks = jax.random.split(key, 12)
        N, E, F_IN, H, D = (N_NODES, 12500, 256, 4, 64)
        s = 1.0 / np.sqrt(F_IN)
        inp = {'x': jax.random.normal(ks[0], (N, F_IN), dtype=jnp.float32), 'src': jax.random.randint(ks[1], (E,), 0, N, dtype=jnp.int32), 'dst': jax.random.randint(ks[2], (E,), 0, N, dtype=jnp.int32)}
        for i in range(3):
            inp[f'W{i}'] = jax.random.normal(ks[3 + 3 * i], (F_IN, H * D), dtype=jnp.float32) * s
            inp[f'al{i}'] = jax.random.normal(ks[4 + 3 * i], (H, D), dtype=jnp.float32) * s
            inp[f'ar{i}'] = jax.random.normal(ks[5 + 3 * i], (H, D), dtype=jnp.float32) * s
        return inp
    _L2_gnn_all = _L2_gnn_setup()
    _L2_gnn_in = {k: v for k, v in _L2_gnn_all.items() if k in ('W0', 'al0', 'ar0', 'W1', 'al1', 'ar1', 'W2', 'al2', 'ar2')}
    del _L2_gnn_all

    def _L3_gnn_setup():
        import jax, jax.numpy as jnp
        import numpy as np
        N_NODES = 50000
        N_EDGES = 25000
        IN_DIM = 256
        OUT_DIM = 64
        HEADS = 4
        NEG_SLOPE = 0.2
        key = jax.random.key(seed)
        k_x, k_e, k_w, k_as, k_ad = jax.random.split(key, 5)
        x = jax.random.normal(k_x, (N_NODES, IN_DIM), dtype=jnp.float32)
        edge_index = jax.random.randint(k_e, (2, N_EDGES), 0, N_NODES, dtype=jnp.int64)
        W = jax.random.normal(k_w, (IN_DIM, HEADS * OUT_DIM), dtype=jnp.float32) / np.sqrt(IN_DIM)
        att_src = jax.random.normal(k_as, (HEADS, OUT_DIM), dtype=jnp.float32) / np.sqrt(OUT_DIM)
        att_dst = jax.random.normal(k_ad, (HEADS, OUT_DIM), dtype=jnp.float32) / np.sqrt(OUT_DIM)
        bias = jnp.zeros((HEADS * OUT_DIM,), dtype=jnp.float32)
        return {'x': x, 'edge_index': edge_index, 'W': W, 'att_src': att_src, 'att_dst': att_dst, 'bias': bias}
    _L3_gnn_all = _L3_gnn_setup()
    _L3_gnn_in = {k: v for k, v in _L3_gnn_all.items() if k in ('W', 'att_src', 'att_dst', 'bias')}
    del _L3_gnn_all
    return {'x': x, 'src': src, 'dst': dst, 'edge_attr_2': edge_attr_2, 'L0_gnn_W1': _L0_gnn_in['W1'], 'L0_gnn_b1': _L0_gnn_in['b1'], 'L0_gnn_W2': _L0_gnn_in['W2'], 'L0_gnn_b2': _L0_gnn_in['b2'], 'L1_gnn_W_forward': _L1_gnn_in['W_forward'], 'L1_gnn_W_reverse': _L1_gnn_in['W_reverse'], 'L1_gnn_attn_forward': _L1_gnn_in['attn_forward'], 'L2_gnn_W0': _L2_gnn_in['W0'], 'L2_gnn_al0': _L2_gnn_in['al0'], 'L2_gnn_ar0': _L2_gnn_in['ar0'], 'L2_gnn_W1': _L2_gnn_in['W1'], 'L2_gnn_al1': _L2_gnn_in['al1'], 'L2_gnn_ar1': _L2_gnn_in['ar1'], 'L2_gnn_W2': _L2_gnn_in['W2'], 'L2_gnn_al2': _L2_gnn_in['al2'], 'L2_gnn_ar2': _L2_gnn_in['ar2'], 'L3_gnn_W': _L3_gnn_in['W'], 'L3_gnn_att_src': _L3_gnn_in['att_src'], 'L3_gnn_att_dst': _L3_gnn_in['att_dst'], 'L3_gnn_bias': _L3_gnn_in['bias']}

def reference(x, src, dst, edge_attr_2, L0_gnn_W1, L0_gnn_b1, L0_gnn_W2, L0_gnn_b2, L1_gnn_W_forward, L1_gnn_W_reverse, L1_gnn_attn_forward, L2_gnn_W0, L2_gnn_al0, L2_gnn_ar0, L2_gnn_W1, L2_gnn_al1, L2_gnn_ar1, L2_gnn_W2, L2_gnn_al2, L2_gnn_ar2, L3_gnn_W, L3_gnn_att_src, L3_gnn_att_dst, L3_gnn_bias):
    import jax
    import jax.numpy as jnp

    def _L0_gnn_ref(node_features, W1, b1, W2, b2, edge_index):
        import jax, jax.numpy as jnp
        import numpy as np
        NUM_NODES = 3125
        IN_CH = 256
        HIDDEN = 128
        OUT_CH = 256
        NUM_EDGES = 100000

        def gcn_conv(x, W, b, src, dst, num_nodes):
            h = x @ W
            loop = jnp.arange(num_nodes, dtype=src.dtype)
            s = jnp.concatenate([src, loop])
            d = jnp.concatenate([dst, loop])
            deg = jax.ops.segment_sum(jnp.ones_like(d, dtype=h.dtype), d, num_segments=num_nodes)
            dinv = jnp.where(deg > 0, jax.lax.rsqrt(deg), 0.0)
            norm = dinv[s] * dinv[d]
            msg = h[s] * norm[:, None]
            out = jax.ops.segment_sum(msg, d, num_segments=num_nodes)
            return out + b
        src, dst = (edge_index[0], edge_index[1])
        x = gcn_conv(node_features, W1, b1, src, dst, NUM_NODES)
        x = jax.nn.relu(x)
        x = gcn_conv(x, W2, b2, src, dst, NUM_NODES)
        return x

    def _L1_gnn_ref(h, adj, direction, W_forward, W_reverse, attn_forward):
        import jax, jax.numpy as jnp
        import numpy as np
        N_NODES = 3125
        N_EDGES = 50000
        IN_FEATS = 256
        OUT_FEATS = 64
        NUM_HEADS = 4
        N = h.shape[0]
        H = attn_forward.shape[1]
        h_fwd = h @ W_forward.T
        h_rev = h @ W_reverse.T
        src, dst = (adj[0], adj[1])
        messages = h_fwd[src] * direction[:, 0:1] + h_rev[src] * direction[:, 1:2]
        scores = jnp.einsum('ef,hf->eh', messages, attn_forward[0])
        scores = jax.nn.leaky_relu(scores, negative_slope=0.2)
        exp_scores = jnp.exp(scores - scores.max(axis=0, keepdims=True))
        sum_exp = jax.ops.segment_sum(exp_scores, dst, num_segments=N)
        norm = exp_scores / (sum_exp[dst] + 1e-10)
        outs = [jax.ops.segment_sum(messages * norm[:, hd:hd + 1], dst, num_segments=N) for hd in range(H)]
        out = jnp.stack(outs, axis=1)
        return out.reshape(N, -1)

    def _L2_gnn_ref(x, src, dst, W0, al0, ar0, W1, al1, ar1, W2, al2, ar2):
        import jax, jax.numpy as jnp
        import numpy as np
        N_NODES = 50000
        NEG_SLOPE = 0.2

        def _gat_layer(h, W, al, ar, src, dst, residual):
            N = h.shape[0]
            H, D = al.shape
            feat = (h @ W).reshape(N, H, D)
            el = jnp.sum(feat * al[None], axis=-1)
            er = jnp.sum(feat * ar[None], axis=-1)
            e = jax.nn.leaky_relu(el[src] + er[dst], NEG_SLOPE)
            m = jax.ops.segment_max(e, dst, num_segments=N)
            m = jnp.where(jnp.isfinite(m), m, jnp.zeros_like(m))
            ex = jnp.exp(e - m[dst])
            den = jax.ops.segment_sum(ex, dst, num_segments=N)
            a = ex / jnp.maximum(den[dst], jnp.asarray(1e-09, ex.dtype))
            msg = a[:, :, None] * feat[src]
            out = jax.ops.segment_sum(msg, dst, num_segments=N)
            if residual:
                out = out + h.reshape(N, H, D)
            out = jax.nn.relu(out)
            return out.reshape(N, H * D)
        h = _gat_layer(x, W0, al0, ar0, src, dst, residual=True)
        h = _gat_layer(h, W1, al1, ar1, src, dst, residual=True)
        h = _gat_layer(h, W2, al2, ar2, src, dst, residual=False)
        return h

    def _L3_gnn_ref(x, edge_index, W, att_src, att_dst, bias):
        import jax, jax.numpy as jnp
        import numpy as np
        N_NODES = 50000
        N_EDGES = 25000
        IN_DIM = 256
        OUT_DIM = 64
        HEADS = 4
        NEG_SLOPE = 0.2
        N = x.shape[0]
        H, C = att_src.shape
        loop = jnp.arange(N, dtype=edge_index.dtype)
        src = jnp.concatenate([edge_index[0], loop])
        dst = jnp.concatenate([edge_index[1], loop])
        xh = (x @ W).reshape(N, H, C)
        a_src = jnp.einsum('nhc,hc->nh', xh, att_src)
        a_dst = jnp.einsum('nhc,hc->nh', xh, att_dst)
        logits = jax.nn.leaky_relu(a_src[src] + a_dst[dst], NEG_SLOPE)
        seg_max = jax.ops.segment_max(logits, dst, num_segments=N)
        e = jnp.exp(logits - seg_max[dst])
        seg_sum = jax.ops.segment_sum(e, dst, num_segments=N)
        alpha = e / seg_sum[dst]
        msgs = alpha[:, :, None] * xh[src]
        out = jax.ops.segment_sum(msgs, dst, num_segments=N)
        out = out.reshape(N, H * C) + bias
        return out
    edge_index = jnp.stack([src, dst])
    h = jnp.maximum(_layernorm(x, axis=-1), 0.0)
    x = x + _L0_gnn_ref(h, L0_gnn_W1, L0_gnn_b1, L0_gnn_W2, L0_gnn_b2, edge_index)
    h = jnp.maximum(_layernorm(x, axis=-1), 0.0)
    x = x + _L1_gnn_ref(h, edge_index, edge_attr_2, L1_gnn_W_forward, L1_gnn_W_reverse, L1_gnn_attn_forward)
    h = jnp.maximum(_layernorm(x, axis=-1), 0.0)
    x = x + _L2_gnn_ref(h, src, dst, L2_gnn_W0, L2_gnn_al0, L2_gnn_ar0, L2_gnn_W1, L2_gnn_al1, L2_gnn_ar1, L2_gnn_W2, L2_gnn_al2, L2_gnn_ar2)
    h = jnp.maximum(_layernorm(x, axis=-1), 0.0)
    x = x + _L3_gnn_ref(h, edge_index, L3_gnn_W, L3_gnn_att_src, L3_gnn_att_dst, L3_gnn_bias)
    return x

_drawn_inputs = setup_inputs


def setup_inputs(seed=0):
    import zlib

    import numpy as np

    out = dict(_drawn_inputs(seed))
    spreads = {'L0_gnn_b1': (0.0, 0.1), 'L0_gnn_b2': (0.0, 0.1), 'L3_gnn_bias': (0.0, 0.1)}
    factors = {'L2_gnn_al0': 8.0,
     'L2_gnn_ar0': 23.822,
     'L2_gnn_al1': 8.0,
     'L2_gnn_ar1': 23.28,
     'L2_gnn_al2': 4.056,
     'L2_gnn_ar2': 8.0,
     'L3_gnn_att_dst': 11.337}
    for name, (base, spread) in spreads.items():
        noise = np.random.default_rng([zlib.crc32(name.encode()), seed]).standard_normal(out[name].shape)
        drawn = base * np.exp(spread * noise) if base else spread * noise
        out[name] = jnp.asarray(drawn.astype(out[name].dtype))
    for name, factor in factors.items():
        out[name] = (out[name] * factor).astype(out[name].dtype)
    return out
```

```python
from contextlib import ExitStack

import concourse.bass as bass
from concourse import mybir
from concourse.alu_op_type import AluOpType as ALU
ACT = mybir.ActivationFunctionType
F32 = mybir.dt.float32
F16 = mybir.dt.float16
BF16 = mybir.dt.bfloat16
I32 = mybir.dt.int32
U32 = mybir.dt.uint32
AX = mybir.AxisListType
P = 128
N = 3125
NB = 25
NP = NB * P
E = 50000
T = 392
GT = 4
G = T // GT
PAD_ROWS = 16
TAB = (NP + PAD_ROWS) * NP
ZW = TAB // P // 4


def adjacency(nc, src, dst, table, key_rows):
    with ExitStack() as ctx:
        s = Scope(nc, ctx, "adj")
        sb, sem = s.sb, s.sem
        src_i = sb("src_i", [P, T], I32)
        dst_i = sb("dst_i", [P, T], I32)
        key = sb("key", [P, T], F32)
        slot = sb("slot", [P, T], I32)
        spare = sb("spare", [P, T], F32)
        count = sb("count", [P, T], F32)
        early = sb("early", [P, T], F32)
        key_t = sb("key_t", [98, 4, P], F32)
        ident = sb("ident", [P, P], F32)
        before = sb("before", [P, GT, GT * P], BF16)
        zeros = sb("zeros", [P, ZW], F16)
        rows = sb("rows", [P, 2, GT * P], F32)
        same = sb("same", [P, GT * P], BF16)
        same2 = sb("same2", [P, GT * P], BF16)
        ones = sb("ones", [P, GT * P], BF16)
        pick = sb("pick", [P, 2, GT], F32)
        cell = sb("cell", [P, 2, GT], U32)
        value = sb("value", [P, 2, GT], F16)
        ps = ctx.enter_context(nc.psum_tensor("adj_ps", [P, 4, P], F32))
        edges_in = sem("edges_in")
        zero_set = sem("zero_set")
        table_zero = sem("table_zero")
        keys_ready = sem("keys_ready")
        ident_ready = sem("ident_ready")
        keys_turned = sem("keys_turned")
        keys_copied = sem("keys_copied")
        keys_out = sem("keys_out")
        row_in = [sem("row_in0"), sem("row_in1")]
        row_free = [sem("row_free0"), sem("row_free1")]
        dve_step = sem("dve_step")
        cells_ready = sem("cells_ready")
        cells_free = sem("cells_free")
        scattered = s.pool_dma_sem("scattered")
        slot_ready = sem("slot_ready")
        pool_pass = sem("pool_pass")
        block = ctx.enter_context(nc.Block())

        @block.sync
        def _(sync):
            sync.dma_start(src_i[:], src).then_inc(edges_in, 16)
            sync.dma_start(dst_i[:], dst).then_inc(edges_in, 16)
            sync.wait_ge(keys_copied, 1)
            sync.dma_start(key_rows.rearrange("(c t) p -> t c p", c=4), key_t[:]).then_inc(keys_out, 16)
            sync.wait_ge(keys_out, 16)
            with sync.Fori(0, G // 2) as i:
                for u in range(2):
                    sync.wait_ge(row_free[u], i + 1)
                    sync.dma_start(rows[:, u, :], key_rows[bass.ds((i * 2 + u) * GT, GT), :].rearrange("(a t) p -> a (t p)", a=1).to_broadcast([P, GT * P])).then_inc(row_in[u], 16)

        @block.scalar
        def _(act):
            act.wait_ge(zero_set, 1)
            for q in range(4):
                act.dma_start(table.rearrange("(q p) w -> q p w", q=4)[q], zeros[:]).then_inc(table_zero, 16)

        @block.gpsimd
        def _(pool):
            pool.memset(ident[:], 0.0).then_inc(ident_ready, 1)
            pool.memset(before[:], 1.0).then_inc(ident_ready, 1)
            pool.iota(slot[:], pattern=[[1, T]], base=NP * NP, channel_multiplier=T).then_inc(slot_ready, 1)
            pool.wait_ge(ident_ready, 2)
            pool.affine_select(out=ident[:], in_=ident[:], compare_op=ALU.not_equal, fill=1.0, base=0,
                               pattern=[[-1, P]], channel_multiplier=1).then_inc(ident_ready, 1)
            pool.affine_select(out=before[:], in_=before[:], compare_op=ALU.is_gt, fill=0.0, base=0,
                               pattern=[[P, GT], [-1, GT * P]], channel_multiplier=1).then_inc(ident_ready, 1)
            pool.wait_ge(table_zero, 64)
            flat = table.rearrange("a (w o) -> (a w) o", o=1)
            with pool.Fori(0, G // 2) as i:
                for u in range(2):
                    g = i * 2 + u
                    pool.wait_ge(scattered, g * (16 * GT))
                    pool.sem_inc(cells_free, 1)
                    pool.wait_ge(cells_ready, g + 1)
                    pool.sem_inc(pool_pass, 1)
                    for k in range(GT):
                        pool.indirect_dma_start(out=flat, out_offset=bass.IndirectOffsetOnAxis(cell[:, u, k:k + 1], 0),
                                                in_=value[:, u, k:k + 1], in_offset=None, bounds_check=TAB - 1,
                                                compute_op=ALU.add).then_inc(scattered, 16)
            pool.wait_ge(scattered, G * 16 * GT)

        @block.tensor
        def _(pe):
            pe.wait_ge(ident_ready, 4)
            pe.wait_ge(keys_ready, 1)
            for c in range(4):
                last = pe.transpose(ps[0:98, c, :], key[:, c * 98:(c + 1) * 98], ident[:])
            last.then_inc(keys_turned, 1)

        @block.vector
        def _(dve):
            dve.memset(zeros[:], 0.0).then_inc(zero_set, 1)
            dve.memset(ones[:], 1.0).then_inc(dve_step, 1)
            dve.wait_ge(edges_in, 32)
            dve.scalar_tensor_tensor(out=key[:], in0=src_i[:], scalar=float(NP), in1=dst_i[:], op0=ALU.mult,
                                     op1=ALU.add).then_inc(keys_ready, 1)
            dve.wait_ge(keys_turned, 1)
            dve.tensor_copy(key_t[:], ps[0:98, :, :]).then_inc(keys_copied, 1)
            dve.wait_ge(keys_ready, 1)
            dve.wait_ge(slot_ready, 1)
            dve.tensor_tensor(spare[:], slot[:], key[:], ALU.subtract).then_inc(dve_step, 1)
            for u in range(2):
                dve.sem_inc(row_free[u], 1)
            dve.wait_ge(ident_ready, 4)
            per = 6
            with dve.Fori(0, G // 2) as i:
                at = i * 24 + 2
                for u in range(2):
                    g = i * 2 + u
                    dve.wait_ge(row_in[u], i * 16 + 16)
                    dve.wait_ge(cells_free, g)
                    for k in range(GT):
                        t = g * GT + k
                        dve.wait_ge(dve_step, at)
                        dve.scalar_tensor_tensor(same[:], rows[:, u, :], key[:, bass.ds(t, 1)], ones[:], ALU.is_equal, ALU.mult, accum_out=count[:, bass.ds(t, 1)]).then_inc(dve_step, 1)
                        at = at + 1
                        dve.wait_ge(dve_step, at)
                        dve.scalar_tensor_tensor(same2[:], rows[:, u, :], key[:, bass.ds(t, 1)], before[:, k, :], ALU.is_equal, ALU.mult, accum_out=early[:, bass.ds(t, 1)]).then_inc(dve_step, 1)
                        at = at + 1
                    dve.wait_ge(dve_step, at)
                    dve.sem_inc(row_free[u], 1)
                    ts = bass.ds(g * GT, GT)
                    dve.tensor_scalar(pick[:, u, :], early[:, ts], 0.0, None, ALU.is_gt).then_inc(dve_step, 1)
                    at = at + 1
                    dve.wait_ge(dve_step, at)
                    dve.tensor_tensor(pick[:, u, :], pick[:, u, :], spare[:, ts], ALU.mult).then_inc(dve_step, 1)
                    at = at + 1
                    dve.wait_ge(dve_step, at)
                    dve.tensor_tensor(cell[:, u, :], pick[:, u, :], key[:, ts], ALU.add).then_inc(dve_step, 1)
                    at = at + 1
                    dve.tensor_copy(value[:, u, :], count[:, ts]).then_inc(dve_step, 1)
                    at = at + 1
                    dve.wait_ge(dve_step, at)
                    dve.sem_inc(cells_ready, 1)


class Count:

    def __init__(self, sem, n=0):
        self.sem, self.n = sem, n

    def add(self, ins, by=1):
        ins.then_inc(self.sem, by)
        self.n = self.n + by
        return self.n

    def enter(self, i, per):
        self.start, self.per = self.n, per
        self.n = self.n + i * per

    def leave(self, turns):
        self.n = self.start + turns * self.per


class Scope:

    def __init__(self, nc, ctx, tag):
        self.nc, self.ctx, self.tag, self.sems = nc, ctx, tag, []
        ctx.callback(self.release)

    def release(self):
        nums = sorted(x.num for x in self.sems)
        while nums:
            k = 1
            while k < len(nums) and nums[k] == nums[0] + k:
                k += 1
            self.nc.gpsimd.sem_clear(range(nums[0], nums[0] + k))
            nums = nums[k:]
        for x in self.sems:
            self.nc.release_semaphore(x)

    def sb(self, name, shape, dt):
        return self.ctx.enter_context(self.nc.sbuf_tensor(f"{self.tag}_{name}", shape, dt))

    def ps(self, name, shape, dt=F32):
        return self.ctx.enter_context(self.nc.psum_tensor(f"{self.tag}_{name}", shape, dt))

    def sem(self, name):
        self.sems.append(self.nc.alloc_semaphore(f"{self.tag}_{name}"))
        return self.sems[-1]

    def pool_dma_sem(self, name):
        return self.nc.alloc_semaphore(f"{self.tag}_{name}")


def rows_of(ap):
    return ap.rearrange("(b p) f -> p b f", p=P)


def load_nodes(nc, x, x_in, ident):
    with ExitStack() as ctx:
        s = Scope(nc, ctx, "load")
        zeroed, x_loaded, ident_set = s.sem("zeroed"), s.sem("x_loaded"), s.sem("ident_set")
        block = ctx.enter_context(nc.Block())

        @block.vector
        def _(dve):
            dve.memset(x[:, NB - 1, :], 0.0).then_inc(zeroed, 1)

        @block.sync
        def _(sync):
            full = (NB - 1) * P
            sync.dma_start(x[:, 0:NB - 1, :], rows_of(x_in[0:full, :])).then_inc(x_loaded, 16)
            sync.wait_ge(zeroed, 1)
            sync.dma_start(x[0:N - full, NB - 1, :], x_in[full:N, :]).then_inc(x_loaded, 16)
            sync.wait_ge(x_loaded, 32)

        @block.gpsimd
        def _(pool):
            pool.memset(ident[:], 0.0).then_inc(ident_set, 1)
            pool.wait_ge(ident_set, 1)
            pool.affine_select(out=ident[:], in_=ident[:], compare_op=ALU.not_equal, fill=1.0, base=0,
                               pattern=[[-1, P]], channel_multiplier=1).then_inc(ident_set, 1)
            pool.wait_ge(ident_set, 2)


def normalise(nc, tag, x, h):
    with ExitStack() as ctx:
        s = Scope(nc, ctx, tag)
        stats = s.sb("stats", [P, NB, 6], F32)
        mv = s.sb("mv", [P, NB, 2], F32)
        sd = s.sb("sd", [P, NB], F32)
        rstd = s.sb("rstd", [P, NB], F32)
        shift = s.sb("shift", [P, NB], F32)
        eps = s.sb("eps", [P, 1], F32)
        eps_set, stats_ready, mv_ready = s.sem("eps_set"), s.sem("stats_ready"), s.sem("mv_ready")
        sd_ready, rstd_ready, shift_ready, h_done = (s.sem(n) for n in ("sd_ready", "rstd_ready", "shift_ready", "h_done"))
        block = ctx.enter_context(nc.Block())

        @block.vector
        def _(dve):
            dve.memset(eps[:], 1e-5).then_inc(eps_set, 1)
            for b in range(NB):
                dve.bn_stats(stats[:, b, :], x[:, b, :]).then_inc(stats_ready, 1)
            dve.wait_ge(stats_ready, NB)
            for b in range(NB):
                dve.bn_aggr(mv[:, b, :], stats[:, b, :]).then_inc(mv_ready, 1)
            dve.wait_ge(sd_ready, 1)
            dve.reciprocal(rstd[:], sd[:]).then_inc(rstd_ready, 1)
            dve.wait_ge(rstd_ready, 1)
            dve.scalar_tensor_tensor(shift[:], mv[:, :, 0], -1.0, rstd[:], ALU.mult, ALU.mult).then_inc(shift_ready, 1)

        @block.scalar
        def _(act):
            act.wait_ge(eps_set, 1)
            act.wait_ge(mv_ready, NB)
            act.activation(sd[:], mv[:, :, 1], ACT.Sqrt, bias=eps[:, 0:1]).then_inc(sd_ready, 1)
            act.wait_ge(shift_ready, 1)
            for b in range(NB):
                act.activation(h[:, b, :], x[:, b, :], ACT.Relu, bias=shift[:, b:b + 1],
                               scale=rstd[:, b:b + 1]).then_inc(h_done, 1)
            act.wait_ge(h_done, NB)


UN = 4


def project(nc, tag, h, kk, weights, width, out, ident, stacked=None):
    with ExitStack() as ctx:
        s = Scope(nc, ctx, tag)
        w = s.sb("w", [P, kk, width], F32)
        raw = s.sb("raw", [P, kk * P], F32)
        turned = s.sb("turned", [P, UN, kk * P], F32)
        ps_t = s.ps("ps_t", [P, UN, 512])
        ps_o = s.ps("ps_o", [P, UN, 512])
        w_in, w_ready, w_turned = s.sem("w_in"), s.sem("w_ready"), s.sem("w_turned")
        turn_ready, turn_copied, made, taken = (s.sem(n) for n in (
            "turn_ready", "turn_copied", "made", "taken"))
        block = ctx.enter_context(nc.Block())

        @block.sync
        def _(sync):
            if stacked:
                sync.dma_start(raw[0:64, :], stacked[0]).then_inc(w_in, 16)
                sync.dma_start(raw[64:P, :], stacked[1]).then_inc(w_in, 16)
            else:
                sync.dma_start(w[:], weights.rearrange("(k p) n -> p k n", p=P)).then_inc(w_in, 16)

        @block.tensor
        def _(pe):
            pe.wait_ge(w_in, 32 if stacked else 16)
            if stacked:
                for k in range(kk):
                    last = pe.transpose(ps_o[:, 0, k * P:(k + 1) * P], raw[:, k * P:(k + 1) * P], ident[:])
                last.then_inc(w_turned, 1)
                pe.wait_ge(w_ready, 1)
            for n in range(NB + 2):
                if n < NB:
                    if n >= UN:
                        pe.wait_ge(turn_copied, n - UN + 1)
                    for k in range(kk):
                        last = pe.transpose(ps_t[:, n % UN, k * P:(k + 1) * P], h[:, n, k * P:(k + 1) * P], ident[:])
                    last.then_inc(turn_ready, 1)
                if n >= 2:
                    b = n - 2
                    pe.wait_ge(turn_copied, b + 1)
                    if b >= UN:
                        pe.wait_ge(taken, b - UN + 1)
                    for k in range(kk):
                        last = pe.matmul(ps_o[:, b % UN, 0:width], turned[:, b % UN, k * P:(k + 1) * P], w[:, k, :],
                                         start=(k == 0), stop=(k == kk - 1))
                    last.then_inc(made, 1)

        @block.scalar
        def _(act):
            for n in range(NB):
                act.wait_ge(turn_ready, n + 1)
                if n >= UN:
                    act.wait_ge(made, n - UN + 1)
                act.copy(turned[:, n % UN, :], ps_t[:, n % UN, 0:kk * P]).then_inc(turn_copied, 1)

        @block.vector
        def _(dve):
            if stacked:
                dve.wait_ge(w_turned, 1)
                dve.tensor_copy(w[:].rearrange("p k n -> p (k n)"), ps_o[:, 0, 0:kk * P]).then_inc(w_ready, 1)
            for n in range(NB):
                dve.wait_ge(made, n + 1)
                dve.tensor_copy(out[:, n, 0:width], ps_o[:, n % UN, 0:width]).then_inc(taken, 1)
            dve.wait_ge(taken, NB)


CW = 256
CS = 4
CBLK = CW // P
TURN = CS * CBLK
TURNS = NB // TURN


def gcn_pass(nc, tag, table, rhs, width, emit, extra=None):
    assert TURNS * TURN + 1 == NB
    with ExitStack() as ctx:
        s = Scope(nc, ctx, tag)
        cols = s.sb("cols", [P, CS, NB, CW], F16)
        ps = s.ps("ps", [P, TURN, 512])
        chunk_in = [s.sem(f"chunk_in{u}") for u in range(CS)]
        chunk_free = s.sem("chunk_free")
        summed, bank_free, pe_pass, dve_step = s.sem("summed"), s.sem("bank_free"), s.sem("pe_pass"), s.sem("dve_step")
        scratch = extra(s) if extra else None
        block = ctx.enter_context(nc.Block())
        tab = table.rearrange("(b p) d -> p b d", p=P)

        @block.sync
        def _(sync):
            with sync.Fori(0, TURNS) as i:
                for u in range(CS):
                    sync.wait_ge(chunk_free, i * CS + u + 1)
                    sync.dma_start(cols[:, u, :, :], tab[:, :, bass.ds((i * CS + u) * CW, CW)]).then_inc(chunk_in[u], 16)
            sync.wait_ge(chunk_free, TURNS * CS + 1)
            sync.dma_start(cols[:, 0, :, 0:P], tab[:, :, TURNS * TURN * P:NB * P]).then_inc(chunk_in[0], 16)

        @block.tensor
        def _(pe):
            pe.sem_inc(chunk_free, CS)

            def one(u, j, bank):
                for b in range(NB):
                    last = pe.matmul(ps[:, bank, 0:width], cols[:, u, b, j * P:(j + 1) * P], rhs[:, b, :],
                                     start=(b == 0), stop=(b == NB - 1))
                last.then_inc(summed, 1)
                return last
            with pe.Fori(0, TURNS) as i:
                for u in range(CS):
                    pe.wait_ge(chunk_in[u], i * 16 + 16)
                    for j in range(CBLK):
                        bank = u * CBLK + j
                        pe.wait_ge(bank_free, i * TURN + bank + 1)
                        pe.sem_inc(pe_pass, 1)
                        one(u, j, bank)
                    pe.wait_ge(summed, i * TURN + bank + 1)
                    pe.sem_inc(chunk_free, 1)
            pe.wait_ge(chunk_in[0], TURNS * 16 + 16)
            pe.wait_ge(bank_free, TURNS * TURN + 1)
            one(0, 0, 0)

        @block.vector
        def _(dve):
            dve.sem_inc(bank_free, TURN)
            step = Count(dve_step)
            per = emit(None, 0, 0, Count(dve_step), scratch)
            with dve.Fori(0, TURNS) as i:
                step.enter(i, TURN * per)
                for bank in range(TURN):
                    dve.wait_ge(summed, i * TURN + bank + 1)
                    emit(dve, bass.ds(i * TURN + bank, 1), ps[:, bank, :], step, scratch)
                    dve.sem_inc(bank_free, 1)
                step.leave(TURNS)
            dve.wait_ge(summed, NB)
            emit(dve, slice(NB - 1, NB), ps[:, 0, :], step, scratch)


def flat(ap):
    return ap.rearrange("p a f -> p (a f)")


def degree(nc, table, dinv):
    with ExitStack() as ctx:
        s = Scope(nc, ctx, "deg")
        ones = s.sb("ones", [P, NB, 1], F16)
        deg = s.sb("deg", [P, NB], F32)
        root = s.sb("root", [P, NB], F32)
        set_, rooted, done = s.sem("set"), s.sem("rooted"), s.sem("done")
        with nc.Block() as block:
            @block.vector
            def _(dve):
                dve.memset(ones[:], 1.0).then_inc(set_, 1)
                dve.wait_ge(set_, 1)

        def emit(dve, at, ps, step, scratch):
            if dve is None:
                return 1
            step.add(dve.tensor_scalar(deg[:, at], ps[:, 0:1], 1.0, None, ALU.add))
            dve.wait_ge(step.sem, step.n)
        gcn_pass(nc, "degp", table, ones, 1, emit)
        with nc.Block() as block:
            @block.scalar
            def _(act):
                act.activation(root[:], deg[:], ACT.Sqrt).then_inc(rooted, 1)

            @block.vector
            def _(dve):
                dve.wait_ge(rooted, 1)
                dve.reciprocal(dinv[:], root[:]).then_inc(done, 1)
                dve.wait_ge(done, 1)


def gcn_conv(nc, tag, table, feats, width, dinv, out, bias=None):
    with ExitStack() as ctx:
        s = Scope(nc, ctx, tag)
        scaled = s.sb("scaled", [P, NB, width], F32)
        parts = s.sb("parts", [P, NB, 3 * width], BF16)
        rest = s.sb("rest", [P, NB, width], F32)
        bias_all = s.sb("bias_all", [P, width], F32)
        step_s, hi_s, mid_s, bias_in = s.sem("step"), s.sem("hi"), s.sem("mid"), s.sem("bias_in")
        with nc.Block() as block:
            @block.sync
            def _(sync):
                if bias is not None:
                    sync.dma_start(bias_all[:], bias.rearrange("(a n) -> a n", a=1).to_broadcast([P, width])).then_inc(bias_in, 16)
                    sync.wait_ge(bias_in, 16)

            @block.vector
            def _(dve):
                for g in range(5):
                    b = slice(5 * g, 5 * g + 5)
                    dve.tensor_tensor(scaled[:, b, :], feats[:, b, :], dinv[:, b].rearrange("p (b o) -> p b o", o=1).to_broadcast([P, 5, width]),
                                      ALU.mult).then_inc(step_s, 1)
                for g in range(5):
                    b = slice(5 * g, 5 * g + 5)
                    dve.wait_ge(hi_s, g + 1)
                    dve.tensor_tensor(rest[:, b, :], scaled[:, b, :], parts[:, b, 0:width], ALU.subtract).then_inc(step_s, 1)
                for g in range(5):
                    b = slice(5 * g, 5 * g + 5)
                    dve.wait_ge(mid_s, g + 1)
                    dve.tensor_tensor(parts[:, b, 2 * width:], rest[:, b, :], parts[:, b, width:2 * width], ALU.subtract).then_inc(step_s, 1)
                dve.wait_ge(step_s, 15)

            @block.scalar
            def _(act):
                for g in range(5):
                    b = slice(5 * g, 5 * g + 5)
                    act.wait_ge(step_s, g + 1)
                    act.copy(parts[:, b, 0:width], scaled[:, b, :]).then_inc(hi_s, 1)
                for g in range(5):
                    b = slice(5 * g, 5 * g + 5)
                    act.wait_ge(step_s, 5 + g + 1)
                    act.copy(parts[:, b, width:2 * width], rest[:, b, :]).then_inc(mid_s, 1)

        def extra(sc):
            return sc.sb("t1", [P, width], F32), sc.sb("t2", [P, width], F32), sc.sb("t3", [P, width], F32)

        def emit(dve, at, ps, step, scratch):
            if dve is None:
                return 4 if bias is not None else 3
            t1, t2, t3 = scratch
            step.add(dve.tensor_reduce(t1[:], ps[:, 0:3 * width].rearrange("p (j f) -> p f j", j=3), AX.X, ALU.add))
            dve.wait_ge(step.sem, step.n)
            step.add(dve.tensor_tensor(t2[:], t1[:], flat(scaled[:, at, :]), ALU.add))
            dve.wait_ge(step.sem, step.n)
            if bias is None:
                step.add(dve.tensor_scalar(flat(out[:, at, :]), t2[:], dinv[:, at], None, ALU.mult))
            else:
                step.add(dve.scalar_tensor_tensor(t3[:], t2[:], dinv[:, at], bias_all[:], ALU.mult, ALU.add))
                dve.wait_ge(step.sem, step.n)
                step.add(dve.tensor_scalar(flat(out[:, at, :]), t3[:], 0.0, None, ALU.max))
            dve.wait_ge(step.sem, step.n)
        gcn_pass(nc, tag + "p", table, parts, 3 * width, emit, extra)


def add_to(nc, tag, x, y, bias):
    with ExitStack() as ctx:
        s = Scope(nc, ctx, tag)
        bias_all = s.sb("bias_all", [P, 256], F32)
        bias_in, added = s.sem("bias_in"), s.sem("added")
        with nc.Block() as block:
            @block.sync
            def _(sync):
                if bias is not None:
                    sync.dma_start(bias_all[:], bias.rearrange("(a n) -> a n", a=1).to_broadcast([P, 256])).then_inc(bias_in, 16)

            @block.vector
            def _(dve):
                done = Count(added)
                if y is not None:
                    done.add(dve.tensor_tensor(x[:], x[:], y[:], ALU.add))
                    dve.wait_ge(done.sem, done.n)
                if bias is not None:
                    dve.wait_ge(bias_in, 16)
                    done.add(dve.tensor_tensor(x[:], x[:], bias_all[:].rearrange("p (o f) -> p o f", o=1).to_broadcast([P, NB, 256]), ALU.add))
                dve.wait_ge(done.sem, done.n)


H = 4
D = 64
DW = D + 1
HW = 3 * DW
GC = 512
GB = GC // P
CHUNKS = NP // GC
MASKS = 4
SG = 5
REACH = 80.0
TINY = 1e-37
RMAX = bass.bass_isa.ReduceOp.max


def spread(ap, n, width):
    return ap.rearrange("p (n o) -> p n o", o=1).to_broadcast([P, n, width])


def attention_terms(nc, tag, feat, att_src, att_dst, ident, t, er_rows, loops):
    with ExitStack() as ctx:
        s = Scope(nc, ctx, tag)
        al = s.sb("al", [P, 256], F32)
        ar = s.sb("ar", [P, 256], F32)
        tmp = s.sb("tmp", [P, 2, 5 * 256], F32)
        ext = s.sb("ext", [P, 12], F32)
        ext_all = s.sb("ext_all", [P, 8], F32)
        mid = s.sb("mid", [P, H], F32)
        cen = s.sb("cen", [P, NB, H], F32)
        z = s.sb("z", [P, NB, H], F32)
        z2 = s.sb("z2", [P, NB, H], F32)
        top = s.sb("top", [P, NB, H], F32)
        e = s.sb("e", [P, NB, H], F32)
        e2 = s.sb("e2", [P, NB, H], F32)
        er_t = s.sb("er_t", [P, P], F32)
        ps = s.ps("ps", [P, 512])
        att_in, step_s, ext_ready, ext_done, er_turned, er_copied, er_out, exps = (s.sem(n) for n in (
            "att_in", "step", "ext_ready", "ext_done", "er_turned", "er_copied", "er_out", "exps"))
        el, er, nel, u, u2, v, v2, ws = (t[k] for k in ("el", "er", "nel", "u", "u2", "v", "v2", "ws"))
        block = ctx.enter_context(nc.Block())

        @block.sync
        def _(sync):
            sync.dma_start(al[:], att_src.rearrange("h (o d) -> o (h d)", o=1).to_broadcast([P, 256])).then_inc(att_in, 16)
            sync.dma_start(ar[:], att_dst.rearrange("h (o d) -> o (h d)", o=1).to_broadcast([P, 256])).then_inc(att_in, 16)
            sync.wait_ge(er_copied, 1)
            sync.dma_start(er_rows, er_t[0:NB * H, :]).then_inc(er_out, 16)
            sync.wait_ge(er_out, 16)

        @block.gpsimd
        def _(pool):
            pool.wait_ge(ext_ready, 1)
            pool.partition_all_reduce(ext_all[:], ext[:, 0:8], P, RMAX).then_inc(ext_done, 1)

        @block.tensor
        def _(pe):
            pe.wait_ge(step_s, 20)
            pe.transpose(ps[0:NB * H, 0:P], er[:].rearrange("p b h -> p (b h)"), ident[:]).then_inc(er_turned, 1)

        CEN, ZV, Z2V, SELF = 27, 31, 32, 36

        @block.scalar
        def _(act):
            act.wait_ge(step_s, CEN)
            act.activation(u[:], cen[:], ACT.Exp).then_inc(exps, 1)
            act.activation(u2[:], cen[:], ACT.Exp, scale=0.2).then_inc(exps, 1)
            act.wait_ge(step_s, Z2V)
            act.activation(v[:], z[:].rearrange("p b h -> p h b"), ACT.Exp).then_inc(exps, 1)
            act.activation(v2[:], z2[:].rearrange("p b h -> p h b"), ACT.Exp).then_inc(exps, 1)
            if loops:
                act.wait_ge(step_s, SELF)
                act.activation(ws[:], e[:].rearrange("p b h -> p h b"), ACT.Exp).then_inc(exps, 1)
            act.wait_ge(exps, 5 if loops else 4)

        @block.vector
        def _(dve):
            step = Count(step_s)

            def do(ins):
                step.add(ins)

            def link(ins):
                step.add(ins)
                dve.wait_ge(step.sem, step.n)
            dve.wait_ge(att_in, 32)
            for k, (w, to) in enumerate(((ar, er), (al, el))):
                for g in range(5):
                    b = slice(5 * g, 5 * g + 5)
                    tm = tmp[:, g % 2, :]
                    link(dve.tensor_tensor(tm.rearrange("p (b f) -> p b f", b=5), feat[:, b, :],
                                           w[:].rearrange("p (o f) -> p o f", o=1).to_broadcast([P, 5, 256]), ALU.mult))
                    do(dve.tensor_reduce(to[:, b, :].rearrange("p b h -> p (b h)"), tm.rearrange("p (n d) -> p n d", d=D), AX.X, ALU.add))
                dve.wait_ge(step.sem, step.n)
            by_head = el[:].rearrange("p b h -> p h b")
            do(dve.tensor_reduce(ext[:, 0:4], by_head, AX.X, ALU.max))
            link(dve.tensor_reduce(ext[:, 8:12], by_head, AX.X, ALU.min))
            dve.tensor_scalar(ext[:, 4:8], ext[:, 8:12], -1.0, None, ALU.mult).then_inc(ext_ready, 1)
            do(dve.tensor_scalar(nel[:], el[:], -1.0, None, ALU.mult))
            dve.wait_ge(er_turned, 1)
            dve.tensor_copy(er_t[0:NB * H, :], ps[0:NB * H, 0:P]).then_inc(er_copied, 1)
            dve.wait_ge(ext_done, 1)
            link(dve.tensor_tensor(mid[:], ext_all[:, 0:4], ext_all[:, 4:8], ALU.subtract))
            link(dve.tensor_scalar(mid[:], mid[:], 0.5, None, ALU.mult))
            link(dve.scalar_tensor_tensor(mid[:], ext_all[:, 0:4], -REACH, mid[:], ALU.add, ALU.max))
            mid_all = mid[:].rearrange("p (o h) -> p o h", o=1).to_broadcast([P, NB, H])
            do(dve.tensor_tensor(cen[:], el[:], mid_all, ALU.subtract))
            assert step.n == CEN
            link(dve.tensor_tensor(z[:], er[:], mid_all, ALU.add))
            link(dve.tensor_scalar(z2[:], z[:], 0.2, None, ALU.mult))
            link(dve.tensor_tensor(top[:], z[:], z2[:], ALU.max))
            do(dve.tensor_tensor(z[:], z[:], top[:], ALU.subtract))
            assert step.n == ZV
            do(dve.tensor_tensor(z2[:], z2[:], top[:], ALU.subtract))
            assert step.n == Z2V
            if loops:
                link(dve.tensor_tensor(e[:], el[:], er[:], ALU.add))
                link(dve.tensor_scalar(e2[:], e[:], 0.2, None, ALU.mult))
                link(dve.tensor_tensor(e[:], e[:], e2[:], ALU.max))
                do(dve.tensor_tensor(e[:], e[:], top[:], ALU.subtract))
                assert step.n == SELF
            dve.wait_ge(step.sem, step.n)


def weighted_features(nc, tag, feat, t, parts):
    with ExitStack() as ctx:
        s = Scope(nc, ctx, tag)
        whole = s.sb("whole", [P, 2, 5, H, DW], F32)
        rest = s.sb("rest", [P, 2, 5, H, DW], F32)
        scaled, hi_done, rest_done, mid_done, lo_done = (s.sem(n) for n in ("scaled", "hi_done", "rest_done", "mid_done", "lo_done"))
        block = ctx.enter_context(nc.Block())
        items = [(g, side) for g in range(5) for side in range(2)]

        def part(n, j):
            g, side = items[n]
            return parts[:, 5 * g:5 * g + 5, side, :, j * DW:(j + 1) * DW]

        @block.vector
        def _(dve):
            def scale(n):
                g, side = items[n]
                b = slice(5 * g, 5 * g + 5)
                w = t["u"] if side == 0 else t["u2"]
                if n >= 2:
                    dve.wait_ge(hi_done, n - 1)
                    dve.wait_ge(rest_done, n - 1)
                dve.tensor_tensor(whole[:, n % 2, :, :, 0:D].rearrange("p b h d -> p (b h) d"), feat[:, b, :].rearrange("p b (h d) -> p (b h) d", h=H),
                                  spread(w[:, b, :].rearrange("p b h -> p (b h)"), 5 * H, D), ALU.mult).then_inc(scaled, 1)
                dve.tensor_copy(whole[:, n % 2, :, :, D], w[:, b, :]).then_inc(scaled, 1)

            def rest_of(n):
                dve.wait_ge(hi_done, n + 1)
                if n >= 2:
                    dve.wait_ge(mid_done, n - 1)
                    dve.wait_ge(lo_done, n - 1)
                dve.tensor_tensor(rest[:, n % 2], whole[:, n % 2], part(n, 0), ALU.subtract).then_inc(rest_done, 1)

            def low(n):
                dve.wait_ge(mid_done, n + 1)
                dve.tensor_tensor(part(n, 2), rest[:, n % 2], part(n, 1), ALU.subtract).then_inc(lo_done, 1)
            for n in range(12):
                if n < 10:
                    scale(n)
                if 1 <= n <= 10:
                    rest_of(n - 1)
                if n >= 2:
                    low(n - 2)
            dve.wait_ge(lo_done, 10)

        @block.scalar
        def _(act):
            for n in range(11):
                if n < 10:
                    act.wait_ge(scaled, 2 * n + 2)
                    act.copy(part(n, 0), whole[:, n % 2]).then_inc(hi_done, 1)
                if n >= 1:
                    act.wait_ge(rest_done, n)
                    act.copy(part(n - 1, 1), rest[:, (n - 1) % 2]).then_inc(mid_done, 1)


def attend(nc, tag, table, t, parts, er_rows, h, residual, loops=None):
    with ExitStack() as ctx:
        s = Scope(nc, ctx, tag)
        cols = s.sb("cols", [P, NB, GC], F16)
        er = s.sb("er", [P, H, GC], F32)
        pos = s.sb("pos", [P, MASKS, GC], F16)
        neg = s.sb("neg", [P, MASKS, GC], F16)
        taken = s.sb("taken", [P, 2, GB, 2 * HW], F32)
        total = s.sb("total", [P, GB, DW], F32)
        den = s.sb("den", [P, GB], F32)
        rden = s.sb("rden", [P, GB], F32)
        own = s.sb("own", [P, GB, D], F32)
        quot = s.sb("quot", [P, 2, GB, D], F32)
        ps = s.ps("ps", [P, 2 * GB, 512])
        col_in = [s.sem(f"col_in{g}") for g in range(NB // SG)]
        er_in = [s.sem(f"er_in{k}") for k in range(H)]
        masks_ready, masks_free, step_s, item_taken, reduced, quot_ready, h_out, pe_pass, act_pass = (s.sem(n) for n in (
            "masks_ready", "masks_free", "step", "item_taken", "reduced", "quot_ready", "h_out", "pe_pass", "act_pass"))
        block = ctx.enter_context(nc.Block())
        tab = table.rearrange("(b p) d -> p b d", p=P)
        er_v = er_rows.rearrange("(b h) p -> h b p", h=H)

        @block.sync
        def _(sync):
            def load_cols(g, at, width):
                sync.dma_start(cols[:, SG * g:SG * g + SG, 0:width], tab[:, SG * g:SG * g + SG, at]).then_inc(col_in[g], 16)

            def load_er(k, at, nblk):
                sync.dma_start(er[:, k, 0:nblk * P].rearrange("p (b q) -> p b q", b=nblk),
                               er_v[k:k + 1, at, :].to_broadcast([P, nblk, P])).then_inc(er_in[k], 16)
            for g in range(NB // SG):
                load_cols(g, slice(0, GC), GC)
                if g < H:
                    load_er(g, slice(0, GB), GB)
            with sync.Fori(0, CHUNKS - 1) as i:
                for k in range(H - 1):
                    sync.wait_ge(masks_ready, (i * H + k + 1) * NB)
                    load_er(k, bass.ds((i + 1) * GB, GB), GB)
                for g in range(NB // SG):
                    sync.wait_ge(masks_ready, (i * H + H - 1) * NB + SG * (g + 1))
                    load_cols(g, bass.ds((i + 1) * GC, GC), GC)
                load_er(H - 1, bass.ds((i + 1) * GB, GB), GB)
            i = CHUNKS - 1
            for k in range(H):
                sync.wait_ge(masks_ready, (i * H + k + 1) * NB)
                load_er(k, slice(CHUNKS * GB, NB), 1)
            for g in range(NB // SG):
                load_cols(g, slice(CHUNKS * GC, NP), P)

        @block.tensor
        def _(pe):
            pe.sem_inc(masks_free, MASKS)

            def item(n, k, nblk):
                pe.wait_ge(item_taken, n + 1)
                pe.sem_inc(pe_pass, 1)
                for b in range(NB):
                    at = n * NB + b
                    slot = (k * NB + b) % MASKS
                    pe.wait_ge(masks_ready, at + 1)
                    pe.sem_inc(pe_pass, 1)
                    for j in range(nblk):
                        bank = ps[:, (k % 2) * GB + j, :]
                        pe.matmul(bank[:, 0:HW], pos[:, slot, j * P:(j + 1) * P], parts[:, b, 0, k, :],
                                  start=(b == 0), stop=False, skip_group_check=True)
                        last = pe.matmul(bank[:, HW:2 * HW], neg[:, slot, j * P:(j + 1) * P], parts[:, b, 1, k, :],
                                         start=False, stop=(b == NB - 1), skip_group_check=True)
                    last.then_inc(masks_free, 1)
            with pe.Fori(0, CHUNKS) as i:
                for k in range(H):
                    item(i * H + k, k, GB)
            for k in range(H):
                item(CHUNKS * H + k, k, 1)

        @block.scalar
        def _(act):
            act.sem_inc(item_taken, 2)

            def item(n, k, blocks, nblk, first):
                act.wait_ge(masks_free, (n + 1) * NB + MASKS)
                act.sem_inc(act_pass, 1)
                act.wait_ge(reduced, n + 1)
                act.sem_inc(act_pass, 1)
                for j in range(nblk):
                    bank = ps[:, (k % 2) * GB + j, :]
                    for side, w in enumerate((t["v"], t["v2"])):
                        last = act.activation(taken[:, k % 2, j, side * HW:(side + 1) * HW], bank[:, side * HW:(side + 1) * HW],
                                              ACT.Copy, scale=w[:, k, blocks(j)])
                last.then_inc(item_taken, 1)
            def put(n, k, at):
                act.wait_ge(quot_ready, n + 1)
                act.sem_inc(act_pass, 1)
                nblk = GB if at is not None else 1
                rows = at if at is not None else slice(NB - 1, NB)
                act.activation(h[:, rows, k * D:(k + 1) * D], quot[:, k % 2, 0:nblk, :], ACT.Relu).then_inc(h_out, 1)
            with act.Fori(0, CHUNKS) as i:
                for k in range(H):
                    item(i * H + k, k, lambda j: bass.ds(i * GB + j, 1), GB, False)
                    if loops is None and k >= 1:
                        put(i * H + k - 1, k - 1, bass.ds(i * GB, GB))
                if loops is None:
                    put(i * H + H - 1, H - 1, bass.ds(i * GB, GB))
            for k in range(H):
                item(CHUNKS * H + k, k, lambda j: slice(NB - 1, NB), 1, False)
                if loops is None:
                    put(CHUNKS * H + k, k, None)

        @block.vector
        def _(dve):
            step = Count(step_s)

            def link(ins):
                step.add(ins)
                dve.wait_ge(step.sem, step.n)
            dve.sem_inc(reduced, 2)
            tail_steps = 8 if loops else (5 if residual else 4)

            def finish(n, k, rows, nblk):
                dve.wait_ge(item_taken, n + 3)
                cols_k = slice(k * D, (k + 1) * D)
                tot = total[:, 0:nblk, :]
                link(dve.tensor_reduce(tot, taken[:, k % 2, 0:nblk, :].rearrange("p j (c f) -> p j f c", c=6), AX.X, ALU.add))
                dve.sem_inc(reduced, 1)
                if loops:
                    w = t["ws"][:, k, rows]
                    link(dve.tensor_tensor(own[:, 0:nblk, :], h[:, rows, cols_k], spread(w, nblk, D), ALU.mult))
                    link(dve.tensor_tensor(tot[:, :, 0:D], tot[:, :, 0:D], own[:, 0:nblk, :], ALU.add))
                    link(dve.tensor_tensor(tot[:, :, D], tot[:, :, D], w, ALU.add))
                link(dve.tensor_scalar(den[:, 0:nblk], tot[:, :, D], TINY, None, ALU.max))
                link(dve.reciprocal(rden[:, 0:nblk], den[:, 0:nblk]))
                q = quot[:, k % 2, 0:nblk, :]
                last = dve.tensor_tensor(q, tot[:, :, 0:D], spread(rden[:, 0:nblk], nblk, D), ALU.mult)
                link(last)
                if loops:
                    link(dve.tensor_tensor(loops[:, rows, cols_k], loops[:, rows, cols_k], q, ALU.add))
                elif residual:
                    link(dve.tensor_tensor(q, q, h[:, rows, cols_k], ALU.add))
                dve.sem_inc(quot_ready, 1)

            def item(n, k, width, late):
                for b in range(NB):
                    at = n * NB + b
                    slot = (k * NB + b) % MASKS
                    if b == 0:
                        dve.wait_ge(er_in[k], late * 16 + 16)
                    if k == 0 and b % SG == 0:
                        dve.wait_ge(col_in[b // SG], late * 16 + 16)
                    dve.wait_ge(masks_free, at + 1)
                    step.add(dve.scalar_tensor_tensor(pos[:, slot, 0:width], er[:, k, 0:width], t["nel"][:, b, k:k + 1],
                                                      cols[:, b, 0:width], ALU.is_gt, ALU.mult))
                    dve.wait_ge(step.sem, step.n)
                    dve.tensor_tensor(neg[:, slot, 0:width], cols[:, b, 0:width], pos[:, slot, 0:width], ALU.subtract).then_inc(masks_ready, 1)
                    if b == 8 and k >= 1:
                        yield
            with dve.Fori(0, CHUNKS) as i:
                step.enter(i, H * (NB + tail_steps))
                rows = bass.ds(i * GB, GB)
                for k in range(H):
                    for _ in item(i * H + k, k, GC, i):
                        finish(i * H + k - 1, k - 1, rows, GB)
                finish(i * H + H - 1, H - 1, rows, GB)
                step.leave(CHUNKS)
            n = CHUNKS * H
            for k in range(H):
                for _ in item(n + k, k, P, CHUNKS):
                    finish(n + k - 1, k - 1, slice(NB - 1, NB), 1)
            finish(n + H - 1, H - 1, slice(NB - 1, NB), 1)


def gat_layer(nc, tag, table, er_rows, h, ident, weights, att_src, att_dst, residual, x=None):
    with ExitStack() as ctx:
        s = Scope(nc, ctx, tag)
        t = {k: s.sb(k, [P, NB, H], F32) for k in ("el", "er", "nel", "u", "u2")}
        t.update({k: s.sb(k, [P, H, NB], F32) for k in ("v", "v2", "ws")})
        parts = s.sb("parts", [P, NB, 2, H, HW], BF16)
        with ExitStack() as inner:
            feat = h if x is not None else inner.enter_context(nc.sbuf_tensor(tag + "_feat", [P, NB, 256], F32))
            project(nc, tag + "p", h, 2, weights, 256, feat, ident)
            attention_terms(nc, tag + "t", feat, att_src, att_dst, ident, t, er_rows, x is not None)
            weighted_features(nc, tag + "w", feat, t, parts)
        attend(nc, tag + "a", table, t, parts, er_rows, h, residual, x)


F1 = 2 * D + 2 * H
EG = 8
MW = H * D + H
CHAINS = 4
ROWS = NP + P
LOWEST = -3.0e38


def source_rows(nc, h, rows, attn, node_rows):
    with ExitStack() as ctx:
        s = Scope(nc, ctx, "l1s")
        at = s.sb("at", [P, H * D], F32)
        tmp = s.sb("tmp", [P, 2, 5, H, D], F32)
        at_in, step_s, out_s = s.sem("at_in"), s.sem("step"), s.sem("out")
        block = ctx.enter_context(nc.Block())

        @block.sync
        def _(sync):
            sync.dma_start(at[:], attn.rearrange("o h d -> o (h d)").to_broadcast([P, H * D])).then_inc(at_in, 16)
            sync.wait_ge(step_s, 20)
            sync.dma_start(rows_of(node_rows), rows[:]).then_inc(out_s, 16)
            sync.wait_ge(out_s, 16)

        @block.vector
        def _(dve):
            dve.wait_ge(at_in, 16)
            step = Count(step_s)
            for n in range(10):
                side, b0 = n // 5, 5 * (n % 5)
                if n >= 2:
                    dve.wait_ge(step_s, step.n)
                tm = tmp[:, n % 2]
                for_heads = rows[:, b0:b0 + 5, side * D:(side + 1) * D].rearrange("p b (o d) -> p b o d", o=1).to_broadcast([P, 5, H, D])
                step.add(dve.tensor_tensor(tm, for_heads, at[:].rearrange("p (o h d) -> p o h d", o=1, h=H).to_broadcast([P, 5, H, D]), ALU.mult))
                dve.wait_ge(step_s, step.n)
                step.add(dve.tensor_reduce(rows[:, b0:b0 + 5, 2 * D + side * H:2 * D + (side + 1) * H],
                                           tm, AX.X, ALU.add))
            dve.wait_ge(step_s, step.n)


def edge_messages(nc, src, attr, node_rows, msg, score):
    groups = T // EG
    with ExitStack() as ctx:
        s = Scope(nc, ctx, "l1g")
        src_i = s.sb("src_i", [P, T], U32)
        at = s.sb("at", [P, T, 2], F32)
        idx = s.sb("idx", [P, 2, EG], U32)
        row = s.sb("row", [P, 2, EG, F1], F32)
        tmp = s.sb("tmp", [P, 2, EG, D], F32)
        tms = s.sb("tms", [P, 2, EG, H], F32)
        loaded, idx_ready, row_done, step_s, pool_pass, act_pass = (s.sem(n) for n in ("loaded", "idx_ready", "row_done", "step", "pool_pass", "act_pass"))
        gathered = [s.pool_dma_sem("gathered0"), s.pool_dma_sem("gathered1")]
        block = ctx.enter_context(nc.Block())

        @block.sync
        def _(sync):
            sync.dma_start(src_i[:], src.bitcast(U32)).then_inc(loaded, 16)
            sync.dma_start(at[:], attr.rearrange("p (t c) -> p t c", c=2)).then_inc(loaded, 16)

        def group(pool, u, g_idx):
            for k in range(EG):
                pool.indirect_dma_start(out=row[:, u, k, :], out_offset=None, in_=node_rows,
                                        in_offset=bass.IndirectOffsetOnAxis(idx[:, u, k:k + 1], 0),
                                        bounds_check=NP - 1).then_inc(gathered[u], 16)

        @block.gpsimd
        def _(pool):
            with pool.Fori(0, groups // 2) as i:
                for u in range(2):
                    pool.wait_ge(idx_ready, i * 2 + u + 1)
                    pool.sem_inc(pool_pass, 1)
                    group(pool, u, None)
            pool.wait_ge(idx_ready, groups)
            group(pool, 0, None)

        @block.scalar
        def _(act):
            act.wait_ge(loaded, 32)
            act.wait_ge(step_s, 2)
            with act.Fori(0, groups // 2) as i:
                for u in range(2):
                    act.wait_ge(row_done, i * 2 + u + 1)
                    act.sem_inc(act_pass, 1)
                    act.copy(idx[:, u, :], src_i[:, bass.ds((i * 2 + u) * EG, EG)]).then_inc(idx_ready, 1)
            act.wait_ge(row_done, groups)
            act.copy(idx[:, 0, :], src_i[:, T - EG:T]).then_inc(idx_ready, 1)

        @block.vector
        def _(dve):
            step = Count(step_s)

            def link(ins):
                step.add(ins)
                dve.wait_ge(step.sem, step.n)
            link(dve.memset(tmp[:], 0.0))
            link(dve.memset(tms[:], 0.0))
            dve.sem_inc(row_done, 2)
            dve.wait_ge(loaded, 32)

            def group(u, tiles, n, turns):
                dve.wait_ge(gathered[u], turns * 16 * EG + 16 * EG)
                for lo, wd, to, tm in ((0, D, msg, tmp), (2 * D, H, score, tms)):
                    a0, a1 = (at[:, tiles, c:c + 1].to_broadcast([P, EG, wd]) for c in range(2))
                    step.add(dve.tensor_tensor(tm[:, u], row[:, u, :, lo + wd:lo + 2 * wd], a1, ALU.mult))
                    link(dve.tensor_tensor(to[:, tiles, :], row[:, u, :, lo:lo + wd], a0, ALU.mult))
                    link(dve.tensor_tensor(to[:, tiles, :], to[:, tiles, :], tm[:, u], ALU.add))
                dve.sem_inc(row_done, 1)
            with dve.Fori(0, groups // 2) as i:
                step.enter(i, 12)
                for u in range(2):
                    group(u, bass.ds((i * 2 + u) * EG, EG), i * 2 + u, i)
                step.leave(groups // 2)
            group(0, slice(T - EG, T), groups - 1, groups // 2)


def edge_weights(nc, score):
    with ExitStack() as ctx:
        s = Scope(nc, ctx, "l1w")
        low = s.sb("low", [P, T, H], F32)
        mx = s.sb("mx", [P, H], F32)
        mx_all = s.sb("mx_all", [P, H], F32)
        step_s, filled, max_ready, max_all, exp_done = (s.sem(n) for n in ("step", "filled", "max_ready", "max_all", "exp_done"))
        block = ctx.enter_context(nc.Block())

        @block.vector
        def _(dve):
            dve.tensor_scalar(low[:], score[:], 0.2, None, ALU.mult).then_inc(step_s, 1)
            dve.wait_ge(step_s, 1)
            dve.tensor_tensor(low[:], score[:], low[:], ALU.max).then_inc(step_s, 1)
            dve.wait_ge(filled, 1)
            dve.tensor_reduce(mx[:], score[:].rearrange("p t h -> p h t"), AX.X, ALU.max).then_inc(max_ready, 1)
            dve.wait_ge(max_all, 1)
            dve.tensor_tensor(low[:], score[:], mx_all[:].rearrange("p (o h) -> p o h", o=1).to_broadcast([P, T, H]), ALU.subtract).then_inc(step_s, 1)

        @block.gpsimd
        def _(pool):
            pool.wait_ge(step_s, 2)
            pool.affine_select(out=score[:], in_=low[:], compare_op=ALU.is_ge, fill=LOWEST, base=E - 1,
                               pattern=[[-1, T], [0, H]], channel_multiplier=-T).then_inc(filled, 1)
            pool.wait_ge(max_ready, 1)
            pool.partition_all_reduce(mx_all[:], mx[:], P, RMAX).then_inc(max_all, 1)

        @block.scalar
        def _(act):
            act.wait_ge(step_s, 3)
            act.activation(score[:], low[:], ACT.Exp).then_inc(exp_done, 1)
            act.wait_ge(exp_done, 1)


def zero_chains(nc, sums):
    with ExitStack() as ctx:
        s = Scope(nc, ctx, "l1z")
        zeros = s.sb("zeros", [P, ROWS // P * MW], F32)
        zset, zout = s.sem("zset"), s.sem("zout")
        block = ctx.enter_context(nc.Block())

        @block.vector
        def _(dve):
            dve.memset(zeros[:], 0.0).then_inc(zset, 1)

        @block.sync
        def _(sync):
            sync.wait_ge(zset, 1)
            for c in range(CHAINS):
                sync.dma_start(sums[c].rearrange("(p r) f -> p (r f)", p=P), zeros[:]).then_inc(zout, 16)
            sync.wait_ge(zout, 16 * CHAINS)


def edge_sums(nc, dst, dst_rows, msg, weight, ident, sums):
    turns = T // CHAINS
    with ExitStack() as ctx:
        s = Scope(nc, ctx, "l1e")
        dst_i = s.sb("dst_i", [P, T], I32)
        dst_f = s.sb("dst_f", [P, T], F32)
        dst_t = s.sb("dst_t", [98, 4, P], F32)
        spare = s.sb("spare", [P, T], F32)
        spare_i = s.sb("spare_i", [P, 1], I32)
        spare_f = s.sb("spare_f", [P, 1], F32)
        before = s.sb("before", [P, P], F32)
        rows = s.sb("rows", [P, 2, CHAINS * P], F32)
        same = s.sb("same", [P, CHAINS, P], F32)
        junk = s.sb("junk", [P, CHAINS, P], F32)
        early = s.sb("early", [P, 2, CHAINS], F32)
        pick = s.sb("pick", [P, 2, CHAINS], F32)
        cell = s.sb("cell", [P, 2, CHAINS], U32)
        value = s.sb("value", [P, CHAINS, MW], F32)
        merged = s.sb("merged", [P, CHAINS, MW], F32)
        ps = s.ps("ps", [P, CHAINS, 512])
        ps_t = s.ps("ps_t", [P, 4, P])
        (loaded, masks_set, key_set, turned, copied, keys_out, step_s, cells_ready, cells_free, value_ready, summed,
         merged_ready, pool_pass, act_pass) = (s.sem(n) for n in (
             "loaded", "masks_set", "key_set", "turned", "copied", "keys_out", "step", "cells_ready", "cells_free",
             "value_ready", "summed", "merged_ready", "pool_pass", "act_pass"))
        row_in = [s.sem("row_in0"), s.sem("row_in1")]
        row_free = s.sem("row_free")
        added = [s.pool_dma_sem(f"added{c}") for c in range(CHAINS)]
        block = ctx.enter_context(nc.Block())

        @block.sync
        def _(sync):
            sync.dma_start(dst_i[:], dst).then_inc(loaded, 16)
            sync.wait_ge(copied, 1)
            sync.dma_start(dst_rows.rearrange("(c t) p -> t c p", c=4), dst_t[:]).then_inc(keys_out, 16)
            sync.wait_ge(keys_out, 16)
            with sync.Fori(0, turns // 2) as i:
                for u in range(2):
                    sync.wait_ge(row_free, i * 2 + u + 1)
                    sync.dma_start(rows[:, u, :], dst_rows[bass.ds((i * 2 + u) * CHAINS, CHAINS), :].rearrange("(a t) p -> a (t p)", a=1).to_broadcast([P, CHAINS * P])).then_inc(row_in[u], 16)

        @block.gpsimd
        def _(pool):
            pool.memset(before[:], 1.0).then_inc(masks_set, 1)
            pool.iota(spare_i[:], pattern=[[0, 1]], base=NP, channel_multiplier=1).then_inc(masks_set, 1)
            pool.wait_ge(masks_set, 2)
            pool.affine_select(out=before[:], in_=before[:], compare_op=ALU.is_gt, fill=0.0, base=0,
                               pattern=[[-1, P]], channel_multiplier=1).then_inc(masks_set, 1)
            with pool.Fori(0, turns // 2) as i:
                for u in range(2):
                    n = i * 2 + u
                    pool.wait_ge(cells_ready, n + 1)
                    pool.sem_inc(pool_pass, 1)
                    for c in range(CHAINS):
                        pool.wait_ge(merged_ready, CHAINS + n * CHAINS + c + 1)
                        pool.sem_inc(pool_pass, 1)
                        pool.wait_ge(added[c], n * 16)
                        if c == CHAINS - 1:
                            pool.sem_inc(cells_free, 1)
                        else:
                            pool.sem_inc(pool_pass, 1)
                        pool.indirect_dma_start(out=sums[c], out_offset=bass.IndirectOffsetOnAxis(cell[:, u, c:c + 1], 0),
                                                in_=merged[:, c, :], in_offset=None, bounds_check=ROWS - 1,
                                                compute_op=ALU.add).then_inc(added[c], 16)
            for c in range(CHAINS):
                pool.wait_ge(added[c], turns * 16)

        @block.tensor
        def _(pe):
            pe.sem_inc(summed, CHAINS)
            pe.wait_ge(key_set, 1)
            for c in range(4):
                last = pe.transpose(ps_t[0:98, c, :], dst_f[:, c * 98:(c + 1) * 98], ident[:])
            last.then_inc(turned, 1)
            with pe.Fori(0, turns) as i:
                for c in range(CHAINS):
                    pe.wait_ge(value_ready, (i * CHAINS + c + 1) * 3)
                    pe.sem_inc(pool_pass, 1)
                    pe.wait_ge(merged_ready, i * CHAINS + c + 1)
                    pe.sem_inc(pool_pass, 1)
                    pe.matmul(ps[:, c, 0:MW], same[:, c, :], value[:, c, :], start=True, stop=True).then_inc(summed, 1)

        @block.scalar
        def _(act):
            act.sem_inc(merged_ready, CHAINS)
            with act.Fori(0, turns) as i:
                for c in range(CHAINS):
                    act.wait_ge(summed, CHAINS + i * CHAINS + c + 1)
                    act.sem_inc(act_pass, 1)
                    act.wait_ge(added[c], i * 16)
                    act.sem_inc(act_pass, 1)
                    act.copy(merged[:, c, :], ps[:, c, 0:MW]).then_inc(merged_ready, 1)

        @block.vector
        def _(dve):
            step = Count(step_s)

            def link(ins):
                step.add(ins)
                dve.wait_ge(step.sem, step.n)
            dve.wait_ge(loaded, 16)
            dve.tensor_copy(dst_f[:], dst_i[:]).then_inc(key_set, 1)
            dve.wait_ge(masks_set, 3)
            link(dve.tensor_copy(spare_f[:], spare_i[:]))
            dve.wait_ge(turned, 1)
            dve.tensor_copy(dst_t[:], ps_t[0:98, :, :]).then_inc(copied, 1)
            dve.wait_ge(key_set, 1)
            link(dve.tensor_scalar(spare[:], dst_f[:], -1.0, spare_f[:, 0:1], ALU.mult, ALU.add))
            dve.sem_inc(row_free, 2)
            with dve.Fori(0, turns // 2) as i:
                step.enter(i, 2 * (CHAINS + 3))
                for u in range(2):
                    n = i * 2 + u
                    dve.wait_ge(row_in[u], i * 16 + 16)
                    for c in range(CHAINS):
                        one = bass.ds(n * CHAINS + c, 1)
                        row = rows[:, u, c * P:(c + 1) * P]
                        step.add(dve.scalar_tensor_tensor(junk[:, c, :], row, dst_f[:, one], before[:],
                                                          ALU.is_equal, ALU.mult, accum_out=early[:, u, c:c + 1]))
                        dve.wait_ge(summed, n * CHAINS + c + 1)
                        dve.tensor_scalar(same[:, c, :], row, dst_f[:, one], None, ALU.is_equal).then_inc(value_ready, 1)
                        w = flat(weight[:, one, :])
                        dve.tensor_tensor(value[:, c, 0:H * D].rearrange("p (h d) -> p h d", h=H), msg[:, one, :].to_broadcast([P, H, D]),
                                          spread(w, H, D), ALU.mult).then_inc(value_ready, 1)
                        dve.tensor_copy(value[:, c, H * D:MW], w).then_inc(value_ready, 1)
                    dve.wait_ge(step.sem, step.n)
                    ts = bass.ds(n * CHAINS, CHAINS)
                    link(dve.tensor_scalar(pick[:, u, :], early[:, u, :], 0.0, None, ALU.is_gt))
                    link(dve.tensor_tensor(pick[:, u, :], pick[:, u, :], spare[:, ts], ALU.mult))
                    dve.wait_ge(cells_free, n)
                    link(dve.tensor_tensor(cell[:, u, :], pick[:, u, :], dst_f[:, ts], ALU.add))
                    dve.sem_inc(cells_ready, 1)
                    dve.wait_ge(value_ready, (n + 1) * CHAINS * 3)
                    dve.sem_inc(row_free, 1)
                step.leave(turns // 2)


def add_quotients(nc, sums, x):
    with ExitStack() as ctx:
        s = Scope(nc, ctx, "l1q")
        part = s.sb("part", [P, CHAINS, NB, MW // 2], F32) if False else s.sb("part", [P, CHAINS, 5, MW], F32)
        rden = s.sb("rden", [P, 5, H], F32)
        part_in, part_free, step_s = s.sem("part_in"), s.sem("part_free"), s.sem("step")
        block = ctx.enter_context(nc.Block())

        @block.sync
        def _(sync):
            for g in range(5):
                if g:
                    sync.wait_ge(part_free, g)
                for c in range(CHAINS):
                    sync.dma_start(part[:, c], rows_of(sums[c][5 * g * P:(5 * g + 5) * P, :])).then_inc(part_in, 16)

        @block.vector
        def _(dve):
            step = Count(step_s)

            def link(ins):
                step.add(ins)
                dve.wait_ge(step.sem, step.n)
            for g in range(5):
                b = slice(5 * g, 5 * g + 5)
                dve.wait_ge(part_in, (g + 1) * CHAINS * 16)
                link(dve.tensor_tensor(part[:, 0], part[:, 0], part[:, 1], ALU.add))
                link(dve.tensor_tensor(part[:, 2], part[:, 2], part[:, 3], ALU.add))
                link(dve.tensor_tensor(part[:, 0], part[:, 0], part[:, 2], ALU.add))
                link(dve.tensor_scalar(rden[:], part[:, 0, :, H * D:MW], 1e-10, None, ALU.add))
                link(dve.reciprocal(rden[:], rden[:]))
                for k in range(5):
                    link(dve.tensor_tensor(part[:, 0, k, 0:H * D].rearrange("p (h d) -> p h d", h=H), part[:, 0, k, 0:H * D].rearrange("p (h d) -> p h d", h=H),
                                           spread(rden[:, k, :], H, D), ALU.mult))
                link(dve.tensor_tensor(x[:, b, :], x[:, b, :], part[:, 0, :, 0:H * D], ALU.add))
                dve.sem_inc(part_free, 1)


def attention_messages(nc, a, x, h, ident):
    node_rows = nc.dram_tensor("node_rows", (NP, F1), F32).ap()
    dst_rows = nc.dram_tensor("dst_rows", (T, P), F32).ap()
    sums = [nc.dram_tensor(f"sums{c}", (ROWS, MW), F32).ap() for c in range(CHAINS)]
    zero_chains(nc, sums)
    normalise(nc, "n1", x, h)
    with ExitStack() as ctx:
        rows = ctx.enter_context(nc.sbuf_tensor("l1_rows", [P, NB, F1], F32))
        project(nc, "pl", h, 2, None, 2 * D, rows, ident, (a["L1_gnn_W_forward"], a["L1_gnn_W_reverse"]))
        source_rows(nc, h, rows, a["L1_gnn_attn_forward"], node_rows)
    with ExitStack() as ctx:
        msg = ctx.enter_context(nc.sbuf_tensor("msg", [P, T, D], F32))
        weight = ctx.enter_context(nc.sbuf_tensor("weight", [P, T, H], F32))
        edge_messages(nc, a["src"], a["edge_attr_2"], node_rows, msg, weight)
        edge_weights(nc, weight)
        edge_sums(nc, a["dst"], dst_rows, msg, weight, ident, sums)
    add_quotients(nc, sums, x)


def program(nc, a, out, dbg):
    table_t = nc.dram_tensor("table", (4 * P, ZW), F16).ap()
    table = table_t.rearrange("a w -> (a w)")[0:NP * NP].rearrange("(s d) -> s d", d=NP)
    key_rows = nc.dram_tensor("key_rows", (T, P), F32).ap()
    adjacency(nc, a["src"], a["dst"], table_t, key_rows)
    with ExitStack() as ctx:
        x = ctx.enter_context(nc.sbuf_tensor("x", [P, NB, 256], F32))
        h = ctx.enter_context(nc.sbuf_tensor("h", [P, NB, 256], F32))
        ident = ctx.enter_context(nc.sbuf_tensor("ident_all", [P, P], F32))
        dinv = ctx.enter_context(nc.sbuf_tensor("dinv", [P, NB], F32))
        load_nodes(nc, x, a["x"], ident)
        with ExitStack() as c0:
            f1 = c0.enter_context(nc.sbuf_tensor("f1", [P, NB, 128], F32))
            degree(nc, table, dinv)
            normalise(nc, "n0", x, h)
            project(nc, "p0", h, 2, a["L0_gnn_W1"], 128, f1, ident)
            gcn_conv(nc, "c0", table, f1, 128, dinv, f1, a["L0_gnn_b1"])
            gcn_conv(nc, "c1", table, f1, 128, dinv, f1)
            project(nc, "p1", f1, 1, a["L0_gnn_W2"], 256, h, ident)
            add_to(nc, "b0", x, h, a["L0_gnn_b2"])
        attention_messages(nc, a, x, h, ident)
        er_rows = nc.dram_tensor("er_rows", (NB * H, P), F32).ap()
        normalise(nc, "n2", x, h)
        for n in range(3):
            gat_layer(nc, f"g{n}", table, er_rows, h, ident, a[f"L2_gnn_W{n}"], a[f"L2_gnn_al{n}"], a[f"L2_gnn_ar{n}"], n < 2)
        add_to(nc, "b2", x, h, None)
        normalise(nc, "n3", x, h)
        gat_layer(nc, "g3", table, er_rows, h, ident, a["L3_gnn_W"], a["L3_gnn_att_src"], a["L3_gnn_att_dst"], False, x)
        add_to(nc, "b3", x, None, a["L3_gnn_bias"])
        store(nc, x, out)


def store(nc, x, out):
    with ExitStack() as ctx:
        s = Scope(nc, ctx, "store")
        stored = s.sem("stored")
        with nc.Block() as block:
            @block.sync
            def _(sync):
                full = (NB - 1) * P
                sync.dma_start(rows_of(out[0:full, :]), x[:, 0:NB - 1, :]).then_inc(stored, 16)
                sync.dma_start(out[full:N, :], x[0:N - full, NB - 1, :]).then_inc(stored, 16)
                sync.wait_ge(stored, 32)


def kernel(**inputs):
    import numpy as np
    import concourse.bacc as bacc
    from concourse.bass_utils import run_bass_kernel_spmd as run
    nc = bacc.Bacc("TRN2", target_bir_lowering=False, num_devices=1)
    arrays = {k: np.ascontiguousarray(v) for k, v in inputs.items()}
    pad = np.full(P * T - E, NP - 1, arrays["src"].dtype)
    for k in ("src", "dst"):
        arrays[k] = np.concatenate([arrays[k], pad]).reshape(P, T)
    arrays["edge_attr_2"] = np.concatenate([arrays["edge_attr_2"], np.zeros((P * T - E, 2), arrays["edge_attr_2"].dtype)]).reshape(P, 2 * T)
    h = {k: nc.dram_tensor("in_" + k, v.shape, mybir.dt.from_np(v.dtype), kind="ExternalInput").ap() for k, v in arrays.items()}
    out = nc.dram_tensor("out", (N, 256), F32, kind="ExternalOutput").ap()
    program(nc, h, out, None)
    r = run(nc, [{"in_" + k: v for k, v in arrays.items()}], core_ids=[0])
    return r.results[0]["out"]
```

```python
from contextlib import ExitStack

import concourse.bass as bass
from concourse import mybir
from concourse.alu_op_type import AluOpType as ALU

ACT = mybir.ActivationFunctionType
AX = mybir.AxisListType
F32 = mybir.dt.float32
F16 = mybir.dt.float16
BF16 = mybir.dt.bfloat16
I32 = mybir.dt.int32
U32 = mybir.dt.uint32
RMAX = bass.bass_isa.ReduceOp.max

P = 128
N = 3125
E = 50000
NB = -(-N // P)
NP = NB * P
T = 392
GT = 14
G = T // GT
SLOTS = 4
RING = GT // 2
TC = T // 4
PAD_ROWS = -(-P * T // NP)
TAB = (NP + PAD_ROWS) * NP
ZD = 8
ZW = TAB // P // ZD
H = 4
D = 64
MW = H * D + H
CHAINS = 7
TURNS_A = G // SLOTS
ROWS = -(-(NP + P) // (TURNS_A * P // 4)) * (TURNS_A * P // 4)
SW = ROWS * MW // TURNS_A // P
assert 2 * SW <= ZW and ROWS * MW == SW * TURNS_A * P and ROWS >= NP + P and P * T >= E and T % GT == 0 and G % SLOTS == 0 and TAB % (P * ZD) == 0 and TAB < 2 ** 24 and T % 8 == 0


def zero_table(nc, zeros, table, table_zero):
    with ExitStack() as ctx:
        s = Scope(nc, ctx, "zero")
        zeros_set = s.sem("zeros_set")
        block = ctx.enter_context(nc.Block())

        @block.vector
        def _(dve):
            dve.memset(zeros[:].bitcast(U32), 0).then_inc(zeros_set, 1)

        @block.scalar
        def _(act):
            act.wait_ge(zeros_set, 1)
            for q in range(ZD):
                act.dma_start(table.rearrange("(q p w) -> q p w", q=ZD, p=P)[q], zeros[:, 0:ZW]).then_inc(table_zero, 16)


def adjacency(nc, src, dst, table, table_zero, zeros, sums, key_rows, ident):
    with ExitStack() as ctx:
        s = Scope(nc, ctx, "adj")
        src_i = s.sb("src_i", [P, T], I32)
        dst_i = s.sb("dst_i", [P, T], I32)
        key = s.sb("key", [P, T], F32)
        key_t = s.sb("key_t", [TC, 4, P], F32)
        slot_i = s.sb("slot_i", [P, T], I32)
        spare = s.sb("spare", [P, T], F32)
        after = s.sb("after", [P, P], BF16)
        pair = s.sb("pair", [P, 4], BF16)
        rows = s.sb("rows", [P, SLOTS, GT * P], F32)
        same = s.sb("same", [P, RING * (GT + 2), P], BF16)
        own = s.sb("own", [P, 2, RING, P], BF16)
        pick = s.sb("pick", [P, SLOTS, GT], F32)
        cell = s.sb("cell", [P, SLOTS, GT], U32)
        value = s.sb("value", [P, SLOTS, GT], F16)
        ps_t = s.ps("ps_t", [P, 4, P])
        ps = s.ps("ps", [P, SLOTS, 512])
        (edges_in, keys_ready, keys_turned, keys_copied, keys_out, consts_set, pair_set, same_ready, same_used, own_ready,
         counted, picked, cells_ready, values_ready, cells_free, row_free, sums_zero, pool_pass, act_pass, sp_pass, pe_pass) = (
             s.sem(n) for n in (
                 "edges_in", "keys_ready", "keys_turned", "keys_copied", "keys_out", "consts_set", "pair_set", "same_ready",
                 "same_used", "own_ready", "counted", "picked", "cells_ready", "values_ready", "cells_free", "row_free", "sums_zero",
                 "pool_pass", "act_pass", "sp_pass", "pe_pass"))
        row_in = [s.sem(f"row_in{u}") for u in range(SLOTS)]
        added = s.pool_dma_sem("added")
        block = ctx.enter_context(nc.Block())
        pieces = [t.rearrange("r f -> (r f)").rearrange("(i p w) -> i p w", i=TURNS_A, p=P) for t in sums]

        @block.sync
        def _(sync):
            sync.dma_start(src_i[:], src).then_inc(edges_in, 16)
            sync.dma_start(dst_i[:], dst).then_inc(edges_in, 16)
            sync.wait_ge(keys_copied, 1)
            sync.dma_start(key_rows.rearrange("(c t) p -> t c p", c=4), key_t[:]).then_inc(keys_out, 16)
            sync.wait_ge(keys_out, 16)
            with sync.Fori(0, TURNS_A) as i:
                for u in range(SLOTS):
                    sync.wait_ge(row_free, i * SLOTS + u + 1)
                    sync.sem_inc(sp_pass, 1)
                    sync.dma_start(rows[:, u, :], key_rows[bass.ds((i * SLOTS + u) * GT, GT), :]
                                   .rearrange("(a t) p -> a (t p)", a=1).to_broadcast([P, GT * P])).then_inc(row_in[u], 16)
                for piece in pieces:
                    sync.dma_start(piece[bass.ds(i, 1)].rearrange("i p w -> (i p) w"), zeros[:, 0:2 * SW].bitcast(F32)).then_inc(sums_zero, 16)
            sync.wait_ge(sums_zero, CHAINS * TURNS_A * 16)

        @block.gpsimd
        def _(pool):
            pool.sem_inc(cells_free, SLOTS)
            pool.memset(after[:], 1.0).then_inc(consts_set, 1)
            pool.iota(slot_i[:], pattern=[[1, T]], base=NP * NP, channel_multiplier=T).then_inc(consts_set, 1)
            pool.wait_ge(consts_set, 2)
            pool.affine_select(out=after[:], in_=after[:], compare_op=ALU.is_gt, fill=0.0, base=0,
                               pattern=[[1, P]], channel_multiplier=-1).then_inc(consts_set, 1)
            pool.wait_ge(table_zero, ZD * 16)
            with pool.Fori(0, TURNS_A) as i:
                for u in range(SLOTS):
                    n = i * SLOTS + u
                    pool.wait_ge(cells_ready, n + 1)
                    pool.sem_inc(pool_pass, 1)
                    pool.wait_ge(values_ready, SLOTS + n + 1)
                    pool.sem_inc(pool_pass, 1)
                    for k in range(GT):
                        pool.indirect_dma_start(out=table.rearrange("(w o) -> w o", o=1),
                                                out_offset=bass.IndirectOffsetOnAxis(cell[:, u, k:k + 1], 0),
                                                in_=value[:, u, k:k + 1], in_offset=None, bounds_check=TAB - 1,
                                                compute_op=ALU.add).then_inc(added, 16)
                    pool.wait_ge(added, (n + 1) * (16 * GT))
                    pool.sem_inc(cells_free, 1)

        @block.tensor
        def _(pe):
            pe.sem_inc(same_used, RING)
            pe.sem_inc(counted, 1)
            pe.wait_ge(keys_ready, 1)
            for c in range(4):
                last = pe.transpose(ps_t[0:TC, c, :], key[:, c * TC:(c + 1) * TC], ident[:])
            last.then_inc(keys_turned, 1)
            both, equal, earlier = pair[:, 0:2], pair[:, 1:3], pair[:, 2:4]
            with pe.Fori(0, TURNS_A) as i:
                for u in range(SLOTS):
                    n = i * SLOTS + u
                    pe.wait_ge(values_ready, n + 1)
                    pe.sem_inc(pe_pass, 1)
                    for half in range(2):
                        for r in range(RING):
                            j = half * RING + r
                            pe.wait_ge(same_ready, n * GT + j + 1)
                            pe.sem_inc(pe_pass, 1)
                            for k in range(GT):
                                last = pe.matmul(ps[:, u, 2 * k:2 * k + 2], same[:, r * GT + k, :], both if j < k else equal,
                                                 start=(j == 0 and k == 0), stop=False, skip_group_check=True)
                            if r < RING - 1:
                                last.then_inc(same_used, 1)
                        last.then_inc(same_used, 1)
                        pe.wait_ge(own_ready, 1 + n * 2 + half + 1)
                        pe.sem_inc(pe_pass, 1)
                        for r in range(RING):
                            k = half * RING + r
                            last = pe.matmul(ps[:, u, 2 * k:2 * k + 2], own[:, half, r, :], earlier, start=False,
                                             stop=(half == 1), skip_group_check=True)
                    last.then_inc(counted, 1)

        @block.scalar
        def _(act):
            act.sem_inc(values_ready, SLOTS)
            with act.Fori(0, TURNS_A) as i:
                for u in range(SLOTS):
                    act.wait_ge(cells_ready, i * SLOTS + u + 1)
                    act.sem_inc(act_pass, 1)
                    act.copy(value[:, u, :], ps[:, u, 0:2 * GT:2]).then_inc(values_ready, 1)

        @block.vector
        def _(dve):
            dve.memset(pair[:], 1.0).then_inc(pair_set, 1)
            dve.wait_ge(pair_set, 1)
            dve.memset(pair[:, 2:3], 0.0).then_inc(pair_set, 1)
            dve.wait_ge(edges_in, 32)
            dve.scalar_tensor_tensor(out=key[:], in0=src_i[:], scalar=float(NP), in1=dst_i[:], op0=ALU.mult,
                                     op1=ALU.add).then_inc(keys_ready, 1)
            dve.wait_ge(keys_ready, 1)
            dve.wait_ge(consts_set, 3)
            dve.tensor_tensor(spare[:], slot_i[:], key[:], ALU.subtract).then_inc(keys_ready, 1)
            dve.wait_ge(keys_turned, 1)
            dve.tensor_copy(key_t[:], ps_t[0:TC, :, :]).then_inc(keys_copied, 1)
            dve.wait_ge(keys_ready, 2)
            dve.wait_ge(pair_set, 2)
            dve.sem_inc(row_free, SLOTS)
            dve.sem_inc(own_ready, 1)

            def cells(n, u):
                ts = bass.ds(n * GT, GT)
                dve.wait_ge(counted, 1 + n + 1)
                dve.wait_ge(cells_free, n + 1)
                dve.scalar_tensor_tensor(pick[:, u, :], ps[:, u, 1:2 * GT:2], 0.0, spare[:, ts], ALU.is_gt, ALU.mult).then_inc(picked, 1)
                dve.wait_ge(picked, n + 1)
                dve.tensor_tensor(cell[:, u, :], pick[:, u, :], key[:, ts], ALU.add).then_inc(cells_ready, 1)
            with dve.Fori(0, TURNS_A) as i:
                for u in range(SLOTS):
                    n = i * SLOTS + u
                    dve.wait_ge(row_in[u], i * 16 + 16)
                    for half in range(2):
                        dve.wait_ge(own_ready, 1 + n * 2 + half)
                        for r in range(RING):
                            j = half * RING + r
                            dve.wait_ge(same_used, n * GT + j + 1)
                            dve.tensor_scalar(same[:, r * GT:(r + 1) * GT, :].rearrange("p k q -> p (k q)"), rows[:, u, :],
                                              key[:, bass.ds(n * GT + j, 1)], None, ALU.is_equal).then_inc(same_ready, 1)
                        dve.wait_ge(same_ready, n * GT + (half + 1) * RING)
                        if half == 0:
                            dve.wait_ge(counted, n + 1)
                        diagonal = same[:, half * RING:half * RING + RING * (GT + 1), :].rearrange(
                            "p (r k) q -> p r k q", r=RING)[:, :, 0, :]
                        dve.tensor_tensor(own[:, half], diagonal, after[:].rearrange("p (o q) -> p o q", o=1).to_broadcast([P, RING, P]),
                                          ALU.mult).then_inc(own_ready, 1)
                    dve.sem_inc(row_free, 1)
                    cells(n, u)


class Count:

    def __init__(self, sem, n=0):
        self.sem, self.n = sem, n

    def add(self, ins, by=1):
        ins.then_inc(self.sem, by)
        self.n = self.n + by
        return self.n

    def enter(self, i, per):
        self.start, self.per = self.n, per
        self.n = self.n + i * per

    def leave(self, turns):
        self.n = self.start + turns * self.per


class Scope:

    def __init__(self, nc, ctx, tag):
        self.nc, self.ctx, self.tag, self.sems = nc, ctx, tag, []
        ctx.callback(self.release)

    def release(self):
        nums = sorted(x.num for x in self.sems)
        while nums:
            k = 1
            while k < len(nums) and nums[k] == nums[0] + k:
                k += 1
            self.nc.gpsimd.sem_clear(range(nums[0], nums[0] + k))
            nums = nums[k:]
        for x in self.sems:
            self.nc.release_semaphore(x)

    def sb(self, name, shape, dt):
        return self.ctx.enter_context(self.nc.sbuf_tensor(f"{self.tag}_{name}", shape, dt))

    def ps(self, name, shape, dt=F32):
        return self.ctx.enter_context(self.nc.psum_tensor(f"{self.tag}_{name}", shape, dt))

    def sem(self, name):
        self.sems.append(self.nc.alloc_semaphore(f"{self.tag}_{name}"))
        return self.sems[-1]

    def pool_dma_sem(self, name):
        return self.nc.alloc_semaphore(f"{self.tag}_{name}")


def rows_of(ap):
    return ap.rearrange("(b p) f -> p b f", p=P)


def load_nodes(nc, x, x_in, w, w_in, ident):
    with ExitStack() as ctx:
        s = Scope(nc, ctx, "load")
        zeroed, x_loaded, ident_set = s.sem("zeroed"), s.sem("x_loaded"), s.sem("ident_set")
        block = ctx.enter_context(nc.Block())

        @block.vector
        def _(dve):
            dve.memset(x[:, NB - 1, :], 0.0).then_inc(zeroed, 1)

        @block.sync
        def _(sync):
            full = (NB - 1) * P
            sync.dma_start(x[:, 0:NB - 1, :], rows_of(x_in[0:full, :])).then_inc(x_loaded, 16)
            sync.wait_ge(zeroed, 1)
            sync.dma_start(x[0:N - full, NB - 1, :], x_in[full:N, :]).then_inc(x_loaded, 16)
            sync.dma_start(w[:], w_in.rearrange("(k p) n -> p k n", p=P)).then_inc(x_loaded, 16)
            sync.wait_ge(x_loaded, 48)

        @block.gpsimd
        def _(pool):
            pool.memset(ident[:], 0.0).then_inc(ident_set, 1)
            pool.wait_ge(ident_set, 1)
            pool.affine_select(out=ident[:], in_=ident[:], compare_op=ALU.not_equal, fill=1.0, base=0,
                               pattern=[[-1, P]], channel_multiplier=1).then_inc(ident_set, 1)
            pool.wait_ge(ident_set, 2)


def normalise(nc, tag, x, h):
    with ExitStack() as ctx:
        s = Scope(nc, ctx, tag)
        stats = s.sb("stats", [P, NB, 6], F32)
        mv = s.sb("mv", [P, NB, 2], F32)
        sd = s.sb("sd", [P, NB], F32)
        rstd = s.sb("rstd", [P, NB], F32)
        shift = s.sb("shift", [P, NB], F32)
        eps = s.sb("eps", [P, 1], F32)
        eps_set, stats_ready, mv_ready = s.sem("eps_set"), s.sem("stats_ready"), s.sem("mv_ready")
        sd_ready, rstd_ready, shift_ready, h_done = (s.sem(n) for n in ("sd_ready", "rstd_ready", "shift_ready", "h_done"))
        block = ctx.enter_context(nc.Block())

        @block.vector
        def _(dve):
            dve.memset(eps[:], 1e-5).then_inc(eps_set, 1)
            for b in range(NB):
                dve.bn_stats(stats[:, b, :], x[:, b, :]).then_inc(stats_ready, 1)
            dve.wait_ge(stats_ready, NB)
            for b in range(NB):
                dve.bn_aggr(mv[:, b, :], stats[:, b, :]).then_inc(mv_ready, 1)
            dve.wait_ge(sd_ready, 1)
            dve.reciprocal(rstd[:], sd[:]).then_inc(rstd_ready, 1)
            dve.wait_ge(rstd_ready, 1)
            dve.scalar_tensor_tensor(shift[:], mv[:, :, 0], -1.0, rstd[:], ALU.mult, ALU.mult).then_inc(shift_ready, 1)

        @block.scalar
        def _(act):
            act.wait_ge(eps_set, 1)
            act.wait_ge(mv_ready, NB)
            act.activation(sd[:], mv[:, :, 1], ACT.Sqrt, bias=eps[:, 0:1]).then_inc(sd_ready, 1)
            act.wait_ge(shift_ready, 1)
            for b in range(NB):
                act.activation(h[:, b, :], x[:, b, :], ACT.Relu, bias=shift[:, b:b + 1],
                               scale=rstd[:, b:b + 1]).then_inc(h_done, 1)
            act.wait_ge(h_done, NB)


UN = 4


def project(nc, tag, h, kk, weights, width, out, ident, stacked=None, loaded=None, attention=None, shared=None):
    full = width + (2 * H if attention or shared is not None else 0)
    with ExitStack() as ctx:
        s = Scope(nc, ctx, tag)
        w = loaded if loaded is not None else s.sb("w", [P, kk, full], F32)
        raw = s.sb("raw", [P, kk * P], F32) if stacked else None
        vectors = s.sb("vectors", [P, 2, H * D], F32) if full > width else None
        products = s.sb("products", [P, 2, kk, H * D], F32) if full > width else None
        turned = s.sb("turned", [P, UN, kk * P], F32)
        ps_t = s.ps("ps_t", [P, UN, 512])
        ps_o = s.ps("ps_o", [P, UN, 512])
        w_in, w_ready, w_turned, w_multiplied = s.sem("w_in"), s.sem("w_ready"), s.sem("w_turned"), s.sem("w_multiplied")
        turn_ready, turn_copied, made, taken = (s.sem(n) for n in (
            "turn_ready", "turn_copied", "made", "taken"))
        block = ctx.enter_context(nc.Block())

        @block.sync
        def _(sync):
            if stacked:
                sync.dma_start(raw[0:64, :], stacked[0]).then_inc(w_in, 16)
                sync.dma_start(raw[64:P, :], stacked[1]).then_inc(w_in, 16)
                sync.dma_start(vectors[:, 0, :], shared.rearrange("o h d -> o (h d)").to_broadcast([P, H * D])).then_inc(w_in, 16)
            elif loaded is None:
                sync.dma_start(w[:, :, 0:width], weights.rearrange("(k p) n -> p k n", p=P)).then_inc(w_in, 16)
            if attention:
                for k in range(2):
                    sync.dma_start(vectors[:, k, :], attention[k].rearrange("h (o d) -> o (h d)", o=1).to_broadcast([P, width])).then_inc(w_in, 16)

        @block.tensor
        def _(pe):
            if stacked:
                pe.wait_ge(w_in, 48)
                for k in range(kk):
                    last = pe.transpose(ps_o[:, 0, k * P:(k + 1) * P], raw[:, k * P:(k + 1) * P], ident[:])
                last.then_inc(w_turned, 1)
            for n in range(NB + 2):
                if n < NB:
                    if n >= UN:
                        pe.wait_ge(turn_copied, n - UN + 1)
                    for k in range(kk):
                        last = pe.transpose(ps_t[:, n % UN, k * P:(k + 1) * P], h[:, n, k * P:(k + 1) * P], ident[:])
                    last.then_inc(turn_ready, 1)
                if n == 1:
                    if stacked:
                        pe.wait_ge(w_ready, 3)
                    elif attention:
                        pe.wait_ge(w_ready, 2)
                    elif loaded is None:
                        pe.wait_ge(w_in, 16)
                if n >= 2:
                    b = n - 2
                    pe.wait_ge(turn_copied, b + 1)
                    if b >= UN:
                        pe.wait_ge(taken, (b - UN + 1) * (2 if attention else 1))
                    for k in range(kk):
                        last = pe.matmul(ps_o[:, b % UN, 0:full], turned[:, b % UN, k * P:(k + 1) * P], w[:, k, :],
                                         start=(k == 0), stop=(k == kk - 1))
                    last.then_inc(made, 1)

        @block.scalar
        def _(act):
            for n in range(NB):
                act.wait_ge(turn_ready, n + 1)
                if n >= UN:
                    act.wait_ge(made, n - UN + 1)
                act.copy(turned[:, n % UN, :], ps_t[:, n % UN, 0:kk * P]).then_inc(turn_copied, 1)

        @block.vector
        def _(dve):
            if stacked:
                dve.wait_ge(w_turned, 1)
                dve.tensor_copy(w[:, :, 0:width], ps_o[:, 0, 0:kk * P].rearrange("p (k n) -> p k n", k=kk)).then_inc(w_ready, 1)
                dve.wait_ge(w_ready, 1)
                by_head = [P, kk, H, D]
                for k in range(2):
                    dve.tensor_tensor(products[:, k].rearrange("p c (h d) -> p c h d", h=H),
                                      w[:, :, k * D:(k + 1) * D].rearrange("p c (o d) -> p c o d", o=1).to_broadcast(by_head),
                                      vectors[:, 0, :].rearrange("p (o h d) -> p o h d", o=1, h=H).to_broadcast(by_head),
                                      ALU.mult).then_inc(w_multiplied, 1)
            if attention:
                dve.wait_ge(w_in, 48)
                for k in range(2):
                    dve.tensor_tensor(products[:, k], w[:, :, 0:width], vectors[:, k:k + 1, :].to_broadcast([P, kk, width]),
                                      ALU.mult).then_inc(w_multiplied, 1)
            if full > width:
                for k in range(2):
                    dve.wait_ge(w_multiplied, k + 1)
                    dve.tensor_reduce(w[:, :, width + k * H:width + (k + 1) * H], products[:, k].rearrange("p c (h d) -> p c h d", h=H),
                                      AX.X, ALU.add).then_inc(w_ready, 1)
            for n in range(NB):
                dve.wait_ge(made, n + 1)
                own = width if attention else full
                dve.tensor_copy(out[:, n, 0:own], ps_o[:, n % UN, 0:own]).then_inc(taken, 1)
                if attention:
                    dve.tensor_copy(attention[2][:, :, n, :], ps_o[:, n % UN, width:full].rearrange("p (k h) -> p k h", k=2)).then_inc(taken, 1)
            dve.wait_ge(taken, NB * (2 if attention else 1))


CW = 256
CS = 4
CBLK = CW // P
TURN = CS * CBLK
TURNS = NB // TURN


def gcn_pass(nc, tag, table, rhs, width, emit, extra=None, other=None):
    assert TURNS * TURN + 1 == NB
    with ExitStack() as ctx:
        s = Scope(nc, ctx, tag)
        cols = s.sb("cols", [P, CS, NB, CW], F16)
        more = s.sb("more", [P, CS, NB, CW], F16) if other is not None else None
        ps = s.ps("ps", [P, TURN, 512])
        chunk_in = [s.sem(f"chunk_in{u}") for u in range(CS)]
        chunk_free = s.sem("chunk_free")
        sp_pass = s.sem("sp_pass")
        added, stored = s.sem("added"), [s.sem(f"stored{u}") for u in range(CS)]
        summed, bank_free, pe_pass, dve_step = s.sem("summed"), s.sem("bank_free"), s.sem("pe_pass"), s.sem("dve_step")
        scratch = extra(s) if extra else None
        block = ctx.enter_context(nc.Block())
        tab = table.rearrange("(b p) d -> p b d", p=P)
        ready = (lambda u, i, n: (added, n + 1)) if other is not None else (lambda u, i, n: (chunk_in[u], i * 16 + 16))

        def load(sync, u, at, width):
            sync.dma_start(cols[:, u, :, 0:width], tab[:, :, at]).then_inc(chunk_in[u], 16)
            if other is not None:
                sync.dma_start(more[:, u, :, 0:width], other.rearrange("(b p) d -> p b d", p=P)[:, :, at]).then_inc(chunk_in[u], 16)

        @block.scalar
        def _(act):
            if other is None:
                return
            with act.Fori(0, TURNS) as i:
                for u in range(CS):
                    act.wait_ge(added, i * CS + u + 1)
                    act.dma_start(tab[:, :, bass.ds((i * CS + u) * CW, CW)], cols[:, u]).then_inc(stored[u], 16)
            act.wait_ge(added, TURNS * CS + 1)
            act.dma_start(tab[:, :, TURNS * TURN * P:NB * P], cols[:, 0, :, 0:P]).then_inc(stored[0], 16)
            for u in range(CS):
                act.wait_ge(stored[u], TURNS * 16 + (16 if u == 0 else 0))

        @block.sync
        def _(sync):
            with sync.Fori(0, TURNS) as i:
                for u in range(CS):
                    sync.wait_ge(chunk_free, i * CS + u + 1)
                    sync.sem_inc(sp_pass, 1)
                    if other is not None:
                        sync.wait_ge(stored[u], i * 16)
                        sync.sem_inc(sp_pass, 1)
                    load(sync, u, bass.ds((i * CS + u) * CW, CW), CW)
            sync.wait_ge(chunk_free, TURNS * CS + 1)
            if other is not None:
                sync.wait_ge(stored[0], TURNS * 16)
            load(sync, 0, slice(TURNS * TURN * P, NB * P), P)

        @block.tensor
        def _(pe):
            pe.sem_inc(chunk_free, CS)

            def one(u, j, bank):
                for b in range(NB):
                    last = pe.matmul(ps[:, bank, 0:width], cols[:, u, b, j * P:(j + 1) * P], rhs[:, b, :],
                                     start=(b == 0), stop=(b == NB - 1))
                last.then_inc(summed, 1)
                return last
            with pe.Fori(0, TURNS) as i:
                for u in range(CS):
                    pe.wait_ge(*ready(u, i, i * CS + u))
                    for j in range(CBLK):
                        bank = u * CBLK + j
                        pe.wait_ge(bank_free, i * TURN + bank + 1)
                        pe.sem_inc(pe_pass, 1)
                        one(u, j, bank)
                    pe.wait_ge(summed, i * TURN + bank + 1)
                    pe.sem_inc(chunk_free, 1)
            pe.wait_ge(*ready(0, TURNS, TURNS * CS))
            pe.wait_ge(bank_free, TURNS * TURN + 1)
            one(0, 0, 0)

        def add(dve, u, turn, width):
            dve.wait_ge(chunk_in[u], turn * 32 + 32)
            dve.tensor_tensor(cols[:, u, :, 0:width], cols[:, u, :, 0:width], more[:, u, :, 0:width], ALU.add).then_inc(added, 1)

        @block.vector
        def _(dve):
            dve.sem_inc(bank_free, TURN)
            step = Count(dve_step)
            per = emit(None, 0, 0, Count(dve_step), scratch)
            with dve.Fori(0, TURNS) as i:
                step.enter(i, TURN * per)
                for bank in range(TURN):
                    if other is not None and bank % CBLK == 0:
                        add(dve, bank // CBLK, i, CW)
                    dve.wait_ge(summed, i * TURN + bank + 1)
                    emit(dve, bass.ds(i * TURN + bank, 1), ps[:, bank, :], step, scratch)
                    dve.sem_inc(bank_free, 1)
                step.leave(TURNS)
            if other is not None:
                add(dve, 0, TURNS, P)
            dve.wait_ge(summed, NB)
            emit(dve, slice(NB - 1, NB), ps[:, 0, :], step, scratch)


def flat(ap):
    return ap.rearrange("p a f -> p (a f)")


def degree(nc, table, other, dinv):
    with ExitStack() as ctx:
        s = Scope(nc, ctx, "deg")
        ones = s.sb("ones", [P, NB, 1], F16)
        deg = s.sb("deg", [P, NB], F32)
        root = s.sb("root", [P, NB], F32)
        set_, rooted, done = s.sem("set"), s.sem("rooted"), s.sem("done")
        with nc.Block() as block:
            @block.vector
            def _(dve):
                dve.memset(ones[:], 1.0).then_inc(set_, 1)
                dve.wait_ge(set_, 1)

        def emit(dve, at, ps, step, scratch):
            if dve is None:
                return 1
            step.add(dve.tensor_scalar(deg[:, at], ps[:, 0:1], 1.0, None, ALU.add))
            dve.wait_ge(step.sem, step.n)
        gcn_pass(nc, "degp", table, ones, 1, emit, None, other)
        with nc.Block() as block:
            @block.scalar
            def _(act):
                act.activation(root[:], deg[:], ACT.Sqrt).then_inc(rooted, 1)

            @block.vector
            def _(dve):
                dve.wait_ge(rooted, 1)
                dve.reciprocal(dinv[:], root[:]).then_inc(done, 1)
                dve.wait_ge(done, 1)


def gcn_conv(nc, tag, table, feats, width, dinv, out, bias=None):
    with ExitStack() as ctx:
        s = Scope(nc, ctx, tag)
        scaled = s.sb("scaled", [P, NB, width], F32)
        parts = s.sb("parts", [P, NB, 3 * width], BF16)
        rest = s.sb("rest", [P, NB, width], F32)
        bias_all = s.sb("bias_all", [P, width], F32)
        step_s, hi_s, mid_s, bias_in = s.sem("step"), s.sem("hi"), s.sem("mid"), s.sem("bias_in")
        with nc.Block() as block:
            @block.sync
            def _(sync):
                if bias is not None:
                    sync.dma_start(bias_all[:], bias.rearrange("(a n) -> a n", a=1).to_broadcast([P, width])).then_inc(bias_in, 16)
                    sync.wait_ge(bias_in, 16)

            @block.vector
            def _(dve):
                for g in range(5):
                    b = slice(5 * g, 5 * g + 5)
                    dve.tensor_tensor(scaled[:, b, :], feats[:, b, :], dinv[:, b].rearrange("p (b o) -> p b o", o=1).to_broadcast([P, 5, width]),
                                      ALU.mult).then_inc(step_s, 1)
                for g in range(5):
                    b = slice(5 * g, 5 * g + 5)
                    dve.wait_ge(hi_s, g + 1)
                    dve.tensor_tensor(rest[:, b, :], scaled[:, b, :], parts[:, b, 0:width], ALU.subtract).then_inc(step_s, 1)
                for g in range(5):
                    b = slice(5 * g, 5 * g + 5)
                    dve.wait_ge(mid_s, g + 1)
                    dve.tensor_tensor(parts[:, b, 2 * width:], rest[:, b, :], parts[:, b, width:2 * width], ALU.subtract).then_inc(step_s, 1)
                dve.wait_ge(step_s, 15)

            @block.scalar
            def _(act):
                for g in range(5):
                    b = slice(5 * g, 5 * g + 5)
                    act.wait_ge(step_s, g + 1)
                    act.copy(parts[:, b, 0:width], scaled[:, b, :]).then_inc(hi_s, 1)
                for g in range(5):
                    b = slice(5 * g, 5 * g + 5)
                    act.wait_ge(step_s, 5 + g + 1)
                    act.copy(parts[:, b, width:2 * width], rest[:, b, :]).then_inc(mid_s, 1)

        def extra(sc):
            return sc.sb("t1", [P, width], F32), sc.sb("t2", [P, width], F32), sc.sb("t3", [P, width], F32)

        def emit(dve, at, ps, step, scratch):
            if dve is None:
                return 4 if bias is not None else 3
            t1, t2, t3 = scratch
            step.add(dve.tensor_reduce(t1[:], ps[:, 0:3 * width].rearrange("p (j f) -> p f j", j=3), AX.X, ALU.add))
            dve.wait_ge(step.sem, step.n)
            step.add(dve.tensor_tensor(t2[:], t1[:], flat(scaled[:, at, :]), ALU.add))
            dve.wait_ge(step.sem, step.n)
            if bias is None:
                step.add(dve.tensor_scalar(flat(out[:, at, :]), t2[:], dinv[:, at], None, ALU.mult))
            else:
                step.add(dve.scalar_tensor_tensor(t3[:], t2[:], dinv[:, at], bias_all[:], ALU.mult, ALU.add))
                dve.wait_ge(step.sem, step.n)
                step.add(dve.tensor_scalar(flat(out[:, at, :]), t3[:], 0.0, None, ALU.max))
            dve.wait_ge(step.sem, step.n)
        gcn_pass(nc, tag + "p", table, parts, 3 * width, emit, extra)


def add_to(nc, tag, x, y, bias):
    with ExitStack() as ctx:
        s = Scope(nc, ctx, tag)
        bias_all = s.sb("bias_all", [P, 256], F32)
        bias_in, added = s.sem("bias_in"), s.sem("added")
        with nc.Block() as block:
            @block.sync
            def _(sync):
                if bias is not None:
                    sync.dma_start(bias_all[:], bias.rearrange("(a n) -> a n", a=1).to_broadcast([P, 256])).then_inc(bias_in, 16)

            @block.vector
            def _(dve):
                done = Count(added)
                if y is not None:
                    done.add(dve.tensor_tensor(x[:], x[:], y[:], ALU.add))
                    dve.wait_ge(done.sem, done.n)
                if bias is not None:
                    dve.wait_ge(bias_in, 16)
                    done.add(dve.tensor_tensor(x[:], x[:], bias_all[:].rearrange("p (o f) -> p o f", o=1).to_broadcast([P, NB, 256]), ALU.add))
                dve.wait_ge(done.sem, done.n)


DW = D + 1
HW = 3 * DW
GC = 512
GB = GC // P
CHUNKS = NP // GC
MASKS = 4
SG = 5
REACH = 80.0
TINY = 1e-37
STEEP = 2.0 ** 60


def spread(ap, n, width):
    return ap.rearrange("p (n o) -> p n o", o=1).to_broadcast([P, n, width])


def attention_terms(nc, tag, ident, t, er_rows, loops):
    with ExitStack() as ctx:
        s = Scope(nc, ctx, tag)
        ext = s.sb("ext", [P, 12], F32)
        ext_all = s.sb("ext_all", [P, 8], F32)
        mid = s.sb("mid", [P, H], F32)
        cen = s.sb("cen", [P, NB, H], F32)
        z = s.sb("z", [P, NB, H], F32)
        z2 = s.sb("z2", [P, NB, H], F32)
        top = s.sb("top", [P, NB, H], F32)
        e = s.sb("e", [P, NB, H], F32)
        e2 = s.sb("e2", [P, NB, H], F32)
        er_t = s.sb("er_t", [P, P], F32)
        ps = s.ps("ps", [P, 512])
        step_s, ext_ready, ext_done, er_turned, er_copied, er_out, exps = (s.sem(n) for n in (
            "step", "ext_ready", "ext_done", "er_turned", "er_copied", "er_out", "exps"))
        er, el = t["er_el"][:, 0], t["er_el"][:, 1]
        elb, u, u2, v, v2, ws = (t[k] for k in ("elb", "u", "u2", "v", "v2", "ws"))
        block = ctx.enter_context(nc.Block())

        @block.sync
        def _(sync):
            sync.wait_ge(er_copied, 1)
            sync.dma_start(er_rows, er_t[0:NB * H, :]).then_inc(er_out, 16)
            sync.wait_ge(er_out, 16)

        @block.gpsimd
        def _(pool):
            pool.wait_ge(ext_ready, 1)
            pool.partition_all_reduce(ext_all[:], ext[:, 0:8], P, RMAX).then_inc(ext_done, 1)

        @block.tensor
        def _(pe):
            pe.transpose(ps[0:NB * H, 0:P], er.rearrange("p b h -> p (b h)"), ident[:]).then_inc(er_turned, 1)

        CEN, ZV, Z2V, SELF = 7, 11, 12, 16

        @block.scalar
        def _(act):
            act.wait_ge(step_s, CEN)
            act.activation(u[:], cen[:], ACT.Exp).then_inc(exps, 1)
            act.activation(u2[:], cen[:], ACT.Exp, scale=0.2).then_inc(exps, 1)
            act.wait_ge(step_s, Z2V)
            act.activation(v[:], z[:].rearrange("p b h -> p h b"), ACT.Exp).then_inc(exps, 1)
            act.activation(v2[:], z2[:].rearrange("p b h -> p h b"), ACT.Exp).then_inc(exps, 1)
            if loops:
                act.wait_ge(step_s, SELF)
                act.activation(ws[:], e[:].rearrange("p b h -> p h b"), ACT.Exp).then_inc(exps, 1)
            act.wait_ge(exps, 5 if loops else 4)

        @block.vector
        def _(dve):
            step = Count(step_s)

            def do(ins):
                step.add(ins)

            def link(ins):
                step.add(ins)
                dve.wait_ge(step.sem, step.n)
            by_head = el.rearrange("p b h -> p h b")
            do(dve.tensor_reduce(ext[:, 0:4], by_head, AX.X, ALU.max))
            link(dve.tensor_reduce(ext[:, 8:12], by_head, AX.X, ALU.min))
            dve.tensor_scalar(ext[:, 4:8], ext[:, 8:12], -1.0, None, ALU.mult).then_inc(ext_ready, 1)
            do(dve.tensor_scalar(elb[:], el, STEEP, None, ALU.mult))
            dve.wait_ge(er_turned, 1)
            dve.tensor_copy(er_t[0:NB * H, :], ps[0:NB * H, 0:P]).then_inc(er_copied, 1)
            dve.wait_ge(ext_done, 1)
            link(dve.tensor_tensor(mid[:], ext_all[:, 0:4], ext_all[:, 4:8], ALU.subtract))
            link(dve.tensor_scalar(mid[:], mid[:], 0.5, None, ALU.mult))
            link(dve.scalar_tensor_tensor(mid[:], ext_all[:, 0:4], -REACH, mid[:], ALU.add, ALU.max))
            mid_all = mid[:].rearrange("p (o h) -> p o h", o=1).to_broadcast([P, NB, H])
            do(dve.tensor_tensor(cen[:], el, mid_all, ALU.subtract))
            assert step.n == CEN
            link(dve.tensor_tensor(z[:], er, mid_all, ALU.add))
            link(dve.tensor_scalar(z2[:], z[:], 0.2, None, ALU.mult))
            link(dve.tensor_tensor(top[:], z[:], z2[:], ALU.max))
            do(dve.tensor_tensor(z[:], z[:], top[:], ALU.subtract))
            assert step.n == ZV
            do(dve.tensor_tensor(z2[:], z2[:], top[:], ALU.subtract))
            assert step.n == Z2V
            if loops:
                link(dve.tensor_tensor(e[:], el, er, ALU.add))
                link(dve.tensor_scalar(e2[:], e[:], 0.2, None, ALU.mult))
                link(dve.tensor_tensor(e[:], e[:], e2[:], ALU.max))
                do(dve.tensor_tensor(e[:], e[:], top[:], ALU.subtract))
                assert step.n == SELF
            dve.wait_ge(step.sem, step.n)


def weighted_features(nc, tag, feat, t, parts):
    with ExitStack() as ctx:
        s = Scope(nc, ctx, tag)
        whole = s.sb("whole", [P, 2, 5, H, DW], F32)
        rest = s.sb("rest", [P, 2, 5, H, DW], F32)
        scaled, column_set, hi_done, rest_done, mid_done, lo_done = (s.sem(n) for n in ("scaled", "column_set", "hi_done", "rest_done", "mid_done", "lo_done"))
        block = ctx.enter_context(nc.Block())
        items = [(g, side) for g in range(5) for side in range(2)]

        def part(n, j):
            g, side = items[n]
            return parts[:, 5 * g:5 * g + 5, side, :, j * DW:(j + 1) * DW]

        @block.gpsimd
        def _(pool):
            for n, (g, side) in enumerate(items):
                b = slice(5 * g, 5 * g + 5)
                w = t["u"] if side == 0 else t["u2"]
                if n >= 2:
                    pool.wait_ge(hi_done, n - 1)
                    pool.wait_ge(rest_done, n - 1)
                pool.tensor_tensor(whole[:, n % 2, :, :, 0:D].rearrange("p b h d -> p (b h) d"), feat[:, b, :].rearrange("p b (h d) -> p (b h) d", h=H),
                                   spread(w[:, b, :].rearrange("p b h -> p (b h)"), 5 * H, D), ALU.mult).then_inc(scaled, 1)

        @block.vector
        def _(dve):
            def column(n):
                g, side = items[n]
                w = t["u"] if side == 0 else t["u2"]
                if n >= 2:
                    dve.wait_ge(hi_done, n - 1)
                    dve.wait_ge(rest_done, n - 1)
                dve.tensor_copy(whole[:, n % 2, :, :, D], w[:, 5 * g:5 * g + 5, :]).then_inc(column_set, 1)

            def rest_of(n):
                dve.wait_ge(hi_done, n + 1)
                if n >= 2:
                    dve.wait_ge(mid_done, n - 1)
                    dve.wait_ge(lo_done, n - 1)
                dve.tensor_tensor(rest[:, n % 2], whole[:, n % 2], part(n, 0), ALU.subtract).then_inc(rest_done, 1)

            def low(n):
                dve.wait_ge(mid_done, n + 1)
                dve.tensor_tensor(part(n, 2), rest[:, n % 2], part(n, 1), ALU.subtract).then_inc(lo_done, 1)
            for n in range(12):
                if n < 10:
                    column(n)
                if 1 <= n <= 10:
                    rest_of(n - 1)
                if n >= 2:
                    low(n - 2)
            dve.wait_ge(lo_done, 10)

        @block.scalar
        def _(act):
            for n in range(11):
                if n < 10:
                    act.wait_ge(scaled, n + 1)
                    act.wait_ge(column_set, n + 1)
                    act.copy(part(n, 0), whole[:, n % 2]).then_inc(hi_done, 1)
                if n >= 1:
                    act.wait_ge(rest_done, n)
                    act.copy(part(n - 1, 1), rest[:, (n - 1) % 2]).then_inc(mid_done, 1)


def attend(nc, tag, table, t, parts, er_rows, h, residual, loops=None):
    units = [(b, min(2, NB - b)) for b in range(0, NB, 2)]
    NU = len(units)
    with ExitStack() as ctx:
        s = Scope(nc, ctx, tag)
        cols = s.sb("cols", [P, NB, GC], F16)
        er = s.sb("er", [P, H, GC], F32)
        side = s.sb("side", [P, MASKS, 2, GC], F16)
        pos = s.sb("pos", [P, MASKS, 2, GC], F16)
        neg = s.sb("neg", [P, MASKS, 2, GC], F16)
        taken = s.sb("taken", [P, 2, GB, 2 * HW], F32)
        sides = s.sb("sides", [P, GB, 2, DW], F32)
        total = s.sb("total", [P, GB, DW], F32)
        den = s.sb("den", [P, GB], F32)
        bound = s.sb("bound", [P, GB], F32)
        rden = s.sb("rden", [P, GB], F32)
        own = s.sb("own", [P, GB, D], F32)
        quot = s.sb("quot", [P, GB, D], F32)
        none = s.sb("none", [P, GB, D], F32)
        ps = s.ps("ps", [P, 2 * GB, 512])
        col_in = [s.sem(f"col_in{g}") for g in range(NB // SG)]
        er_in = [s.sem(f"er_in{k}") for k in range(H)]
        (side_ready, pos_ready, masks_ready, masks_free, act_taken, dve_taken, consumed, den_ready, rden_ready, set_up, bounded, finished, emptied,
         step_s, pe_pass, act_pass, pool_pass) = (s.sem(n) for n in (
             "side_ready", "pos_ready", "masks_ready", "masks_free", "act_taken", "dve_taken", "consumed", "den_ready",
             "rden_ready", "set_up", "bounded", "finished", "emptied", "step", "pe_pass", "act_pass", "pool_pass"))
        block = ctx.enter_context(nc.Block())
        tab = table.rearrange("(b p) d -> p b d", p=P)
        er_v = er_rows.rearrange("(b h) p -> h b p", h=H)

        @block.sync
        def _(sync):
            def load_cols(g, at, width):
                sync.dma_start(cols[:, SG * g:SG * g + SG, 0:width], tab[:, SG * g:SG * g + SG, at]).then_inc(col_in[g], 16)

            def load_er(k, at, nblk):
                sync.dma_start(er[:, k, 0:nblk * P].rearrange("p (b q) -> p b q", b=nblk),
                               er_v[k:k + 1, at, :].to_broadcast([P, nblk, P])).then_inc(er_in[k], 16)

            def cols_used(i, g):
                q = (SG * (g + 1) - 1) // 2
                sync.wait_ge(masks_ready, (i * H + H - 1) * NU + q + 1)
            for g in range(NB // SG):
                if g < H:
                    load_er(g, slice(0, GB), GB)
                load_cols(g, slice(0, GC), GC)
            with sync.Fori(0, CHUNKS - 1) as i:
                for k in range(H - 1):
                    sync.wait_ge(side_ready, (i * H + k + 1) * NU)
                    load_er(k, bass.ds((i + 1) * GB, GB), GB)
                for g in range(NB // SG):
                    cols_used(i, g)
                    load_cols(g, bass.ds((i + 1) * GC, GC), GC)
                sync.wait_ge(side_ready, (i * H + H) * NU)
                load_er(H - 1, bass.ds((i + 1) * GB, GB), GB)
            for k in range(H):
                sync.wait_ge(side_ready, ((CHUNKS - 1) * H + k + 1) * NU)
                load_er(k, slice(CHUNKS * GB, NB), 1)
            for g in range(NB // SG):
                cols_used(CHUNKS - 1, g)
                load_cols(g, slice(CHUNKS * GC, NP), P)

        @block.tensor
        def _(pe):
            pe.sem_inc(masks_free, MASKS)

            def item(n, k, nblk):
                pe.wait_ge(act_taken, 1 + n)
                pe.sem_inc(pe_pass, 1)
                pe.wait_ge(dve_taken, 1 + n)
                pe.sem_inc(pe_pass, 1)
                for q, (b0, nb) in enumerate(units):
                    slot = (k * NU + q) % MASKS
                    pe.wait_ge(masks_ready, n * NU + q + 1)
                    pe.sem_inc(pe_pass, 1)
                    for b in range(b0, b0 + nb):
                        for j in range(nblk):
                            bank = ps[:, (k % 2) * GB + j, :]
                            pe.matmul(bank[:, 0:HW], pos[:, slot, b - b0, j * P:(j + 1) * P], parts[:, b, 0, k, :],
                                      start=(b == 0), stop=False, skip_group_check=True)
                            last = pe.matmul(bank[:, HW:2 * HW], neg[:, slot, b - b0, j * P:(j + 1) * P], parts[:, b, 1, k, :],
                                             start=False, stop=(b == NB - 1), skip_group_check=True)
                    last.then_inc(masks_free, 1)
            with pe.Fori(0, CHUNKS) as i:
                for k in range(H):
                    item(i * H + k, k, GB)
            for k in range(H):
                item(CHUNKS * H + k, k, 1)

        def previous(k, nblk):
            return (k + 1) % 2, GB if k == 0 else nblk

        @block.scalar
        def _(act):
            def take(n, half, nblk):
                act.wait_ge(masks_free, MASKS + n * NU)
                act.sem_inc(act_pass, 1)
                act.wait_ge(consumed, 1 + n)
                act.sem_inc(act_pass, 1)
                na = (nblk + 1) // 2
                act.copy(taken[:, half, 0:na, :], ps[:, half * GB:half * GB + na, 0:2 * HW]).then_inc(act_taken, 1)

            def item(n, k, nblk, turn):
                act.wait_ge(er_in[k], turn * 16 + 16)
                act.sem_inc(act_pass, 1)
                for q, (b0, nb) in enumerate(units):
                    slot = (k * NU + q) % MASKS
                    act.wait_ge(pos_ready, n * NU + q + 1)
                    act.sem_inc(act_pass, 1)
                    for b in range(b0, b0 + nb):
                        last = act.activation(side[:, slot, b - b0, 0:nblk * P], er[:, k, 0:nblk * P], ACT.Sigmoid,
                                              bias=t["elb"][:, b, k:k + 1], scale=STEEP)
                    last.then_inc(side_ready, 1)
                    if q == 3:
                        take(n, *previous(k, nblk))
            act.sem_inc(act_taken, 1)
            act.wait_ge(set_up, 1)
            with act.Fori(0, CHUNKS) as i:
                for k in range(H):
                    item(i * H + k, k, GB, i)
            for k in range(H):
                item(CHUNKS * H + k, k, 1, CHUNKS)
            take((CHUNKS + 1) * H, *previous(H, 1))

        @block.vector
        def _(dve):
            dve.memset(ps[:, GB:2 * GB, 0:2 * HW], 0.0).then_inc(emptied, 1)
            dve.memset(den[:], 1.0).then_inc(emptied, 1)
            dve.wait_ge(emptied, 2)
            dve.sem_inc(set_up, 1)
            dve.sem_inc(dve_taken, 1)
            dve.sem_inc(pos_ready, MASKS)

            def take(n, half, nblk):
                dve.wait_ge(masks_free, MASKS + n * NU)
                dve.wait_ge(consumed, 1 + n)
                na = (nblk + 1) // 2
                if na < nblk:
                    dve.tensor_copy(taken[:, half, na:nblk, :], ps[:, half * GB + na:half * GB + nblk, 0:2 * HW]).then_inc(dve_taken, 1)
                else:
                    dve.sem_inc(dve_taken, 1)

            def invert(n):
                dve.wait_ge(den_ready, 1 + n)
                dve.tensor_scalar(bound[:], den[:], TINY, None, ALU.max).then_inc(bounded, 1)
                dve.wait_ge(bounded, n + 1)
                dve.reciprocal(rden[:], bound[:]).then_inc(rden_ready, 1)

            def item(n, k, nblk, turn):
                width = nblk * P
                for q in range(NU + 1):
                    if q < NU:
                        b0, nb = units[q]
                        slot = (k * NU + q) % MASKS
                        if k == 0:
                            for g in range(NB // SG):
                                if b0 <= SG * g < b0 + nb:
                                    dve.wait_ge(col_in[g], turn * 16 + 16)
                        dve.wait_ge(side_ready, n * NU + q + 1)
                        dve.wait_ge(masks_free, n * NU + q + 1)
                        dve.tensor_tensor(pos[:, slot, 0:nb, 0:width], cols[:, b0:b0 + nb, 0:width], side[:, slot, 0:nb, 0:width],
                                          ALU.mult).then_inc(pos_ready, 1)
                    if q >= 1:
                        b0, nb = units[q - 1]
                        slot = (k * NU + q - 1) % MASKS
                        dve.wait_ge(pos_ready, MASKS + n * NU + q)
                        dve.tensor_tensor(neg[:, slot, 0:nb, 0:width], cols[:, b0:b0 + nb, 0:width], pos[:, slot, 0:nb, 0:width],
                                          ALU.subtract).then_inc(masks_ready, 1)
                    if q == 3:
                        take(n, *previous(k, nblk))
                    if q == NU - 2:
                        invert(n)
            with dve.Fori(0, CHUNKS) as i:
                for k in range(H):
                    item(i * H + k, k, GB, i)
            for k in range(H):
                item(CHUNKS * H + k, k, 1, CHUNKS)
            take((CHUNKS + 1) * H, *previous(H, 1))
            invert((CHUNKS + 1) * H)
            if not loops:
                dve.wait_ge(finished, 1)
                dve.tensor_scalar(h[:], h[:], 0.0, None, ALU.max).then_inc(finished, 1)
                dve.wait_ge(finished, 2)

        @block.gpsimd
        def _(pool):
            pool.memset(none[:], 0.0).then_inc(step_s, 1)
            pool.sem_inc(consumed, 3)
            pool.sem_inc(den_ready, 1)
            step = Count(step_s, 1)
            pool.wait_ge(step_s, 1)
            pool.sem_inc(pool_pass, 1)

            def link(ins):
                step.add(ins)
                pool.wait_ge(step.sem, step.n)
                pool.sem_inc(pool_pass, 1)

            def finish(n, k, rows, nblk):
                at = slice(k * D, (k + 1) * D)
                got = taken[:, k % 2, 0:nblk, :].rearrange("p j (s c f) -> p j s c f", s=2, c=3)
                both, tot, q = sides[:, 0:nblk], total[:, 0:nblk, :], quot[:, 0:nblk, :]
                pool.wait_ge(act_taken, 1 + n + 2)
                pool.sem_inc(pool_pass, 1)
                pool.wait_ge(dve_taken, 1 + n + 2)
                pool.sem_inc(pool_pass, 1)
                link(pool.tensor_tensor(both, got[:, :, :, 0, :], got[:, :, :, 1, :], ALU.add))
                link(pool.tensor_tensor(both, both, got[:, :, :, 2, :], ALU.add))
                pool.sem_inc(consumed, 1)
                link(pool.tensor_tensor(tot, both[:, :, 0, :], spread(t["v"][:, k, rows], nblk, DW), ALU.mult))
                link(pool.tensor_tensor(both[:, :, 1, :], both[:, :, 1, :], spread(t["v2"][:, k, rows], nblk, DW), ALU.mult))
                link(pool.tensor_tensor(tot, tot, both[:, :, 1, :], ALU.add))
                if loops:
                    w = t["ws"][:, k, rows]
                    link(pool.tensor_tensor(own[:, 0:nblk, :], h[:, rows, at], spread(w, nblk, D), ALU.mult))
                    link(pool.tensor_tensor(tot[:, :, 0:D], tot[:, :, 0:D], own[:, 0:nblk, :], ALU.add))
                    link(pool.tensor_tensor(tot[:, :, D], tot[:, :, D], w, ALU.add))
                link(pool.tensor_tensor(den[:, 0:nblk], tot[:, :, D], none[:, 0:nblk, 0], ALU.add))
                pool.sem_inc(den_ready, 1)
                pool.wait_ge(rden_ready, n + 2)
                pool.sem_inc(pool_pass, 1)
                link(pool.tensor_tensor(q, tot[:, :, 0:D], spread(rden[:, 0:nblk], nblk, D), ALU.mult))
                if loops:
                    link(pool.tensor_tensor(loops[:, rows, at], loops[:, rows, at], q, ALU.add))
                else:
                    link(pool.tensor_tensor(h[:, rows, at], q, h[:, rows, at] if residual else none[:, 0:nblk, :], ALU.add))
            per = 11 if loops else 8
            with pool.Fori(0, CHUNKS) as i:
                step.enter(i, H * per)
                for k in range(H):
                    finish(i * H + k, k, bass.ds(i * GB, GB), GB)
                step.leave(CHUNKS)
            for k in range(H):
                finish(CHUNKS * H + k, k, slice(NB - 1, NB), 1)
            pool.sem_inc(finished, 1)


def gat_layer(nc, tag, table, er_rows, h, ident, weights, att_src, att_dst, residual, x=None):
    with ExitStack() as ctx:
        s = Scope(nc, ctx, tag)
        t = {k: s.sb(k, [P, NB, H], F32) for k in ("elb", "u", "u2")}
        t["er_el"] = s.sb("er_el", [P, 2, NB, H], F32)
        t.update({k: s.sb(k, [P, H, NB], F32) for k in ("v", "v2", "ws")})
        parts = s.sb("parts", [P, NB, 2, H, HW], BF16)
        with ExitStack() as inner:
            feat = h if x is not None else inner.enter_context(nc.sbuf_tensor(tag + "_feat", [P, NB, 256], F32))
            project(nc, tag + "p", h, 2, weights, 256, feat, ident, attention=(att_dst, att_src, t["er_el"]))
            attention_terms(nc, tag + "t", ident, t, er_rows, x is not None)
            weighted_features(nc, tag + "w", feat, t, parts)
        attend(nc, tag + "a", table, t, parts, er_rows, h, residual, x)


F1 = 2 * D + 2 * H
EG = 8
LOWEST = -3.0e38


def source_rows(nc, rows, node_rows):
    with ExitStack() as ctx:
        s = Scope(nc, ctx, "l1s")
        written = s.sem("written")
        block = ctx.enter_context(nc.Block())

        @block.sync
        def _(sync):
            sync.dma_start(rows_of(node_rows), rows[:]).then_inc(written, 16)
            sync.wait_ge(written, 16)


def edge_messages(nc, src, attr, node_rows, msg, score):
    groups = T // EG
    with ExitStack() as ctx:
        s = Scope(nc, ctx, "l1g")
        src_i = s.sb("src_i", [P, T], U32)
        at = s.sb("at", [P, T, 2], F32)
        idx = s.sb("idx", [P, 2, EG], U32)
        row = s.sb("row", [P, 2, EG, F1], F32)
        tmp = s.sb("tmp", [P, 2, EG, D], F32)
        tms = s.sb("tms", [P, 2, EG, H], F32)
        loaded, idx_ready, row_done, step_s, pool_pass, act_pass = (s.sem(n) for n in ("loaded", "idx_ready", "row_done", "step", "pool_pass", "act_pass"))
        gathered = [s.pool_dma_sem("gathered0"), s.pool_dma_sem("gathered1")]
        block = ctx.enter_context(nc.Block())

        @block.sync
        def _(sync):
            sync.dma_start(src_i[:], src.bitcast(U32)).then_inc(loaded, 16)
            sync.dma_start(at[:], attr.rearrange("p (t c) -> p t c", c=2)).then_inc(loaded, 16)

        def group(pool, u, g_idx):
            for k in range(EG):
                pool.indirect_dma_start(out=row[:, u, k, :], out_offset=None, in_=node_rows,
                                        in_offset=bass.IndirectOffsetOnAxis(idx[:, u, k:k + 1], 0),
                                        bounds_check=NP - 1).then_inc(gathered[u], 16)

        @block.gpsimd
        def _(pool):
            with pool.Fori(0, groups // 2) as i:
                for u in range(2):
                    pool.wait_ge(idx_ready, i * 2 + u + 1)
                    pool.sem_inc(pool_pass, 1)
                    group(pool, u, None)
            pool.wait_ge(idx_ready, groups)
            group(pool, 0, None)

        @block.scalar
        def _(act):
            act.wait_ge(loaded, 32)
            act.wait_ge(step_s, 2)
            with act.Fori(0, groups // 2) as i:
                for u in range(2):
                    act.wait_ge(row_done, i * 2 + u + 1)
                    act.sem_inc(act_pass, 1)
                    act.copy(idx[:, u, :], src_i[:, bass.ds((i * 2 + u) * EG, EG)]).then_inc(idx_ready, 1)
            act.wait_ge(row_done, groups)
            act.copy(idx[:, 0, :], src_i[:, T - EG:T]).then_inc(idx_ready, 1)

        @block.vector
        def _(dve):
            step = Count(step_s)

            def link(ins):
                step.add(ins)
                dve.wait_ge(step.sem, step.n)
            link(dve.memset(tmp[:], 0.0))
            link(dve.memset(tms[:], 0.0))
            dve.sem_inc(row_done, 2)
            dve.wait_ge(loaded, 32)

            def group(u, tiles, n, turns):
                dve.wait_ge(gathered[u], turns * 16 * EG + 16 * EG)
                for lo, wd, to, tm in ((0, D, msg, tmp), (2 * D, H, score, tms)):
                    a0, a1 = (at[:, tiles, c:c + 1].to_broadcast([P, EG, wd]) for c in range(2))
                    step.add(dve.tensor_tensor(tm[:, u], row[:, u, :, lo + wd:lo + 2 * wd], a1, ALU.mult))
                    link(dve.tensor_tensor(to[:, tiles, :], row[:, u, :, lo:lo + wd], a0, ALU.mult))
                    link(dve.tensor_tensor(to[:, tiles, :], to[:, tiles, :], tm[:, u], ALU.add))
                dve.sem_inc(row_done, 1)
            with dve.Fori(0, groups // 2) as i:
                step.enter(i, 12)
                for u in range(2):
                    group(u, bass.ds((i * 2 + u) * EG, EG), i * 2 + u, i)
                step.leave(groups // 2)
            group(0, slice(T - EG, T), groups - 1, groups // 2)


def edge_weights(nc, score):
    with ExitStack() as ctx:
        s = Scope(nc, ctx, "l1w")
        low = s.sb("low", [P, T, H], F32)
        mx = s.sb("mx", [P, H], F32)
        mx_all = s.sb("mx_all", [P, H], F32)
        step_s, filled, max_ready, max_all, exp_done = (s.sem(n) for n in ("step", "filled", "max_ready", "max_all", "exp_done"))
        block = ctx.enter_context(nc.Block())

        @block.vector
        def _(dve):
            dve.tensor_scalar(low[:], score[:], 0.2, None, ALU.mult).then_inc(step_s, 1)
            dve.wait_ge(step_s, 1)
            dve.tensor_tensor(low[:], score[:], low[:], ALU.max).then_inc(step_s, 1)
            dve.wait_ge(filled, 1)
            dve.tensor_reduce(mx[:], score[:].rearrange("p t h -> p h t"), AX.X, ALU.max).then_inc(max_ready, 1)
            dve.wait_ge(max_all, 1)
            dve.tensor_tensor(low[:], score[:], mx_all[:].rearrange("p (o h) -> p o h", o=1).to_broadcast([P, T, H]), ALU.subtract).then_inc(step_s, 1)

        @block.gpsimd
        def _(pool):
            pool.wait_ge(step_s, 2)
            pool.affine_select(out=score[:], in_=low[:], compare_op=ALU.is_ge, fill=LOWEST, base=E - 1,
                               pattern=[[-1, T], [0, H]], channel_multiplier=-T).then_inc(filled, 1)
            pool.wait_ge(max_ready, 1)
            pool.partition_all_reduce(mx_all[:], mx[:], P, RMAX).then_inc(max_all, 1)

        @block.scalar
        def _(act):
            act.wait_ge(step_s, 3)
            act.activation(score[:], low[:], ACT.Exp).then_inc(exp_done, 1)
            act.wait_ge(exp_done, 1)


def edge_sums(nc, dst, dst_rows, msg, weight, ident, sums):
    turns = T // CHAINS
    with ExitStack() as ctx:
        s = Scope(nc, ctx, "l1e")
        dst_i = s.sb("dst_i", [P, T], I32)
        dst_f = s.sb("dst_f", [P, T], F32)
        dst_t = s.sb("dst_t", [98, 4, P], F32)
        spare = s.sb("spare", [P, T], F32)
        spare_i = s.sb("spare_i", [P, 1], I32)
        spare_f = s.sb("spare_f", [P, 1], F32)
        before = s.sb("before", [P, P], F32)
        rows = s.sb("rows", [P, 2, CHAINS * P], F32)
        same = s.sb("same", [P, CHAINS, P], F32)
        junk = s.sb("junk", [P, CHAINS, P], F32)
        early = s.sb("early", [P, 2, CHAINS], F32)
        pick = s.sb("pick", [P, 2, CHAINS], F32)
        cell = s.sb("cell", [P, 2, CHAINS], U32)
        value = s.sb("value", [P, CHAINS, MW], F32)
        merged = s.sb("merged", [P, 2, CHAINS, MW], F32)
        ps = s.ps("ps", [P, CHAINS, 512])
        ps_t = s.ps("ps_t", [P, 4, P])
        (loaded, masks_set, key_set, turned, copied, keys_out, step_s, cells_ready, slot_free, value_ready, summed,
         merged_ready, pool_pass, act_pass) = (s.sem(n) for n in (
             "loaded", "masks_set", "key_set", "turned", "copied", "keys_out", "step", "cells_ready", "slot_free",
             "value_ready", "summed", "merged_ready", "pool_pass", "act_pass"))
        row_in = [s.sem("row_in0"), s.sem("row_in1")]
        row_free = s.sem("row_free")
        added = [s.pool_dma_sem(f"added{c}") for c in range(CHAINS)]
        block = ctx.enter_context(nc.Block())

        @block.sync
        def _(sync):
            sync.dma_start(dst_i[:], dst).then_inc(loaded, 16)
            sync.wait_ge(copied, 1)
            sync.dma_start(dst_rows.rearrange("(c t) p -> t c p", c=4), dst_t[:]).then_inc(keys_out, 16)
            sync.wait_ge(keys_out, 16)
            with sync.Fori(0, turns // 2) as i:
                for u in range(2):
                    sync.wait_ge(row_free, i * 2 + u + 1)
                    sync.dma_start(rows[:, u, :], dst_rows[bass.ds((i * 2 + u) * CHAINS, CHAINS), :].rearrange("(a t) p -> a (t p)", a=1).to_broadcast([P, CHAINS * P])).then_inc(row_in[u], 16)

        @block.gpsimd
        def _(pool):
            pool.sem_inc(slot_free, CHAINS)
            pool.memset(before[:], 1.0).then_inc(masks_set, 1)
            pool.iota(spare_i[:], pattern=[[0, 1]], base=NP, channel_multiplier=1).then_inc(masks_set, 1)
            pool.wait_ge(masks_set, 2)
            pool.affine_select(out=before[:], in_=before[:], compare_op=ALU.is_gt, fill=0.0, base=0,
                               pattern=[[-1, P]], channel_multiplier=1).then_inc(masks_set, 1)

            def add(n, u):
                pool.wait_ge(cells_ready, n + 1)
                pool.sem_inc(pool_pass, 1)
                for c in range(CHAINS):
                    pool.wait_ge(merged_ready, CHAINS + n * CHAINS + c + 1)
                    pool.sem_inc(pool_pass, 1)
                    if type(n) is not int or n:
                        pool.wait_ge(added[c], n * 16)
                    pool.sem_inc(slot_free, 1)
                    pool.indirect_dma_start(out=sums[c], out_offset=bass.IndirectOffsetOnAxis(cell[:, u, c:c + 1], 0),
                                            in_=merged[:, u, c, :], in_offset=None, bounds_check=ROWS - 1,
                                            compute_op=ALU.add).then_inc(added[c], 16)
            add(0, 0)
            add(1, 1)
            with pool.Fori(1, turns // 2) as i:
                for u in range(2):
                    add(i * 2 + u, u)
            for c in range(CHAINS):
                pool.wait_ge(added[c], turns * 16)

        @block.tensor
        def _(pe):
            pe.sem_inc(summed, CHAINS)
            pe.wait_ge(key_set, 1)
            for c in range(4):
                last = pe.transpose(ps_t[0:98, c, :], dst_f[:, c * 98:(c + 1) * 98], ident[:])
            last.then_inc(turned, 1)
            with pe.Fori(0, turns) as i:
                for c in range(CHAINS):
                    pe.wait_ge(value_ready, (i * CHAINS + c + 1) * 3)
                    pe.sem_inc(pool_pass, 1)
                    pe.wait_ge(merged_ready, i * CHAINS + c + 1)
                    pe.sem_inc(pool_pass, 1)
                    pe.matmul(ps[:, c, 0:MW], same[:, c, :], value[:, c, :], start=True, stop=True).then_inc(summed, 1)

        @block.scalar
        def _(act):
            act.sem_inc(merged_ready, CHAINS)
            with act.Fori(0, turns // 2) as i:
                for u in range(2):
                    for c in range(CHAINS):
                        m = (i * 2 + u) * CHAINS + c
                        act.wait_ge(summed, CHAINS + m + 1)
                        act.sem_inc(act_pass, 1)
                        act.wait_ge(slot_free, m + 1)
                        act.sem_inc(act_pass, 1)
                        act.copy(merged[:, u, c, :], ps[:, c, 0:MW]).then_inc(merged_ready, 1)

        @block.vector
        def _(dve):
            step = Count(step_s)

            def link(ins):
                step.add(ins)
                dve.wait_ge(step.sem, step.n)
            dve.wait_ge(loaded, 16)
            dve.tensor_copy(dst_f[:], dst_i[:]).then_inc(key_set, 1)
            dve.wait_ge(masks_set, 3)
            link(dve.tensor_copy(spare_f[:], spare_i[:]))
            dve.wait_ge(turned, 1)
            dve.tensor_copy(dst_t[:], ps_t[0:98, :, :]).then_inc(copied, 1)
            dve.wait_ge(key_set, 1)
            link(dve.tensor_scalar(spare[:], dst_f[:], -1.0, spare_f[:, 0:1], ALU.mult, ALU.add))
            dve.sem_inc(row_free, 2)
            with dve.Fori(0, turns // 2) as i:
                step.enter(i, 2 * (CHAINS + 3))
                for u in range(2):
                    n = i * 2 + u
                    dve.wait_ge(row_in[u], i * 16 + 16)
                    for c in range(CHAINS):
                        one = bass.ds(n * CHAINS + c, 1)
                        row = rows[:, u, c * P:(c + 1) * P]
                        step.add(dve.scalar_tensor_tensor(junk[:, c, :], row, dst_f[:, one], before[:],
                                                          ALU.is_equal, ALU.mult, accum_out=early[:, u, c:c + 1]))
                        dve.wait_ge(summed, n * CHAINS + c + 1)
                        dve.tensor_scalar(same[:, c, :], row, dst_f[:, one], None, ALU.is_equal).then_inc(value_ready, 1)
                        w = flat(weight[:, one, :])
                        dve.tensor_tensor(value[:, c, 0:H * D].rearrange("p (h d) -> p h d", h=H), msg[:, one, :].to_broadcast([P, H, D]),
                                          spread(w, H, D), ALU.mult).then_inc(value_ready, 1)
                        dve.tensor_copy(value[:, c, H * D:MW], w).then_inc(value_ready, 1)
                    dve.wait_ge(step.sem, step.n)
                    ts = bass.ds(n * CHAINS, CHAINS)
                    link(dve.tensor_scalar(pick[:, u, :], early[:, u, :], 0.0, None, ALU.is_gt))
                    link(dve.tensor_tensor(pick[:, u, :], pick[:, u, :], spare[:, ts], ALU.mult))
                    dve.wait_ge(slot_free, (n + 1) * CHAINS)
                    link(dve.tensor_tensor(cell[:, u, :], pick[:, u, :], dst_f[:, ts], ALU.add))
                    dve.sem_inc(cells_ready, 1)
                    dve.wait_ge(value_ready, (n + 1) * CHAINS * 3)
                    dve.sem_inc(row_free, 1)
                step.leave(turns // 2)


def add_quotients(nc, sums, x):
    groups = 5
    nb = NB // groups
    with ExitStack() as ctx:
        s = Scope(nc, ctx, "l1q")
        part = s.sb("part", [P, 3, CHAINS, nb, MW], F32)
        rden = s.sb("rden", [P, nb, H], F32)
        part_in, step_s = [s.sem(f"part_in{g}") for g in range(groups)], s.sem("step")
        part_free = s.sem("part_free")
        block = ctx.enter_context(nc.Block())

        @block.sync
        def _(sync):
            for g in range(groups):
                if g >= 3:
                    sync.wait_ge(part_free, g - 2)
                for c in range(CHAINS):
                    sync.dma_start(part[:, g % 3, c], rows_of(sums[c][nb * g * P:nb * (g + 1) * P, :])).then_inc(part_in[g], 16)

        @block.vector
        def _(dve):
            step = Count(step_s)

            def do(ins):
                step.add(ins)

            def link(ins):
                step.add(ins)
                dve.wait_ge(step.sem, step.n)
            for g in range(groups):
                b = slice(nb * g, nb * (g + 1))
                p = part[:, g % 3]
                dve.wait_ge(part_in[g], CHAINS * 16)
                for c in range(1, CHAINS):
                    link(dve.tensor_tensor(p[:, 0], p[:, 0], p[:, c], ALU.add))
                link(dve.tensor_scalar(rden[:], p[:, 0, :, H * D:MW], 1e-10, None, ALU.add))
                link(dve.reciprocal(rden[:], rden[:]))
                for k in range(nb):
                    heads = p[:, 0, k, 0:H * D].rearrange("p (h d) -> p h d", h=H)
                    do(dve.tensor_tensor(heads, heads, spread(rden[:, k, :], H, D), ALU.mult))
                dve.wait_ge(step.sem, step.n)
                link(dve.tensor_tensor(x[:, b, :], x[:, b, :], p[:, 0, :, 0:H * D], ALU.add))
                dve.sem_inc(part_free, 1)


def attention_messages(nc, a, x, h, ident, sums):
    node_rows = nc.dram_tensor("node_rows", (NP, F1), F32).ap()
    dst_rows = nc.dram_tensor("dst_rows", (T, P), F32).ap()
    normalise(nc, "n1", x, h)
    with ExitStack() as ctx:
        rows = ctx.enter_context(nc.sbuf_tensor("l1_rows", [P, NB, F1], F32))
        project(nc, "pl", h, 2, None, 2 * D, rows, ident, (a["L1_gnn_W_forward"], a["L1_gnn_W_reverse"]),
                shared=a["L1_gnn_attn_forward"])
        source_rows(nc, rows, node_rows)
    with ExitStack() as ctx:
        msg = ctx.enter_context(nc.sbuf_tensor("msg", [P, T, D], F32))
        weight = ctx.enter_context(nc.sbuf_tensor("weight", [P, T, H], F32))
        edge_messages(nc, a["src"], a["edge_attr_2"], node_rows, msg, weight)
        edge_weights(nc, weight)
        edge_sums(nc, a["dst"], dst_rows, msg, weight, ident, sums)
    add_quotients(nc, sums, x)


def program(nc, a, out):
    cells = nc.dram_tensor("table", (TAB,), F16).ap()
    table = cells[0:NP * NP].rearrange("(s d) -> s d", d=NP)
    key_rows = nc.dram_tensor("key_rows", (T, P), F32).ap()
    er_rows = nc.dram_tensor("er_rows", (NB * H, P), F32).ap()
    sums = [nc.dram_tensor(f"sums{c}", (ROWS, MW), F32).ap() for c in range(CHAINS)]
    with ExitStack() as ctx:
        x = ctx.enter_context(nc.sbuf_tensor("x", [P, NB, 256], F32))
        h = ctx.enter_context(nc.sbuf_tensor("h", [P, NB, 256], F32))
        ident = ctx.enter_context(nc.sbuf_tensor("ident", [P, P], F32))
        with ExitStack() as c0:
            dinv = c0.enter_context(nc.sbuf_tensor("dinv", [P, NB], F32))
            f1 = c0.enter_context(nc.sbuf_tensor("f1", [P, NB, 128], F32))
            with ExitStack() as c1:
                zeros = c1.enter_context(nc.sbuf_tensor("zeros", [P, ZW + ZW % 2], F16))
                w1 = c1.enter_context(nc.sbuf_tensor("w1", [P, 2, 128], F32))
                table_zero = nc.alloc_semaphore("table_zero")
                load_nodes(nc, x, a["x"], w1, a["L0_gnn_W1"], ident)
                zero_table(nc, zeros, cells, table_zero)
                normalise(nc, "n0", x, h)
                project(nc, "p0", h, 2, None, 128, f1, ident, None, w1)
                adjacency(nc, a["src"], a["dst"], cells, table_zero, zeros, sums, key_rows, ident)
            degree(nc, table, None, dinv)
            gcn_conv(nc, "c0", table, f1, 128, dinv, f1, a["L0_gnn_b1"])
            gcn_conv(nc, "c1", table, f1, 128, dinv, f1)
            project(nc, "p1", f1, 1, a["L0_gnn_W2"], 256, h, ident)
            add_to(nc, "b0", x, h, a["L0_gnn_b2"])
        attention_messages(nc, a, x, h, ident, sums)
        normalise(nc, "n2", x, h)
        for n in range(3):
            gat_layer(nc, f"g{n}", table, er_rows, h, ident, a[f"L2_gnn_W{n}"], a[f"L2_gnn_al{n}"], a[f"L2_gnn_ar{n}"], n < 2)
        add_to(nc, "b2", x, h, None)
        normalise(nc, "n3", x, h)
        gat_layer(nc, "g3", table, er_rows, h, ident, a["L3_gnn_W"], a["L3_gnn_att_src"], a["L3_gnn_att_dst"], False, x)
        add_to(nc, "b3", x, None, a["L3_gnn_bias"])
        store(nc, x, out)


def store(nc, x, out):
    with ExitStack() as ctx:
        s = Scope(nc, ctx, "store")
        stored = s.sem("stored")
        with nc.Block() as block:
            @block.sync
            def _(sync):
                full = (NB - 1) * P
                sync.dma_start(rows_of(out[0:full, :]), x[:, 0:NB - 1, :]).then_inc(stored, 16)
                sync.dma_start(out[full:N, :], x[0:N - full, NB - 1, :]).then_inc(stored, 16)
                sync.wait_ge(stored, 32)


def kernel(**inputs):
    import numpy as np
    import concourse.bacc as bacc
    from concourse.bass_utils import run_bass_kernel_spmd as run
    nc = bacc.Bacc("TRN2", target_bir_lowering=False, num_devices=1)
    arrays = {k: np.ascontiguousarray(v) for k, v in inputs.items()}
    pad = np.full(P * T - E, NP - 1, arrays["src"].dtype)
    for k in ("src", "dst"):
        arrays[k] = np.concatenate([arrays[k], pad]).reshape(P, T)
    arrays["edge_attr_2"] = np.concatenate([arrays["edge_attr_2"], np.zeros((P * T - E, 2), arrays["edge_attr_2"].dtype)]).reshape(P, 2 * T)
    h = {k: nc.dram_tensor("in_" + k, v.shape, mybir.dt.from_np(v.dtype), kind="ExternalInput").ap() for k, v in arrays.items()}
    out = nc.dram_tensor("out", (N, 256), F32, kind="ExternalOutput").ap()
    program(nc, h, out)
    r = run(nc, [{"in_" + k: v for k, v in arrays.items()}], core_ids=[0])
    return r.results[0]["out"]
```

```python
from contextlib import ExitStack

import concourse.bass as bass
from concourse import mybir
from concourse.alu_op_type import AluOpType as ALU

ACT = mybir.ActivationFunctionType
AX = mybir.AxisListType
F32 = mybir.dt.float32
F16 = mybir.dt.float16
BF16 = mybir.dt.bfloat16
I32 = mybir.dt.int32
U32 = mybir.dt.uint32
RMAX = bass.bass_isa.ReduceOp.max

P = 128
N = 3125
E = 50000
NB = -(-N // P)
NP = NB * P
T = 392
GT = 14
G = T // GT
SLOTS = 4
RING = GT // 2
TC = T // 4
PAD_ROWS = -(-P * T // NP)
TAB = (NP + PAD_ROWS) * NP
ZD = 8
ZW = TAB // P // ZD
H = 4
D = 64
MW = H * D + H
CHAINS = 7
CELL_TURNS = G // SLOTS
ROW_UNIT = CELL_TURNS * P // 4
ROWS = -(-(NP + P) // ROW_UNIT) * ROW_UNIT
PIECE = ROWS * MW // CELL_TURNS // P
assert P * T >= E and G % SLOTS == 0 and GT * G == T and 4 * TC == T and TC <= P
assert ZW * P * ZD == TAB and TAB < 2 ** 24 and 2 * PIECE <= ZW and PIECE * P * CELL_TURNS == ROWS * MW
assert (T // CHAINS) % 2 == 0 and T % CHAINS == 0


class Count:

    def __init__(self, sem, n=0):
        self.sem, self.n = sem, n

    def add(self, ins, by=1):
        ins.then_inc(self.sem, by)
        self.n = self.n + by
        return self.n

    def enter(self, i, per):
        self.start, self.per = self.n, per
        self.n = self.n + i * per

    def leave(self, turns):
        self.n = self.start + turns * self.per


class Scope:

    def __init__(self, nc, ctx, tag):
        self.nc, self.ctx, self.tag, self.sems = nc, ctx, tag, []
        ctx.callback(self.release)

    def release(self):
        nums = sorted(x.num for x in self.sems)
        while nums:
            k = 1
            while k < len(nums) and nums[k] == nums[0] + k:
                k += 1
            self.nc.gpsimd.sem_clear(range(nums[0], nums[0] + k))
            nums = nums[k:]
        for x in self.sems:
            self.nc.release_semaphore(x)

    def sb(self, name, shape, dt):
        return self.ctx.enter_context(self.nc.sbuf_tensor(f"{self.tag}_{name}", shape, dt))

    def ps(self, name, shape, dt=F32):
        return self.ctx.enter_context(self.nc.psum_tensor(f"{self.tag}_{name}", shape, dt))

    def sem(self, name):
        self.sems.append(self.nc.alloc_semaphore(f"{self.tag}_{name}"))
        return self.sems[-1]

    def pool_dma_sem(self, name):
        return self.nc.alloc_semaphore(f"{self.tag}_{name}")


def flat(ap):
    return ap.rearrange("p a f -> p (a f)")


def spread(ap, n, width):
    return ap.rearrange("p (n o) -> p n o", o=1).to_broadcast([P, n, width])


def rows_of(ap):
    return ap.rearrange("(b p) f -> p b f", p=P)


def load_nodes(nc, x, x_in, w, w_in, ident):
    with ExitStack() as ctx:
        s = Scope(nc, ctx, "load")
        zeroed, x_loaded, ident_set = s.sem("zeroed"), s.sem("x_loaded"), s.sem("ident_set")
        block = ctx.enter_context(nc.Block())

        @block.vector
        def _(dve):
            dve.memset(x[:, NB - 1, :], 0.0).then_inc(zeroed, 1)

        @block.sync
        def _(sync):
            full = (NB - 1) * P
            sync.dma_start(x[:, 0:NB - 1, :], rows_of(x_in[0:full, :])).then_inc(x_loaded, 16)
            sync.wait_ge(zeroed, 1)
            sync.dma_start(x[0:N - full, NB - 1, :], x_in[full:N, :]).then_inc(x_loaded, 16)
            sync.dma_start(w[:], w_in.rearrange("(k p) n -> p k n", p=P)).then_inc(x_loaded, 16)
            sync.wait_ge(x_loaded, 48)

        @block.gpsimd
        def _(pool):
            pool.memset(ident[:], 0.0).then_inc(ident_set, 1)
            pool.wait_ge(ident_set, 1)
            pool.affine_select(out=ident[:], in_=ident[:], compare_op=ALU.not_equal, fill=1.0, base=0,
                               pattern=[[-1, P]], channel_multiplier=1).then_inc(ident_set, 1)
            pool.wait_ge(ident_set, 2)


NG = 5
BG = NB // NG


def normalise(nc, tag, x, h):
    with ExitStack() as ctx:
        s = Scope(nc, ctx, tag)
        stats = s.sb("stats", [P, NB, 6], F32)
        mv = s.sb("mv", [P, NB, 2], F32)
        sd = s.sb("sd", [P, NB], F32)
        rstd = s.sb("rstd", [P, NB], F32)
        shift = s.sb("shift", [P, NB], F32)
        eps = s.sb("eps", [P, 1], F32)
        eps_set, stats_ready, mv_ready = s.sem("eps_set"), s.sem("stats_ready"), s.sem("mv_ready")
        sd_ready, rstd_ready, shift_ready, h_done = (s.sem(n) for n in ("sd_ready", "rstd_ready", "shift_ready", "h_done"))
        block = ctx.enter_context(nc.Block())

        def group(g):
            return slice(g * BG, (g + 1) * BG)

        @block.vector
        def _(dve):
            dve.memset(eps[:], 1e-5).then_inc(eps_set, 1)
            for g in range(NG + 1):
                if g < NG:
                    for b in range(g * BG, (g + 1) * BG):
                        dve.bn_stats(stats[:, b, :], x[:, b, :]).then_inc(stats_ready, 1)
                    dve.wait_ge(stats_ready, (g + 1) * BG)
                    for b in range(g * BG, (g + 1) * BG):
                        dve.bn_aggr(mv[:, b, :], stats[:, b, :]).then_inc(mv_ready, 1)
                if g >= 1:
                    at = group(g - 1)
                    dve.wait_ge(sd_ready, g)
                    dve.reciprocal(rstd[:, at], sd[:, at]).then_inc(rstd_ready, 1)
                    dve.wait_ge(rstd_ready, g)
                    dve.scalar_tensor_tensor(shift[:, at], mv[:, at, 0], -1.0, rstd[:, at], ALU.mult, ALU.mult).then_inc(shift_ready, 1)

        @block.scalar
        def _(act):
            act.wait_ge(eps_set, 1)
            for g in range(NG + 1):
                if g < NG:
                    act.wait_ge(mv_ready, (g + 1) * BG)
                    act.activation(sd[:, group(g)], mv[:, group(g), 1], ACT.Sqrt, bias=eps[:, 0:1]).then_inc(sd_ready, 1)
                if g >= 1:
                    act.wait_ge(shift_ready, g)
                    for b in range((g - 1) * BG, g * BG):
                        act.activation(h[:, b, :], x[:, b, :], ACT.Relu, bias=shift[:, b:b + 1],
                                       scale=rstd[:, b:b + 1]).then_inc(h_done, 1)
            act.wait_ge(h_done, NB)


UN = 4


def project(nc, tag, h, kk, weights, width, out, ident, stacked=None, loaded=None, attention=None, shared=None,
            added=False, biased=None):
    full = width + (2 * H if attention or shared is not None else 0)
    with ExitStack() as ctx:
        s = Scope(nc, ctx, tag)
        w = loaded if loaded is not None else s.sb("w", [P, kk, full], F32)
        raw = s.sb("raw", [P, kk * P], F32) if stacked else None
        vectors = s.sb("vectors", [P, 2, H * D], F32) if full > width else None
        products = s.sb("products", [P, 2, kk, H * D], F32) if full > width else None
        turned = s.sb("turned", [P, UN, kk * P], F32)
        bias_all = s.sb("bias_all", [P, 1, 256], F32) if biased else None
        bias_in, bias_added = s.sem("bias_in"), s.sem("bias_added")
        ps_t = s.ps("ps_t", [P, UN, 512])
        ps_o = s.ps("ps_o", [P, UN, 512])
        w_in, w_ready, w_turned, w_multiplied = s.sem("w_in"), s.sem("w_ready"), s.sem("w_turned"), s.sem("w_multiplied")
        turn_ready, turn_copied, made, taken = (s.sem(n) for n in (
            "turn_ready", "turn_copied", "made", "taken"))
        block = ctx.enter_context(nc.Block())

        @block.sync
        def _(sync):
            if biased:
                sync.dma_start(bias_all[:, 0, :], biased[1].rearrange("(a n) -> a n", a=1).to_broadcast([P, 256])).then_inc(bias_in, 16)
            if stacked:
                sync.dma_start(raw[0:64, :], stacked[0]).then_inc(w_in, 16)
                sync.dma_start(raw[64:P, :], stacked[1]).then_inc(w_in, 16)
                sync.dma_start(vectors[:, 0, :], shared.rearrange("o h d -> o (h d)").to_broadcast([P, H * D])).then_inc(w_in, 16)
            elif loaded is None:
                sync.dma_start(w[:, :, 0:width], weights.rearrange("(k p) n -> p k n", p=P)).then_inc(w_in, 16)
            if attention:
                for k in range(2):
                    sync.dma_start(vectors[:, k, :], attention[k].rearrange("h (o d) -> o (h d)", o=1).to_broadcast([P, width])).then_inc(w_in, 16)

        @block.gpsimd
        def _(pool):
            if biased:
                pool.wait_ge(bias_in, 16)
                for g in range(NG):
                    rows = biased[0][:, g * BG:(g + 1) * BG, :]
                    pool.tensor_tensor(rows, rows, bias_all[:].to_broadcast([P, BG, 256]), ALU.add).then_inc(bias_added, 1)
                pool.wait_ge(bias_added, NG)

        @block.tensor
        def _(pe):
            if stacked:
                pe.wait_ge(w_in, 48)
                for k in range(kk):
                    last = pe.transpose(ps_o[:, 0, k * P:(k + 1) * P], raw[:, k * P:(k + 1) * P], ident[:])
                last.then_inc(w_turned, 1)
            for n in range(NB + 2):
                if n < NB:
                    if n >= UN:
                        pe.wait_ge(turn_copied, n - UN + 1)
                    for k in range(kk):
                        last = pe.transpose(ps_t[:, n % UN, k * P:(k + 1) * P], h[:, n, k * P:(k + 1) * P], ident[:])
                    last.then_inc(turn_ready, 1)
                if n == 1:
                    if stacked:
                        pe.wait_ge(w_ready, 3)
                    elif attention:
                        pe.wait_ge(w_ready, 2)
                    elif loaded is None:
                        pe.wait_ge(w_in, 16)
                if n >= 2:
                    b = n - 2
                    pe.wait_ge(turn_copied, b + 1)
                    if b >= UN:
                        pe.wait_ge(taken, (b - UN + 1) * (2 if attention else 1))
                    for k in range(kk):
                        last = pe.matmul(ps_o[:, b % UN, 0:full], turned[:, b % UN, k * P:(k + 1) * P], w[:, k, :],
                                         start=(k == 0), stop=(k == kk - 1))
                    last.then_inc(made, 1)

        @block.scalar
        def _(act):
            for n in range(NB):
                act.wait_ge(turn_ready, n + 1)
                if n >= UN:
                    act.wait_ge(made, n - UN + 1)
                act.copy(turned[:, n % UN, :], ps_t[:, n % UN, 0:kk * P]).then_inc(turn_copied, 1)

        @block.vector
        def _(dve):
            if stacked:
                dve.wait_ge(w_turned, 1)
                dve.tensor_copy(w[:, :, 0:width], ps_o[:, 0, 0:kk * P].rearrange("p (k n) -> p k n", k=kk)).then_inc(w_ready, 1)
                dve.wait_ge(w_ready, 1)
                by_head = [P, kk, H, D]
                for k in range(2):
                    dve.tensor_tensor(products[:, k].rearrange("p c (h d) -> p c h d", h=H),
                                      w[:, :, k * D:(k + 1) * D].rearrange("p c (o d) -> p c o d", o=1).to_broadcast(by_head),
                                      vectors[:, 0, :].rearrange("p (o h d) -> p o h d", o=1, h=H).to_broadcast(by_head),
                                      ALU.mult).then_inc(w_multiplied, 1)
            if attention:
                dve.wait_ge(w_in, 48)
                for k in range(2):
                    dve.tensor_tensor(products[:, k], w[:, :, 0:width], vectors[:, k:k + 1, :].to_broadcast([P, kk, width]),
                                      ALU.mult).then_inc(w_multiplied, 1)
            if full > width:
                for k in range(2):
                    dve.wait_ge(w_multiplied, k + 1)
                    dve.tensor_reduce(w[:, :, width + k * H:width + (k + 1) * H], products[:, k].rearrange("p c (h d) -> p c h d", h=H),
                                      AX.X, ALU.add).then_inc(w_ready, 1)
            for n in range(NB):
                dve.wait_ge(made, n + 1)
                own = width if attention else full
                if added:
                    dve.wait_ge(bias_added, n // BG + 1)
                    dve.tensor_tensor(out[:, n, 0:own], out[:, n, 0:own], ps_o[:, n % UN, 0:own], ALU.add).then_inc(taken, 1)
                else:
                    dve.tensor_copy(out[:, n, 0:own], ps_o[:, n % UN, 0:own]).then_inc(taken, 1)
                if attention:
                    dve.tensor_copy(attention[2][:, :, n, :], ps_o[:, n % UN, width:full].rearrange("p (k h) -> p k h", k=2)).then_inc(taken, 1)
            dve.wait_ge(taken, NB * (2 if attention else 1))


def zero_table(nc, zeros, table, table_zero):
    with ExitStack() as ctx:
        s = Scope(nc, ctx, "zero")
        zeros_set = s.sem("zeros_set")
        block = ctx.enter_context(nc.Block())

        @block.vector
        def _(dve):
            dve.memset(zeros[:].bitcast(U32), 0).then_inc(zeros_set, 1)

        @block.scalar
        def _(act):
            act.wait_ge(zeros_set, 1)
            for q in range(ZD):
                act.dma_start(table.rearrange("(q p w) -> q p w", q=ZD, p=P)[q], zeros[:, 0:ZW]).then_inc(table_zero, 16)


def adjacency(nc, src, dst, table, table_zero, zeros, sums, key_rows, ident, dinv):
    with ExitStack() as ctx:
        s = Scope(nc, ctx, "adj")
        src_i = s.sb("src_i", [P, T], I32)
        dst_i = s.sb("dst_i", [P, T], I32)
        key = s.sb("key", [P, T], F32)
        key_t = s.sb("key_t", [TC, 4, P], F32)
        slot_i = s.sb("slot_i", [P, T], I32)
        spare = s.sb("spare", [P, T], F32)
        after = s.sb("after", [P, P], BF16)
        pair = s.sb("pair", [P, 4], BF16)
        rows = s.sb("rows", [P, SLOTS, GT * P], F32)
        same = s.sb("same", [P, RING * (GT + 2), P], BF16)
        own = s.sb("own", [P, 2, RING, P], BF16)
        pick = s.sb("pick", [P, SLOTS, GT], F32)
        cell = s.sb("cell", [P, SLOTS, GT], U32)
        value = s.sb("value", [P, SLOTS, GT], F16)
        number_i = s.sb("number_i", [P, P], I32)
        number = s.sb("number", [P, P], F32)
        p_i = s.sb("p_i", [P, T], I32)
        minus_p = s.sb("minus_p", [P, T], F32)
        node_b = s.sb("node_b", [P, T], F32)
        one = s.sb("one", [P, 1], F32)
        nothing = s.sb("nothing", [P, P], BF16)
        away = s.sb("away", [P, 2, GT, P], BF16)
        hot_p = s.sb("hot_p", [P, 2, GT, P], BF16)
        hot_b = s.sb("hot_b", [P, 2, GT, NB], BF16)
        root = s.sb("root", [P, NB], F32)
        ps_t = s.ps("ps_t", [P, 4, P])
        ps_deg = s.ps("ps_deg", [P, 512])
        ps = s.ps("ps", [P, SLOTS, 512])
        (edges_in, keys_ready, keys_turned, keys_copied, keys_out, consts_set, pair_set, same_ready, same_used, own_ready,
         counted, picked, cells_ready, values_ready, cells_free, row_free, sums_zero, pool_pass, act_pass, sp_pass, pe_pass) = (
             s.sem(n) for n in (
                 "edges_in", "keys_ready", "keys_turned", "keys_copied", "keys_out", "consts_set", "pair_set", "same_ready",
                 "same_used", "own_ready", "counted", "picked", "cells_ready", "values_ready", "cells_free", "row_free", "sums_zero",
                 "pool_pass", "act_pass", "sp_pass", "pe_pass"))
        numbers_set, places_set, away_ready, hot_p_ready, hot_b_ready, hot_used, rooted, dinv_ready = (
            s.sem(n) for n in ("numbers_set", "places_set", "away_ready", "hot_p_ready", "hot_b_ready", "hot_used", "rooted", "dinv_ready"))
        row_in = [s.sem(f"row_in{u}") for u in range(SLOTS)]
        added = s.pool_dma_sem("added")
        block = ctx.enter_context(nc.Block())
        pieces = [t.rearrange("r f -> (r f)").rearrange("(i p w) -> i p w", i=CELL_TURNS, p=P) for t in sums]

        @block.sync
        def _(sync):
            sync.dma_start(src_i[:], src).then_inc(edges_in, 16)
            sync.dma_start(dst_i[:], dst).then_inc(edges_in, 16)
            sync.wait_ge(keys_copied, 1)
            sync.dma_start(key_rows.rearrange("(c t) p -> t c p", c=4), key_t[:]).then_inc(keys_out, 16)
            sync.wait_ge(keys_out, 16)
            with sync.Fori(0, CELL_TURNS) as i:
                for u in range(SLOTS):
                    sync.wait_ge(row_free, i * SLOTS + u + 1)
                    sync.sem_inc(sp_pass, 1)
                    sync.dma_start(rows[:, u, :], key_rows[bass.ds((i * SLOTS + u) * GT, GT), :]
                                   .rearrange("(a t) p -> a (t p)", a=1).to_broadcast([P, GT * P])).then_inc(row_in[u], 16)
                for piece in pieces:
                    sync.dma_start(piece[bass.ds(i, 1)].rearrange("i p w -> (i p) w"), zeros[:, 0:2 * PIECE].bitcast(F32)).then_inc(sums_zero, 16)
            sync.wait_ge(sums_zero, CHAINS * CELL_TURNS * 16)

        @block.gpsimd
        def _(pool):
            pool.sem_inc(cells_free, SLOTS)
            pool.memset(after[:], 1.0).then_inc(consts_set, 1)
            pool.iota(slot_i[:], pattern=[[1, T]], base=NP * NP, channel_multiplier=T).then_inc(consts_set, 1)
            pool.iota(number_i[:], pattern=[[1, P]], base=0, channel_multiplier=0).then_inc(consts_set, 1)
            pool.wait_ge(consts_set, 3)
            pool.affine_select(out=after[:], in_=after[:], compare_op=ALU.is_gt, fill=0.0, base=0,
                               pattern=[[1, P]], channel_multiplier=-1).then_inc(consts_set, 1)
            pool.wait_ge(table_zero, ZD * 16)
            with pool.Fori(0, CELL_TURNS) as i:
                for u in range(SLOTS):
                    n = i * SLOTS + u
                    pool.wait_ge(cells_ready, n + 1)
                    pool.sem_inc(pool_pass, 1)
                    pool.wait_ge(values_ready, SLOTS + n + 1)
                    pool.sem_inc(pool_pass, 1)
                    for k in range(GT):
                        pool.indirect_dma_start(out=table.rearrange("(w o) -> w o", o=1),
                                                out_offset=bass.IndirectOffsetOnAxis(cell[:, u, k:k + 1], 0),
                                                in_=value[:, u, k:k + 1], in_offset=None, bounds_check=TAB - 1,
                                                compute_op=ALU.add).then_inc(added, 16)
                    pool.wait_ge(added, (n + 1) * (16 * GT))
                    pool.sem_inc(cells_free, 1)

        @block.tensor
        def _(pe):
            pe.sem_inc(same_used, RING)
            pe.sem_inc(counted, 1)
            pe.wait_ge(keys_ready, 1)
            for c in range(4):
                last = pe.transpose(ps_t[0:TC, c, :], key[:, c * TC:(c + 1) * TC], ident[:])
            last.then_inc(keys_turned, 1)
            pe.sem_inc(hot_used, 2)
            pe.wait_ge(numbers_set, 3)
            pe.matmul(ps_deg[:, 0:NB], nothing[:], nothing[:, 0:NB], start=True, stop=False, skip_group_check=True)
            both, equal, earlier = pair[:, 0:2], pair[:, 1:3], pair[:, 2:4]
            with pe.Fori(0, CELL_TURNS) as i:
                for u in range(SLOTS):
                    n = i * SLOTS + u
                    pe.wait_ge(values_ready, n + 1)
                    pe.sem_inc(pe_pass, 1)
                    for half in range(2):
                        for r in range(RING):
                            j = half * RING + r
                            pe.wait_ge(same_ready, n * GT + j + 1)
                            pe.sem_inc(pe_pass, 1)
                            for k in range(GT):
                                last = pe.matmul(ps[:, u, 2 * k:2 * k + 2], same[:, r * GT + k, :], both if j < k else equal,
                                                 start=(j == 0 and k == 0), stop=False, skip_group_check=True)
                            if r < RING - 1:
                                last.then_inc(same_used, 1)
                        last.then_inc(same_used, 1)
                        pe.wait_ge(own_ready, 1 + n * 2 + half + 1)
                        pe.sem_inc(pe_pass, 1)
                        for r in range(RING):
                            k = half * RING + r
                            last = pe.matmul(ps[:, u, 2 * k:2 * k + 2], own[:, half, r, :], earlier, start=False,
                                             stop=(half == 1), skip_group_check=True)
                    last.then_inc(counted, 1)
                    pe.wait_ge(hot_p_ready, n + 1)
                    pe.sem_inc(pe_pass, 1)
                    pe.wait_ge(hot_b_ready, n + 1)
                    pe.sem_inc(pe_pass, 1)
                    for k in range(GT):
                        last = pe.matmul(ps_deg[:, 0:NB], hot_p[:, u % 2, k, :], hot_b[:, u % 2, k, :], start=False, stop=True,
                                         skip_group_check=True)
                    last.then_inc(hot_used, 1)

        @block.scalar
        def _(act):
            act.sem_inc(values_ready, SLOTS)
            act.wait_ge(numbers_set, 3)
            act.wait_ge(places_set, 3)
            with act.Fori(0, CELL_TURNS) as i:
                for u in range(SLOTS):
                    n = i * SLOTS + u
                    act.wait_ge(hot_used, n + 1)
                    act.sem_inc(act_pass, 1)
                    for k in range(GT):
                        last = act.activation(away[:, u % 2, k, :], number[:], ACT.Abs, bias=minus_p[:, bass.ds(n * GT + k, 1)])
                    last.then_inc(away_ready, 1)
                    act.wait_ge(away_ready, n + 1)
                    act.sem_inc(act_pass, 1)
                    act.activation(hot_p[:, u % 2], away[:, u % 2], ACT.Relu, bias=one[:, 0:1], scale=-1.0).then_inc(hot_p_ready, 1)
                    act.wait_ge(cells_ready, i * SLOTS + u + 1)
                    act.sem_inc(act_pass, 1)
                    act.copy(value[:, u, :], ps[:, u, 0:2 * GT:2]).then_inc(values_ready, 1)
            act.wait_ge(hot_used, 2 + G)
            act.activation(root[:], ps_deg[:, 0:NB], ACT.Sqrt, bias=one[:, 0:1]).then_inc(rooted, 1)

        @block.vector
        def _(dve):
            dve.memset(pair[:], 1.0).then_inc(pair_set, 1)
            dve.wait_ge(pair_set, 1)
            dve.memset(pair[:, 2:3], 0.0).then_inc(pair_set, 1)
            dve.wait_ge(edges_in, 32)
            dve.scalar_tensor_tensor(out=key[:], in0=src_i[:], scalar=float(NP), in1=dst_i[:], op0=ALU.mult,
                                     op1=ALU.add).then_inc(keys_ready, 1)
            dve.wait_ge(keys_ready, 1)
            dve.wait_ge(consts_set, 4)
            dve.tensor_tensor(spare[:], slot_i[:], key[:], ALU.subtract).then_inc(keys_ready, 1)
            dve.tensor_copy(number[:], number_i[:]).then_inc(numbers_set, 1)
            dve.memset(one[:], 1.0).then_inc(numbers_set, 1)
            dve.memset(nothing[:], 0.0).then_inc(numbers_set, 1)
            dve.tensor_scalar(p_i[:], dst_i[:], P - 1, None, ALU.bitwise_and).then_inc(places_set, 1)
            dve.wait_ge(places_set, 1)
            dve.tensor_scalar(minus_p[:], p_i[:], -1.0, None, ALU.mult).then_inc(places_set, 1)
            dve.wait_ge(places_set, 2)
            dve.tensor_tensor(node_b[:], dst_i[:], minus_p[:], ALU.add).then_inc(places_set, 1)
            dve.wait_ge(places_set, 3)
            dve.wait_ge(numbers_set, 3)
            dve.tensor_scalar(node_b[:], node_b[:], 1.0 / P, None, ALU.mult).then_inc(places_set, 1)
            dve.wait_ge(places_set, 4)
            dve.wait_ge(keys_turned, 1)
            dve.tensor_copy(key_t[:], ps_t[0:TC, :, :]).then_inc(keys_copied, 1)
            dve.wait_ge(keys_ready, 2)
            dve.wait_ge(pair_set, 2)
            dve.sem_inc(row_free, SLOTS)
            dve.sem_inc(own_ready, 1)

            def cells(n, u):
                ts = bass.ds(n * GT, GT)
                dve.wait_ge(counted, 1 + n + 1)
                dve.wait_ge(cells_free, n + 1)
                dve.scalar_tensor_tensor(pick[:, u, :], ps[:, u, 1:2 * GT:2], 0.0, spare[:, ts], ALU.is_gt, ALU.mult).then_inc(picked, 1)
                dve.wait_ge(picked, n + 1)
                dve.tensor_tensor(cell[:, u, :], pick[:, u, :], key[:, ts], ALU.add).then_inc(cells_ready, 1)
            with dve.Fori(0, CELL_TURNS) as i:
                for u in range(SLOTS):
                    n = i * SLOTS + u
                    dve.wait_ge(row_in[u], i * 16 + 16)
                    for half in range(2):
                        dve.wait_ge(own_ready, 1 + n * 2 + half)
                        for r in range(RING):
                            j = half * RING + r
                            dve.wait_ge(same_used, n * GT + j + 1)
                            dve.tensor_scalar(same[:, r * GT:(r + 1) * GT, :].rearrange("p k q -> p (k q)"), rows[:, u, :],
                                              key[:, bass.ds(n * GT + j, 1)], None, ALU.is_equal).then_inc(same_ready, 1)
                        dve.wait_ge(same_ready, n * GT + (half + 1) * RING)
                        if half == 0:
                            dve.wait_ge(counted, n + 1)
                        diagonal = same[:, half * RING:half * RING + RING * (GT + 1), :].rearrange(
                            "p (r k) q -> p r k q", r=RING)[:, :, 0, :]
                        dve.tensor_tensor(own[:, half], diagonal, after[:].rearrange("p (o q) -> p o q", o=1).to_broadcast([P, RING, P]),
                                          ALU.mult).then_inc(own_ready, 1)
                    dve.sem_inc(row_free, 1)
                    dve.wait_ge(hot_used, n + 1)
                    dve.tensor_tensor(hot_b[:, u % 2], number[:, 0:NB].rearrange("p (o b) -> p o b", o=1).to_broadcast([P, GT, NB]),
                                      spread(node_b[:, bass.ds(n * GT, GT)], GT, NB), ALU.is_equal).then_inc(hot_b_ready, 1)
                    cells(n, u)
            dve.wait_ge(rooted, 1)
            dve.reciprocal(dinv[:], root[:]).then_inc(dinv_ready, 1)
            dve.wait_ge(dinv_ready, 1)


CW = 256
CS = 4
CBLK = CW // P
TURN = CS * CBLK
TURNS = NB // TURN


def gcn_pass(nc, tag, table, rhs, width, emit, per, scratch):
    assert TURNS * TURN + 1 == NB
    with ExitStack() as ctx:
        s = Scope(nc, ctx, tag)
        cols = s.sb("cols", [P, CS, NB, CW], F16)
        ps = s.ps("ps", [P, TURN, 512])
        chunk_in = [s.sem(f"chunk_in{u}") for u in range(CS)]
        chunk_free, sp_pass = s.sem("chunk_free"), s.sem("sp_pass")
        summed, bank_free, pe_pass, dve_step = s.sem("summed"), s.sem("bank_free"), s.sem("pe_pass"), s.sem("dve_step")
        tensors = scratch(s)
        block = ctx.enter_context(nc.Block())
        tab = table.rearrange("(b p) d -> p b d", p=P)

        @block.sync
        def _(sync):
            with sync.Fori(0, TURNS) as i:
                for u in range(CS):
                    sync.wait_ge(chunk_free, i * CS + u + 1)
                    sync.sem_inc(sp_pass, 1)
                    sync.dma_start(cols[:, u], tab[:, :, bass.ds((i * CS + u) * CW, CW)]).then_inc(chunk_in[u], 16)
            sync.wait_ge(chunk_free, TURNS * CS + 1)
            sync.dma_start(cols[:, 0, :, 0:P], tab[:, :, TURNS * TURN * P:NB * P]).then_inc(chunk_in[0], 16)

        @block.tensor
        def _(pe):
            pe.sem_inc(chunk_free, CS)

            def one(u, j, bank):
                for b in range(NB):
                    last = pe.matmul(ps[:, bank, 0:width], cols[:, u, b, j * P:(j + 1) * P], rhs[:, b, :],
                                     start=(b == 0), stop=(b == NB - 1))
                last.then_inc(summed, 1)
            with pe.Fori(0, TURNS) as i:
                for u in range(CS):
                    pe.wait_ge(chunk_in[u], i * 16 + 16)
                    for j in range(CBLK):
                        bank = u * CBLK + j
                        pe.wait_ge(bank_free, i * TURN + bank + 1)
                        pe.sem_inc(pe_pass, 1)
                        one(u, j, bank)
                    pe.wait_ge(summed, i * TURN + bank + 1)
                    pe.sem_inc(chunk_free, 1)
            pe.wait_ge(chunk_in[0], TURNS * 16 + 16)
            pe.wait_ge(bank_free, TURNS * TURN + 1)
            one(0, 0, 0)

        @block.vector
        def _(dve):
            dve.sem_inc(bank_free, TURN)
            step = Count(dve_step)
            with dve.Fori(0, TURNS) as i:
                step.enter(i, TURN * per)
                for bank in range(TURN):
                    dve.wait_ge(summed, i * TURN + bank + 1)
                    emit(dve, bass.ds(i * TURN + bank, 1), ps[:, bank, :], step, tensors)
                    dve.sem_inc(bank_free, 1)
                step.leave(TURNS)
            dve.wait_ge(summed, NB)
            emit(dve, slice(NB - 1, NB), ps[:, 0, :], step, tensors)


def split_scaled(nc, feats, width, dinv, scaled, parts):
    with ExitStack() as ctx:
        s = Scope(nc, ctx, "split")
        rest = s.sb("rest", [P, NB, width], F32)
        step, hi_done, mid_done = s.sem("step"), s.sem("hi_done"), s.sem("mid_done")
        block = ctx.enter_context(nc.Block())
        groups = [slice(g * BG, (g + 1) * BG) for g in range(NG)]

        @block.vector
        def _(dve):
            for b in groups:
                dve.tensor_tensor(scaled[:, b, :], feats[:, b, :], spread(dinv[:, b], BG, width), ALU.mult).then_inc(step, 1)
            for g, b in enumerate(groups):
                dve.wait_ge(hi_done, g + 1)
                dve.tensor_tensor(rest[:, b, :], scaled[:, b, :], parts[:, b, 0:width], ALU.subtract).then_inc(step, 1)
            for g, b in enumerate(groups):
                dve.wait_ge(mid_done, g + 1)
                dve.tensor_tensor(parts[:, b, 2 * width:], rest[:, b, :], parts[:, b, width:2 * width], ALU.subtract).then_inc(step, 1)
            dve.wait_ge(step, 3 * NG)

        @block.scalar
        def _(act):
            for g, b in enumerate(groups):
                act.wait_ge(step, g + 1)
                act.copy(parts[:, b, 0:width], scaled[:, b, :]).then_inc(hi_done, 1)
            for g, b in enumerate(groups):
                act.wait_ge(step, NG + g + 1)
                act.copy(parts[:, b, width:2 * width], rest[:, b, :]).then_inc(mid_done, 1)


def gcn_layers(nc, table, feats, width, dinv, bias):
    with ExitStack() as ctx:
        s = Scope(nc, ctx, "gcn")
        scaled = s.sb("scaled", [P, NB, width], F32)
        parts = s.sb("parts", [P, NB, 3 * width], BF16)
        next_parts = s.sb("next_parts", [P, NB, 3 * width], BF16)
        bias_all = s.sb("bias_all", [P, width], F32)
        bias_in = s.sem("bias_in")
        split_scaled(nc, feats, width, dinv, scaled, parts)
        with nc.Block() as block:
            @block.sync
            def _(sync):
                sync.dma_start(bias_all[:], bias.rearrange("(a n) -> a n", a=1).to_broadcast([P, width])).then_inc(bias_in, 16)
                sync.wait_ge(bias_in, 16)

        def scratch(scope):
            return [scope.sb(f"t{k}", [P, width], F32) for k in range(2)]

        def chain(dve, step):
            def link(ins):
                step.add(ins)
                dve.wait_ge(step.sem, step.n)
            return link

        def summed(link, dve, at, ps, t1, t2):
            link(dve.tensor_reduce(t1[:], ps[:, 0:3 * width].rearrange("p (j f) -> p f j", j=3), AX.X, ALU.add))
            link(dve.tensor_tensor(t2[:], t1[:], flat(scaled[:, at, :]), ALU.add))

        def first(dve, at, ps, step, tensors):
            t1, t2 = tensors
            link = chain(dve, step)
            own, hi, mid, lo = flat(scaled[:, at, :]), *(flat(next_parts[:, at, k * width:(k + 1) * width]) for k in range(3))
            summed(link, dve, at, ps, t1, t2)
            link(dve.scalar_tensor_tensor(t1[:], t2[:], dinv[:, at], bias_all[:], ALU.mult, ALU.add))
            link(dve.tensor_scalar(own, t1[:], 0.0, dinv[:, at], ALU.max, ALU.mult))
            link(dve.tensor_copy(hi, own))
            link(dve.tensor_tensor(t2[:], own, hi, ALU.subtract))
            link(dve.tensor_copy(mid, t2[:]))
            link(dve.tensor_tensor(lo, t2[:], mid, ALU.subtract))

        def second(dve, at, ps, step, tensors):
            t1, t2 = tensors
            link = chain(dve, step)
            summed(link, dve, at, ps, t1, t2)
            link(dve.tensor_scalar(flat(feats[:, at, :]), t2[:], dinv[:, at], None, ALU.mult))
        gcn_pass(nc, "gcn1", table, parts, 3 * width, first, 8, scratch)
        gcn_pass(nc, "gcn2", table, next_parts, 3 * width, second, 3, scratch)


F1 = 2 * D + 2 * H
EG = 8
LOWEST = -3.0e38


def source_rows(nc, rows, node_rows):
    with ExitStack() as ctx:
        s = Scope(nc, ctx, "l1s")
        written = s.sem("written")
        block = ctx.enter_context(nc.Block())

        @block.sync
        def _(sync):
            sync.dma_start(rows_of(node_rows), rows[:]).then_inc(written, 16)
            sync.wait_ge(written, 16)


def edge_messages(nc, src, attr, node_rows, msg, score):
    groups = T // EG
    with ExitStack() as ctx:
        s = Scope(nc, ctx, "l1g")
        src_i = s.sb("src_i", [P, T], U32)
        at = s.sb("at", [P, T, 2], F32)
        idx = s.sb("idx", [P, 2, EG], U32)
        row = s.sb("row", [P, 2, EG, F1], F32)
        tmp = s.sb("tmp", [P, 2, EG, D], F32)
        tms = s.sb("tms", [P, 2, EG, H], F32)
        loaded, idx_ready, row_done, step_s, pool_pass, act_pass = (s.sem(n) for n in ("loaded", "idx_ready", "row_done", "step", "pool_pass", "act_pass"))
        gathered = [s.pool_dma_sem("gathered0"), s.pool_dma_sem("gathered1")]
        block = ctx.enter_context(nc.Block())

        @block.sync
        def _(sync):
            sync.dma_start(src_i[:], src.bitcast(U32)).then_inc(loaded, 16)
            sync.dma_start(at[:], attr.rearrange("p (t c) -> p t c", c=2)).then_inc(loaded, 16)

        def gather(pool, u):
            for k in range(EG):
                pool.indirect_dma_start(out=row[:, u, k, :], out_offset=None, in_=node_rows,
                                        in_offset=bass.IndirectOffsetOnAxis(idx[:, u, k:k + 1], 0),
                                        bounds_check=NP - 1).then_inc(gathered[u], 16)

        @block.gpsimd
        def _(pool):
            with pool.Fori(0, groups // 2) as i:
                for u in range(2):
                    pool.wait_ge(idx_ready, i * 2 + u + 1)
                    pool.sem_inc(pool_pass, 1)
                    gather(pool, u)
            pool.wait_ge(idx_ready, groups)
            gather(pool, 0)

        @block.scalar
        def _(act):
            act.wait_ge(loaded, 32)
            act.wait_ge(step_s, 2)
            with act.Fori(0, groups // 2) as i:
                for u in range(2):
                    act.wait_ge(row_done, i * 2 + u + 1)
                    act.sem_inc(act_pass, 1)
                    act.copy(idx[:, u, :], src_i[:, bass.ds((i * 2 + u) * EG, EG)]).then_inc(idx_ready, 1)
            act.wait_ge(row_done, groups)
            act.copy(idx[:, 0, :], src_i[:, T - EG:T]).then_inc(idx_ready, 1)

        @block.vector
        def _(dve):
            step = Count(step_s)

            def link(ins):
                step.add(ins)
                dve.wait_ge(step.sem, step.n)
            link(dve.memset(tmp[:], 0.0))
            link(dve.memset(tms[:], 0.0))
            dve.sem_inc(row_done, 2)
            dve.wait_ge(loaded, 32)

            def group(u, tiles, turns):
                dve.wait_ge(gathered[u], turns * 16 * EG + 16 * EG)
                for lo, wd, to, tm in ((0, D, msg, tmp), (2 * D, H, score, tms)):
                    a0, a1 = (at[:, tiles, c:c + 1].to_broadcast([P, EG, wd]) for c in range(2))
                    step.add(dve.tensor_tensor(tm[:, u], row[:, u, :, lo + wd:lo + 2 * wd], a1, ALU.mult))
                    link(dve.tensor_tensor(to[:, tiles, :], row[:, u, :, lo:lo + wd], a0, ALU.mult))
                    link(dve.tensor_tensor(to[:, tiles, :], to[:, tiles, :], tm[:, u], ALU.add))
                dve.sem_inc(row_done, 1)
            with dve.Fori(0, groups // 2) as i:
                step.enter(i, 12)
                for u in range(2):
                    group(u, bass.ds((i * 2 + u) * EG, EG), i)
                step.leave(groups // 2)
            group(0, slice(T - EG, T), groups // 2)


def edge_weights(nc, score):
    with ExitStack() as ctx:
        s = Scope(nc, ctx, "l1w")
        low = s.sb("low", [P, T, H], F32)
        mx = s.sb("mx", [P, H], F32)
        mx_all = s.sb("mx_all", [P, H], F32)
        step_s, filled, max_ready, max_all, exp_done = (s.sem(n) for n in ("step", "filled", "max_ready", "max_all", "exp_done"))
        block = ctx.enter_context(nc.Block())

        @block.vector
        def _(dve):
            dve.tensor_scalar(low[:], score[:], 0.2, None, ALU.mult).then_inc(step_s, 1)
            dve.wait_ge(step_s, 1)
            dve.tensor_tensor(low[:], score[:], low[:], ALU.max).then_inc(step_s, 1)
            dve.wait_ge(filled, 1)
            dve.tensor_reduce(mx[:], score[:].rearrange("p t h -> p h t"), AX.X, ALU.max).then_inc(max_ready, 1)
            dve.wait_ge(max_all, 1)
            dve.tensor_tensor(low[:], score[:], mx_all[:].rearrange("p (o h) -> p o h", o=1).to_broadcast([P, T, H]), ALU.subtract).then_inc(step_s, 1)

        @block.gpsimd
        def _(pool):
            pool.wait_ge(step_s, 2)
            pool.affine_select(out=score[:], in_=low[:], compare_op=ALU.is_ge, fill=LOWEST, base=E - 1,
                               pattern=[[-1, T], [0, H]], channel_multiplier=-T).then_inc(filled, 1)
            pool.wait_ge(max_ready, 1)
            pool.partition_all_reduce(mx_all[:], mx[:], P, RMAX).then_inc(max_all, 1)

        @block.scalar
        def _(act):
            act.wait_ge(step_s, 3)
            act.activation(score[:], low[:], ACT.Exp).then_inc(exp_done, 1)
            act.wait_ge(exp_done, 1)


def edge_sums(nc, dst, dst_rows, msg, weight, ident, sums):
    turns = T // CHAINS
    with ExitStack() as ctx:
        s = Scope(nc, ctx, "l1e")
        dst_i = s.sb("dst_i", [P, T], I32)
        dst_f = s.sb("dst_f", [P, T], F32)
        dst_t = s.sb("dst_t", [TC, 4, P], F32)
        spare = s.sb("spare", [P, T], F32)
        spare_i = s.sb("spare_i", [P, 1], I32)
        spare_f = s.sb("spare_f", [P, 1], F32)
        before = s.sb("before", [P, P], F32)
        rows = s.sb("rows", [P, 2, CHAINS * P], F32)
        same = s.sb("same", [P, CHAINS, P], F32)
        junk = s.sb("junk", [P, CHAINS, P], F32)
        early = s.sb("early", [P, 2, CHAINS], F32)
        pick = s.sb("pick", [P, 2, CHAINS], F32)
        cell = s.sb("cell", [P, 2, CHAINS], U32)
        value = s.sb("value", [P, CHAINS, MW], F32)
        merged = s.sb("merged", [P, 2, CHAINS, MW], F32)
        ps = s.ps("ps", [P, CHAINS, 512])
        ps_t = s.ps("ps_t", [P, 4, P])
        (loaded, masks_set, key_set, turned, copied, keys_out, step_s, cells_ready, slot_free, value_ready, summed,
         merged_ready, pool_pass, act_pass, pe_pass) = (s.sem(n) for n in (
             "loaded", "masks_set", "key_set", "turned", "copied", "keys_out", "step", "cells_ready", "slot_free",
             "value_ready", "summed", "merged_ready", "pool_pass", "act_pass", "pe_pass"))
        row_in = [s.sem("row_in0"), s.sem("row_in1")]
        row_free = s.sem("row_free")
        added = [s.pool_dma_sem(f"added{c}") for c in range(CHAINS)]
        block = ctx.enter_context(nc.Block())

        @block.sync
        def _(sync):
            sync.dma_start(dst_i[:], dst).then_inc(loaded, 16)
            sync.wait_ge(copied, 1)
            sync.dma_start(dst_rows.rearrange("(c t) p -> t c p", c=4), dst_t[:]).then_inc(keys_out, 16)
            sync.wait_ge(keys_out, 16)
            with sync.Fori(0, turns // 2) as i:
                for u in range(2):
                    sync.wait_ge(row_free, i * 2 + u + 1)
                    sync.dma_start(rows[:, u, :], dst_rows[bass.ds((i * 2 + u) * CHAINS, CHAINS), :].rearrange("(a t) p -> a (t p)", a=1).to_broadcast([P, CHAINS * P])).then_inc(row_in[u], 16)

        @block.gpsimd
        def _(pool):
            pool.sem_inc(slot_free, CHAINS)
            pool.memset(before[:], 1.0).then_inc(masks_set, 1)
            pool.iota(spare_i[:], pattern=[[0, 1]], base=NP, channel_multiplier=1).then_inc(masks_set, 1)
            pool.wait_ge(masks_set, 2)
            pool.affine_select(out=before[:], in_=before[:], compare_op=ALU.is_gt, fill=0.0, base=0,
                               pattern=[[-1, P]], channel_multiplier=1).then_inc(masks_set, 1)

            def add(n, u, first=False):
                pool.wait_ge(cells_ready, n + 1)
                pool.sem_inc(pool_pass, 1)
                for c in range(CHAINS):
                    pool.wait_ge(merged_ready, CHAINS + n * CHAINS + c + 1)
                    pool.sem_inc(pool_pass, 1)
                    if not first:
                        pool.wait_ge(added[c], n * 16)
                    pool.sem_inc(slot_free, 1)
                    pool.indirect_dma_start(out=sums[c], out_offset=bass.IndirectOffsetOnAxis(cell[:, u, c:c + 1], 0),
                                            in_=merged[:, u, c, :], in_offset=None, bounds_check=ROWS - 1,
                                            compute_op=ALU.add).then_inc(added[c], 16)
            add(0, 0, first=True)
            add(1, 1)
            with pool.Fori(1, turns // 2) as i:
                for u in range(2):
                    add(i * 2 + u, u)
            for c in range(CHAINS):
                pool.wait_ge(added[c], turns * 16)

        @block.tensor
        def _(pe):
            pe.sem_inc(summed, CHAINS)
            pe.wait_ge(key_set, 1)
            for c in range(4):
                last = pe.transpose(ps_t[0:TC, c, :], dst_f[:, c * TC:(c + 1) * TC], ident[:])
            last.then_inc(turned, 1)
            with pe.Fori(0, turns) as i:
                for c in range(CHAINS):
                    pe.wait_ge(value_ready, (i * CHAINS + c + 1) * 3)
                    pe.sem_inc(pe_pass, 1)
                    pe.wait_ge(merged_ready, i * CHAINS + c + 1)
                    pe.sem_inc(pe_pass, 1)
                    pe.matmul(ps[:, c, 0:MW], same[:, c, :], value[:, c, :], start=True, stop=True).then_inc(summed, 1)

        @block.scalar
        def _(act):
            act.sem_inc(merged_ready, CHAINS)
            with act.Fori(0, turns // 2) as i:
                for u in range(2):
                    for c in range(CHAINS):
                        m = (i * 2 + u) * CHAINS + c
                        act.wait_ge(summed, CHAINS + m + 1)
                        act.sem_inc(act_pass, 1)
                        act.wait_ge(slot_free, m + 1)
                        act.sem_inc(act_pass, 1)
                        act.copy(merged[:, u, c, :], ps[:, c, 0:MW]).then_inc(merged_ready, 1)

        @block.vector
        def _(dve):
            step = Count(step_s)

            def link(ins):
                step.add(ins)
                dve.wait_ge(step.sem, step.n)
            dve.wait_ge(loaded, 16)
            dve.tensor_copy(dst_f[:], dst_i[:]).then_inc(key_set, 1)
            dve.wait_ge(masks_set, 3)
            link(dve.tensor_copy(spare_f[:], spare_i[:]))
            dve.wait_ge(turned, 1)
            dve.tensor_copy(dst_t[:], ps_t[0:TC, :, :]).then_inc(copied, 1)
            dve.wait_ge(key_set, 1)
            link(dve.tensor_scalar(spare[:], dst_f[:], -1.0, spare_f[:, 0:1], ALU.mult, ALU.add))
            dve.sem_inc(row_free, 2)
            with dve.Fori(0, turns // 2) as i:
                step.enter(i, 2 * (CHAINS + 3))
                for u in range(2):
                    n = i * 2 + u
                    dve.wait_ge(row_in[u], i * 16 + 16)
                    for c in range(CHAINS):
                        one = bass.ds(n * CHAINS + c, 1)
                        row = rows[:, u, c * P:(c + 1) * P]
                        step.add(dve.scalar_tensor_tensor(junk[:, c, :], row, dst_f[:, one], before[:],
                                                          ALU.is_equal, ALU.mult, accum_out=early[:, u, c:c + 1]))
                        dve.wait_ge(summed, n * CHAINS + c + 1)
                        dve.tensor_scalar(same[:, c, :], row, dst_f[:, one], None, ALU.is_equal).then_inc(value_ready, 1)
                        w = flat(weight[:, one, :])
                        dve.tensor_tensor(value[:, c, 0:H * D].rearrange("p (h d) -> p h d", h=H), msg[:, one, :].to_broadcast([P, H, D]),
                                          spread(w, H, D), ALU.mult).then_inc(value_ready, 1)
                        dve.tensor_copy(value[:, c, H * D:MW], w).then_inc(value_ready, 1)
                    dve.wait_ge(step.sem, step.n)
                    ts = bass.ds(n * CHAINS, CHAINS)
                    link(dve.tensor_scalar(pick[:, u, :], early[:, u, :], 0.0, None, ALU.is_gt))
                    link(dve.tensor_tensor(pick[:, u, :], pick[:, u, :], spare[:, ts], ALU.mult))
                    dve.wait_ge(slot_free, (n + 1) * CHAINS)
                    link(dve.tensor_tensor(cell[:, u, :], pick[:, u, :], dst_f[:, ts], ALU.add))
                    dve.sem_inc(cells_ready, 1)
                    dve.wait_ge(value_ready, (n + 1) * CHAINS * 3)
                    dve.sem_inc(row_free, 1)
                step.leave(turns // 2)


def add_quotients(nc, sums, x):
    nb, slots = BG, 3
    with ExitStack() as ctx:
        s = Scope(nc, ctx, "l1q")
        part = s.sb("part", [P, slots, CHAINS, nb, MW], F32)
        rden = s.sb("rden", [P, nb, H], F32)
        part_in, step_s = [s.sem(f"part_in{g}") for g in range(NG)], s.sem("step")
        part_free = s.sem("part_free")
        block = ctx.enter_context(nc.Block())

        @block.sync
        def _(sync):
            for g in range(NG):
                if g >= slots:
                    sync.wait_ge(part_free, g - slots + 1)
                for c in range(CHAINS):
                    sync.dma_start(part[:, g % slots, c], rows_of(sums[c][nb * g * P:nb * (g + 1) * P, :])).then_inc(part_in[g], 16)

        @block.vector
        def _(dve):
            step = Count(step_s)

            def do(ins):
                step.add(ins)

            def link(ins):
                step.add(ins)
                dve.wait_ge(step.sem, step.n)
            for g in range(NG):
                b = slice(nb * g, nb * (g + 1))
                p = part[:, g % slots]
                dve.wait_ge(part_in[g], CHAINS * 16)
                for c in range(1, CHAINS):
                    link(dve.tensor_tensor(p[:, 0], p[:, 0], p[:, c], ALU.add))
                link(dve.tensor_scalar(rden[:], p[:, 0, :, H * D:MW], 1e-10, None, ALU.add))
                link(dve.reciprocal(rden[:], rden[:]))
                for k in range(nb):
                    heads = p[:, 0, k, 0:H * D].rearrange("p (h d) -> p h d", h=H)
                    do(dve.tensor_tensor(heads, heads, spread(rden[:, k, :], H, D), ALU.mult))
                dve.wait_ge(step.sem, step.n)
                link(dve.tensor_tensor(x[:, b, :], x[:, b, :], p[:, 0, :, 0:H * D], ALU.add))
                dve.sem_inc(part_free, 1)


def attention_messages(nc, a, x, h, ident, sums):
    node_rows = nc.dram_tensor("node_rows", (NP, F1), F32).ap()
    dst_rows = nc.dram_tensor("dst_rows", (T, P), F32).ap()
    normalise(nc, "n1", x, h)
    with ExitStack() as ctx:
        rows = ctx.enter_context(nc.sbuf_tensor("l1_rows", [P, NB, F1], F32))
        project(nc, "pl", h, 2, None, 2 * D, rows, ident, (a["L1_gnn_W_forward"], a["L1_gnn_W_reverse"]),
                shared=a["L1_gnn_attn_forward"])
        source_rows(nc, rows, node_rows)
    with ExitStack() as ctx:
        msg = ctx.enter_context(nc.sbuf_tensor("msg", [P, T, D], F32))
        weight = ctx.enter_context(nc.sbuf_tensor("weight", [P, T, H], F32))
        edge_messages(nc, a["src"], a["edge_attr_2"], node_rows, msg, weight)
        edge_weights(nc, weight)
        edge_sums(nc, a["dst"], dst_rows, msg, weight, ident, sums)
    add_quotients(nc, sums, x)


DW = D + 1
HW = 3 * DW
GC = 512
GB = GC // P
CHUNKS = NP // GC
MASKS = 4
SG = 5
REACH = 80.0
TINY = 1e-37
STEEP = 2.0 ** 60


def attention_terms(nc, tag, ident, t, er_rows, loops):
    with ExitStack() as ctx:
        s = Scope(nc, ctx, tag)
        ext = s.sb("ext", [P, 12], F32)
        ext_all = s.sb("ext_all", [P, 8], F32)
        mid = s.sb("mid", [P, H], F32)
        cen = s.sb("cen", [P, NB, H], F32)
        z = s.sb("z", [P, NB, H], F32)
        z2 = s.sb("z2", [P, NB, H], F32)
        top = s.sb("top", [P, NB, H], F32)
        e = s.sb("e", [P, NB, H], F32)
        e2 = s.sb("e2", [P, NB, H], F32)
        er_t = s.sb("er_t", [P, P], F32)
        ps = s.ps("ps", [P, 512])
        step_s, ext_ready, ext_done, er_turned, er_copied, er_out, exps = (s.sem(n) for n in (
            "step", "ext_ready", "ext_done", "er_turned", "er_copied", "er_out", "exps"))
        er, el = t["er_el"][:, 0], t["er_el"][:, 1]
        elb, u, u2, v, v2, ws = (t[k] for k in ("elb", "u", "u2", "v", "v2", "ws"))
        block = ctx.enter_context(nc.Block())

        @block.sync
        def _(sync):
            sync.wait_ge(er_copied, 1)
            sync.dma_start(er_rows, er_t[0:NB * H, :]).then_inc(er_out, 16)
            sync.wait_ge(er_out, 16)

        @block.gpsimd
        def _(pool):
            pool.wait_ge(ext_ready, 1)
            pool.partition_all_reduce(ext_all[:], ext[:, 0:8], P, RMAX).then_inc(ext_done, 1)

        @block.tensor
        def _(pe):
            pe.transpose(ps[0:NB * H, 0:P], er.rearrange("p b h -> p (b h)"), ident[:]).then_inc(er_turned, 1)

        CEN, ZV, Z2V, SELF = 7, 11, 12, 16

        @block.scalar
        def _(act):
            act.wait_ge(step_s, CEN)
            act.activation(u[:], cen[:], ACT.Exp).then_inc(exps, 1)
            act.activation(u2[:], cen[:], ACT.Exp, scale=0.2).then_inc(exps, 1)
            act.wait_ge(step_s, Z2V)
            act.activation(v[:], z[:].rearrange("p b h -> p h b"), ACT.Exp).then_inc(exps, 1)
            act.activation(v2[:], z2[:].rearrange("p b h -> p h b"), ACT.Exp).then_inc(exps, 1)
            if loops:
                act.wait_ge(step_s, SELF)
                act.activation(ws[:], e[:].rearrange("p b h -> p h b"), ACT.Exp).then_inc(exps, 1)
            act.wait_ge(exps, 5 if loops else 4)

        @block.vector
        def _(dve):
            step = Count(step_s)

            def do(ins):
                step.add(ins)

            def link(ins):
                step.add(ins)
                dve.wait_ge(step.sem, step.n)
            by_head = el.rearrange("p b h -> p h b")
            do(dve.tensor_reduce(ext[:, 0:4], by_head, AX.X, ALU.max))
            link(dve.tensor_reduce(ext[:, 8:12], by_head, AX.X, ALU.min))
            dve.tensor_scalar(ext[:, 4:8], ext[:, 8:12], -1.0, None, ALU.mult).then_inc(ext_ready, 1)
            do(dve.tensor_scalar(elb[:], el, STEEP, None, ALU.mult))
            dve.wait_ge(er_turned, 1)
            dve.tensor_copy(er_t[0:NB * H, :], ps[0:NB * H, 0:P]).then_inc(er_copied, 1)
            dve.wait_ge(ext_done, 1)
            link(dve.tensor_tensor(mid[:], ext_all[:, 0:4], ext_all[:, 4:8], ALU.subtract))
            link(dve.tensor_scalar(mid[:], mid[:], 0.5, None, ALU.mult))
            link(dve.scalar_tensor_tensor(mid[:], ext_all[:, 0:4], -REACH, mid[:], ALU.add, ALU.max))
            mid_all = mid[:].rearrange("p (o h) -> p o h", o=1).to_broadcast([P, NB, H])
            do(dve.tensor_tensor(cen[:], el, mid_all, ALU.subtract))
            assert step.n == CEN
            link(dve.tensor_tensor(z[:], er, mid_all, ALU.add))
            link(dve.tensor_scalar(z2[:], z[:], 0.2, None, ALU.mult))
            link(dve.tensor_tensor(top[:], z[:], z2[:], ALU.max))
            do(dve.tensor_tensor(z[:], z[:], top[:], ALU.subtract))
            assert step.n == ZV
            do(dve.tensor_tensor(z2[:], z2[:], top[:], ALU.subtract))
            assert step.n == Z2V
            if loops:
                link(dve.tensor_tensor(e[:], el, er, ALU.add))
                link(dve.tensor_scalar(e2[:], e[:], 0.2, None, ALU.mult))
                link(dve.tensor_tensor(e[:], e[:], e2[:], ALU.max))
                do(dve.tensor_tensor(e[:], e[:], top[:], ALU.subtract))
                assert step.n == SELF
            dve.wait_ge(step.sem, step.n)


def weighted_features(nc, tag, feat, t, parts):
    with ExitStack() as ctx:
        s = Scope(nc, ctx, tag)
        whole = s.sb("whole", [P, 2, 5, H, DW], F32)
        rest = s.sb("rest", [P, 2, 5, H, DW], F32)
        scaled, column_set, hi_done, rest_done, mid_done, lo_done = (s.sem(n) for n in ("scaled", "column_set", "hi_done", "rest_done", "mid_done", "lo_done"))
        block = ctx.enter_context(nc.Block())
        items = [(g, side) for g in range(5) for side in range(2)]

        def part(n, j):
            g, side = items[n]
            return parts[:, 5 * g:5 * g + 5, side, :, j * DW:(j + 1) * DW]

        @block.gpsimd
        def _(pool):
            for n, (g, side) in enumerate(items):
                b = slice(5 * g, 5 * g + 5)
                w = t["u"] if side == 0 else t["u2"]
                if n >= 2:
                    pool.wait_ge(hi_done, n - 1)
                    pool.wait_ge(rest_done, n - 1)
                pool.tensor_tensor(whole[:, n % 2, :, :, 0:D].rearrange("p b h d -> p (b h) d"), feat[:, b, :].rearrange("p b (h d) -> p (b h) d", h=H),
                                   spread(w[:, b, :].rearrange("p b h -> p (b h)"), 5 * H, D), ALU.mult).then_inc(scaled, 1)

        @block.vector
        def _(dve):
            def column(n):
                g, side = items[n]
                w = t["u"] if side == 0 else t["u2"]
                if n >= 2:
                    dve.wait_ge(hi_done, n - 1)
                    dve.wait_ge(rest_done, n - 1)
                dve.tensor_copy(whole[:, n % 2, :, :, D], w[:, 5 * g:5 * g + 5, :]).then_inc(column_set, 1)

            def rest_of(n):
                dve.wait_ge(hi_done, n + 1)
                if n >= 2:
                    dve.wait_ge(mid_done, n - 1)
                    dve.wait_ge(lo_done, n - 1)
                dve.tensor_tensor(rest[:, n % 2], whole[:, n % 2], part(n, 0), ALU.subtract).then_inc(rest_done, 1)

            def low(n):
                dve.wait_ge(mid_done, n + 1)
                dve.tensor_tensor(part(n, 2), rest[:, n % 2], part(n, 1), ALU.subtract).then_inc(lo_done, 1)
            for n in range(12):
                if n < 10:
                    column(n)
                if 1 <= n <= 10:
                    rest_of(n - 1)
                if n >= 2:
                    low(n - 2)
            dve.wait_ge(lo_done, 10)

        @block.scalar
        def _(act):
            for n in range(11):
                if n < 10:
                    act.wait_ge(scaled, n + 1)
                    act.wait_ge(column_set, n + 1)
                    act.copy(part(n, 0), whole[:, n % 2]).then_inc(hi_done, 1)
                if n >= 1:
                    act.wait_ge(rest_done, n)
                    act.copy(part(n - 1, 1), rest[:, (n - 1) % 2]).then_inc(mid_done, 1)


def attend(nc, tag, table, t, parts, er_rows, h, residual, loops=None, last_x=None):
    units = [(b, min(2, NB - b)) for b in range(0, NB, 2)]
    NU = len(units)
    with ExitStack() as ctx:
        s = Scope(nc, ctx, tag)
        cols = s.sb("cols", [P, NB, GC], F16)
        er = s.sb("er", [P, H, GC], F32)
        side = s.sb("side", [P, MASKS, 2, GC], F16)
        pos = s.sb("pos", [P, MASKS, 2, GC], F16)
        neg = s.sb("neg", [P, MASKS, 2, GC], F16)
        taken = s.sb("taken", [P, 2, GB, 2 * HW], F32)
        sides = s.sb("sides", [P, GB, 2, DW], F32)
        total = s.sb("total", [P, GB, DW], F32)
        den = s.sb("den", [P, GB], F32)
        bound = s.sb("bound", [P, GB], F32)
        rden = s.sb("rden", [P, GB], F32)
        own = s.sb("own", [P, GB, D], F32)
        quot = s.sb("quot", [P, GB, D], F32)
        none = s.sb("none", [P, GB, D], F32)
        ps = s.ps("ps", [P, 2 * GB, 512])
        col_in = [s.sem(f"col_in{g}") for g in range(NB // SG)]
        er_in = [s.sem(f"er_in{k}") for k in range(H)]
        (side_ready, pos_ready, masks_ready, masks_free, act_taken, dve_taken, consumed, den_ready, rden_ready, set_up, bounded, finished, emptied,
         step_s, pe_pass, act_pass, pool_pass) = (s.sem(n) for n in (
             "side_ready", "pos_ready", "masks_ready", "masks_free", "act_taken", "dve_taken", "consumed", "den_ready",
             "rden_ready", "set_up", "bounded", "finished", "emptied", "step", "pe_pass", "act_pass", "pool_pass"))
        block = ctx.enter_context(nc.Block())
        tab = table.rearrange("(b p) d -> p b d", p=P)
        er_v = er_rows.rearrange("(b h) p -> h b p", h=H)

        @block.sync
        def _(sync):
            def load_cols(g, at, width):
                sync.dma_start(cols[:, SG * g:SG * g + SG, 0:width], tab[:, SG * g:SG * g + SG, at]).then_inc(col_in[g], 16)

            def load_er(k, at, nblk):
                sync.dma_start(er[:, k, 0:nblk * P].rearrange("p (b q) -> p b q", b=nblk),
                               er_v[k:k + 1, at, :].to_broadcast([P, nblk, P])).then_inc(er_in[k], 16)

            def cols_used(i, g):
                q = (SG * (g + 1) - 1) // 2
                sync.wait_ge(masks_ready, (i * H + H - 1) * NU + q + 1)
            for g in range(NB // SG):
                if g < H:
                    load_er(g, slice(0, GB), GB)
                load_cols(g, slice(0, GC), GC)
            with sync.Fori(0, CHUNKS - 1) as i:
                for k in range(H - 1):
                    sync.wait_ge(side_ready, (i * H + k + 1) * NU)
                    load_er(k, bass.ds((i + 1) * GB, GB), GB)
                for g in range(NB // SG):
                    cols_used(i, g)
                    load_cols(g, bass.ds((i + 1) * GC, GC), GC)
                sync.wait_ge(side_ready, (i * H + H) * NU)
                load_er(H - 1, bass.ds((i + 1) * GB, GB), GB)
            for k in range(H):
                sync.wait_ge(side_ready, ((CHUNKS - 1) * H + k + 1) * NU)
                load_er(k, slice(CHUNKS * GB, NB), 1)
            for g in range(NB // SG):
                cols_used(CHUNKS - 1, g)
                load_cols(g, slice(CHUNKS * GC, NP), P)

        @block.tensor
        def _(pe):
            pe.sem_inc(masks_free, MASKS)

            def item(n, k, nblk):
                pe.wait_ge(act_taken, 1 + n)
                pe.sem_inc(pe_pass, 1)
                pe.wait_ge(dve_taken, 1 + n)
                pe.sem_inc(pe_pass, 1)
                for q, (b0, nb) in enumerate(units):
                    slot = (k * NU + q) % MASKS
                    pe.wait_ge(masks_ready, n * NU + q + 1)
                    pe.sem_inc(pe_pass, 1)
                    for b in range(b0, b0 + nb):
                        for j in range(nblk):
                            bank = ps[:, (k % 2) * GB + j, :]
                            pe.matmul(bank[:, 0:HW], pos[:, slot, b - b0, j * P:(j + 1) * P], parts[:, b, 0, k, :],
                                      start=(b == 0), stop=False, skip_group_check=True)
                            last = pe.matmul(bank[:, HW:2 * HW], neg[:, slot, b - b0, j * P:(j + 1) * P], parts[:, b, 1, k, :],
                                             start=False, stop=(b == NB - 1), skip_group_check=True)
                    last.then_inc(masks_free, 1)
            with pe.Fori(0, CHUNKS) as i:
                for k in range(H):
                    item(i * H + k, k, GB)
            for k in range(H):
                item(CHUNKS * H + k, k, 1)

        def previous(k, nblk):
            return (k + 1) % 2, GB if k == 0 else nblk

        @block.scalar
        def _(act):
            def take(n, half, nblk):
                act.wait_ge(masks_free, MASKS + n * NU)
                act.sem_inc(act_pass, 1)
                act.wait_ge(consumed, 1 + n)
                act.sem_inc(act_pass, 1)
                na = (nblk + 1) // 2
                act.copy(taken[:, half, 0:na, :], ps[:, half * GB:half * GB + na, 0:2 * HW]).then_inc(act_taken, 1)

            def item(n, k, nblk, turn):
                act.wait_ge(er_in[k], turn * 16 + 16)
                act.sem_inc(act_pass, 1)
                for q, (b0, nb) in enumerate(units):
                    slot = (k * NU + q) % MASKS
                    act.wait_ge(pos_ready, n * NU + q + 1)
                    act.sem_inc(act_pass, 1)
                    for b in range(b0, b0 + nb):
                        last = act.activation(side[:, slot, b - b0, 0:nblk * P], er[:, k, 0:nblk * P], ACT.Sigmoid,
                                              bias=t["elb"][:, b, k:k + 1], scale=STEEP)
                    last.then_inc(side_ready, 1)
                    if q == 3:
                        take(n, *previous(k, nblk))
            act.sem_inc(act_taken, 1)
            act.wait_ge(set_up, 1)
            with act.Fori(0, CHUNKS) as i:
                for k in range(H):
                    item(i * H + k, k, GB, i)
            for k in range(H):
                item(CHUNKS * H + k, k, 1, CHUNKS)
            take((CHUNKS + 1) * H, *previous(H, 1))

        @block.vector
        def _(dve):
            dve.memset(ps[:, GB:2 * GB, 0:2 * HW], 0.0).then_inc(emptied, 1)
            dve.memset(den[:], 1.0).then_inc(emptied, 1)
            dve.wait_ge(emptied, 2)
            dve.sem_inc(set_up, 1)
            dve.sem_inc(dve_taken, 1)
            dve.sem_inc(pos_ready, MASKS)

            def take(n, half, nblk):
                dve.wait_ge(masks_free, MASKS + n * NU)
                dve.wait_ge(consumed, 1 + n)
                na = (nblk + 1) // 2
                if na < nblk:
                    dve.tensor_copy(taken[:, half, na:nblk, :], ps[:, half * GB + na:half * GB + nblk, 0:2 * HW]).then_inc(dve_taken, 1)
                else:
                    dve.sem_inc(dve_taken, 1)

            def invert(n):
                dve.wait_ge(den_ready, 1 + n)
                dve.tensor_scalar(bound[:], den[:], TINY, None, ALU.max).then_inc(bounded, 1)
                dve.wait_ge(bounded, n + 1)
                dve.reciprocal(rden[:], bound[:]).then_inc(rden_ready, 1)

            def item(n, k, nblk, turn):
                width = nblk * P
                for q in range(NU + 1):
                    if q < NU:
                        b0, nb = units[q]
                        slot = (k * NU + q) % MASKS
                        if k == 0:
                            for g in range(NB // SG):
                                if b0 <= SG * g < b0 + nb:
                                    dve.wait_ge(col_in[g], turn * 16 + 16)
                        dve.wait_ge(side_ready, n * NU + q + 1)
                        dve.wait_ge(masks_free, n * NU + q + 1)
                        dve.tensor_tensor(pos[:, slot, 0:nb, 0:width], cols[:, b0:b0 + nb, 0:width], side[:, slot, 0:nb, 0:width],
                                          ALU.mult).then_inc(pos_ready, 1)
                    if q >= 1:
                        b0, nb = units[q - 1]
                        slot = (k * NU + q - 1) % MASKS
                        dve.wait_ge(pos_ready, MASKS + n * NU + q)
                        dve.tensor_tensor(neg[:, slot, 0:nb, 0:width], cols[:, b0:b0 + nb, 0:width], pos[:, slot, 0:nb, 0:width],
                                          ALU.subtract).then_inc(masks_ready, 1)
                    if q == 3:
                        take(n, *previous(k, nblk))
                    if q == NU - 2:
                        invert(n)
            with dve.Fori(0, CHUNKS) as i:
                for k in range(H):
                    item(i * H + k, k, GB, i)
            for k in range(H):
                item(CHUNKS * H + k, k, 1, CHUNKS)
            take((CHUNKS + 1) * H, *previous(H, 1))
            invert((CHUNKS + 1) * H)
            if not loops:
                dve.wait_ge(finished, 1)
                if last_x is not None:
                    dve.scalar_tensor_tensor(last_x[:], h[:], 0.0, last_x[:], ALU.max, ALU.add).then_inc(finished, 1)
                else:
                    dve.tensor_scalar(h[:], h[:], 0.0, None, ALU.max).then_inc(finished, 1)
                dve.wait_ge(finished, 2)

        @block.gpsimd
        def _(pool):
            pool.memset(none[:], 0.0).then_inc(step_s, 1)
            pool.sem_inc(consumed, 3)
            pool.sem_inc(den_ready, 1)
            step = Count(step_s, 1)
            pool.wait_ge(step_s, 1)
            pool.sem_inc(pool_pass, 1)

            def link(ins):
                step.add(ins)
                pool.wait_ge(step.sem, step.n)
                pool.sem_inc(pool_pass, 1)

            def finish(n, k, rows, nblk):
                at = slice(k * D, (k + 1) * D)
                got = taken[:, k % 2, 0:nblk, :].rearrange("p j (s c f) -> p j s c f", s=2, c=3)
                both, tot, q = sides[:, 0:nblk], total[:, 0:nblk, :], quot[:, 0:nblk, :]
                pool.wait_ge(act_taken, 1 + n + 2)
                pool.sem_inc(pool_pass, 1)
                pool.wait_ge(dve_taken, 1 + n + 2)
                pool.sem_inc(pool_pass, 1)
                link(pool.tensor_tensor(both, got[:, :, :, 0, :], got[:, :, :, 1, :], ALU.add))
                link(pool.tensor_tensor(both, both, got[:, :, :, 2, :], ALU.add))
                pool.sem_inc(consumed, 1)
                link(pool.tensor_tensor(tot, both[:, :, 0, :], spread(t["v"][:, k, rows], nblk, DW), ALU.mult))
                link(pool.tensor_tensor(both[:, :, 1, :], both[:, :, 1, :], spread(t["v2"][:, k, rows], nblk, DW), ALU.mult))
                link(pool.tensor_tensor(tot, tot, both[:, :, 1, :], ALU.add))
                if loops:
                    w = t["ws"][:, k, rows]
                    link(pool.tensor_tensor(own[:, 0:nblk, :], h[:, rows, at], spread(w, nblk, D), ALU.mult))
                    link(pool.tensor_tensor(tot[:, :, 0:D], tot[:, :, 0:D], own[:, 0:nblk, :], ALU.add))
                    link(pool.tensor_tensor(tot[:, :, D], tot[:, :, D], w, ALU.add))
                link(pool.tensor_tensor(den[:, 0:nblk], tot[:, :, D], none[:, 0:nblk, 0], ALU.add))
                pool.sem_inc(den_ready, 1)
                pool.wait_ge(rden_ready, n + 2)
                pool.sem_inc(pool_pass, 1)
                link(pool.tensor_tensor(q, tot[:, :, 0:D], spread(rden[:, 0:nblk], nblk, D), ALU.mult))
                if loops:
                    link(pool.tensor_tensor(loops[:, rows, at], loops[:, rows, at], q, ALU.add))
                else:
                    link(pool.tensor_tensor(h[:, rows, at], q, h[:, rows, at] if residual else none[:, 0:nblk, :], ALU.add))
            per = 11 if loops else 8
            with pool.Fori(0, CHUNKS) as i:
                step.enter(i, H * per)
                for k in range(H):
                    finish(i * H + k, k, bass.ds(i * GB, GB), GB)
                step.leave(CHUNKS)
            for k in range(H):
                finish(CHUNKS * H + k, k, slice(NB - 1, NB), 1)
            pool.sem_inc(finished, 1)


def gat_layer(nc, tag, table, er_rows, h, ident, weights, att_src, att_dst, residual, x=None, bias=None, last_x=None):
    with ExitStack() as ctx:
        s = Scope(nc, ctx, tag)
        t = {k: s.sb(k, [P, NB, H], F32) for k in ("elb", "u", "u2")}
        t["er_el"] = s.sb("er_el", [P, 2, NB, H], F32)
        t.update({k: s.sb(k, [P, H, NB], F32) for k in ("v", "v2", "ws")})
        parts = s.sb("parts", [P, NB, 2, H, HW], BF16)
        with ExitStack() as inner:
            feat = h if x is not None else inner.enter_context(nc.sbuf_tensor(tag + "_feat", [P, NB, 256], F32))
            project(nc, tag + "p", h, 2, weights, 256, feat, ident, attention=(att_dst, att_src, t["er_el"]),
                    biased=(x, bias) if x is not None else None)
            attention_terms(nc, tag + "t", ident, t, er_rows, x is not None)
            weighted_features(nc, tag + "w", feat, t, parts)
        attend(nc, tag + "a", table, t, parts, er_rows, h, residual, x, last_x)


def program(nc, a, out):
    cells = nc.dram_tensor("table", (TAB,), F16).ap()
    table = cells[0:NP * NP].rearrange("(s d) -> s d", d=NP)
    key_rows = nc.dram_tensor("key_rows", (T, P), F32).ap()
    er_rows = nc.dram_tensor("er_rows", (NB * H, P), F32).ap()
    sums = [nc.dram_tensor(f"sums{c}", (ROWS, MW), F32).ap() for c in range(CHAINS)]
    with ExitStack() as ctx:
        x = ctx.enter_context(nc.sbuf_tensor("x", [P, NB, 256], F32))
        h = ctx.enter_context(nc.sbuf_tensor("h", [P, NB, 256], F32))
        ident = ctx.enter_context(nc.sbuf_tensor("ident", [P, P], F32))
        with ExitStack() as c0:
            dinv = c0.enter_context(nc.sbuf_tensor("dinv", [P, NB], F32))
            f1 = c0.enter_context(nc.sbuf_tensor("f1", [P, NB, 128], F32))
            with ExitStack() as c1:
                zeros = c1.enter_context(nc.sbuf_tensor("zeros", [P, ZW + ZW % 2], F16))
                w1 = c1.enter_context(nc.sbuf_tensor("w1", [P, 2, 128], F32))
                table_zero = nc.alloc_semaphore("table_zero")
                load_nodes(nc, x, a["x"], w1, a["L0_gnn_W1"], ident)
                zero_table(nc, zeros, cells, table_zero)
                normalise(nc, "n0", x, h)
                project(nc, "p0", h, 2, None, 128, f1, ident, None, w1)
                adjacency(nc, a["src"], a["dst"], cells, table_zero, zeros, sums, key_rows, ident, dinv)
            gcn_layers(nc, table, f1, 128, dinv, a["L0_gnn_b1"])
            project(nc, "p1", f1, 1, a["L0_gnn_W2"], 256, x, ident, added=True, biased=(x, a["L0_gnn_b2"]))
        attention_messages(nc, a, x, h, ident, sums)
        normalise(nc, "n2", x, h)
        for n in range(3):
            gat_layer(nc, f"g{n}", table, er_rows, h, ident, a[f"L2_gnn_W{n}"], a[f"L2_gnn_al{n}"], a[f"L2_gnn_ar{n}"], n < 2,
                      last_x=x if n == 2 else None)
        normalise(nc, "n3", x, h)
        gat_layer(nc, "g3", table, er_rows, h, ident, a["L3_gnn_W"], a["L3_gnn_att_src"], a["L3_gnn_att_dst"], False, x, a["L3_gnn_bias"])
        store(nc, x, out)


def store(nc, x, out):
    with ExitStack() as ctx:
        s = Scope(nc, ctx, "store")
        stored = s.sem("stored")
        with nc.Block() as block:
            @block.sync
            def _(sync):
                full = (NB - 1) * P
                sync.dma_start(rows_of(out[0:full, :]), x[:, 0:NB - 1, :]).then_inc(stored, 16)
                sync.dma_start(out[full:N, :], x[0:N - full, NB - 1, :]).then_inc(stored, 16)
                sync.wait_ge(stored, 32)


def kernel(**inputs):
    import numpy as np
    import concourse.bacc as bacc
    from concourse.bass_utils import run_bass_kernel_spmd as run
    nc = bacc.Bacc("TRN2", target_bir_lowering=False, num_devices=1)
    arrays = {k: np.ascontiguousarray(v) for k, v in inputs.items()}
    pad = np.full(P * T - E, NP - 1, arrays["src"].dtype)
    for k in ("src", "dst"):
        arrays[k] = np.concatenate([arrays[k], pad]).reshape(P, T)
    arrays["edge_attr_2"] = np.concatenate([arrays["edge_attr_2"], np.zeros((P * T - E, 2), arrays["edge_attr_2"].dtype)]).reshape(P, 2 * T)
    h = {k: nc.dram_tensor("in_" + k, v.shape, mybir.dt.from_np(v.dtype), kind="ExternalInput").ap() for k, v in arrays.items()}
    out = nc.dram_tensor("out", (N, 256), F32, kind="ExternalOutput").ap()
    program(nc, h, out)
    r = run(nc, [{"in_" + k: v for k, v in arrays.items()}], core_ids=[0])
    return r.results[0]["out"]
```
